# Optimizing a Trainium2 kernel written in Bass

```python
import numpy as np
import jax
import jax.numpy as jnp

def _softmax(x, axis=-1):
    return jax.nn.softmax(x, axis=axis)

def _gelu(x):
    return jax.nn.gelu(x, approximate=True)

def _silu(x):
    return jax.nn.silu(x)

def _sigmoid(x):
    return jax.nn.sigmoid(x)

def _layernorm(x, axis=-1, eps=1e-05):
    m = jnp.mean(x, axis=axis, keepdims=True)
    v = jnp.var(x, axis=axis, keepdims=True)
    return (x - m) / jnp.sqrt(v + eps)

def _scatter_add(tgt, idx, src, axis=0):
    return tgt.at[idx].add(src)

def _segment_sum(src, seg, n):
    return jax.ops.segment_sum(src, seg, n)
kernel_name = 'mk_flamingo_gated_d2_seqx_r4_d53333'

def setup_inputs(seed: int=0):
    np.random.seed(seed)
    _w = jnp.asarray

    def _rec_inputs():
        import jax
        import jax.numpy as jnp
        _rk = jax.random.key(seed)
        x = 0.5 + 0.2887 * jax.random.normal(jax.random.fold_in(_rk, 1), (4, 512, 512), jnp.float32)
        _lenS = 512 - jax.random.randint(jax.random.fold_in(_rk, 7), (4,), 0, max(1, 512 // 4) + 1, jnp.int32)
        _lenS2 = 512 - jax.random.randint(jax.random.fold_in(_rk, 8), (4,), 0, max(1, 512 // 4) + 1, jnp.int32)
        _ctx_512P = jax.random.normal(jax.random.fold_in(_rk, 11), (4, 16, 128), jnp.float32)
        _ctx_512c = jax.random.dirichlet(jax.random.fold_in(_rk, 511), 0.3 * jnp.ones((16,), jnp.float32), (4, 512))
        _ctx_512t = jnp.einsum('bsk,bkd->bsd', _ctx_512c, _ctx_512P)
        _ctx_512t = _ctx_512t * jax.lax.rsqrt(jnp.mean(jnp.square(_ctx_512t)) + 1e-12) * 0.953939
        ctx_512 = -0.000392918 + 0.999932 * (_ctx_512t + 0.3 * jax.random.normal(jax.random.fold_in(_rk, 611), (4, 512, 128), jnp.float32))
        _g = jax.random.normal(jax.random.fold_in(_rk, 9001), (2, 2), jnp.float32)
        _g = jnp.sign(_g) * jnp.maximum(jnp.abs(_g), 1.0) + (_g == 0) * 1.0
        g_xattn = _g[0]
        g_ffn = _g[1]
        return (x, ctx_512, g_xattn, g_ffn)
    x, ctx_512, g_xattn, g_ffn = _rec_inputs()

    def _L0_xattn_setup():
        import jax, jax.numpy as jnp
        import numpy as np
        B, N, D = (16, 512, 128)
        H = 4
        TOP_K_RATIO = 0.3
        key = jax.random.key(seed)
        k1, k2, k3, k4 = jax.random.split(key, 4)
        h = jax.random.normal(k1, (B, N, D), dtype=jnp.float32)
        adj_raw = jax.random.uniform(k2, (B, N, N), dtype=jnp.float32)
        lim = 1.0 / np.sqrt(D)
        Wq = jax.random.uniform(k3, (D, D), minval=-lim, maxval=lim, dtype=jnp.float32)
        Wk = jax.random.uniform(k4, (D, D), minval=-lim, maxval=lim, dtype=jnp.float32)
        gamma_raw = jnp.float32(-0.85)
        return {'h': h, 'adj_raw': adj_raw, 'Wq': Wq, 'Wk': Wk, 'gamma_raw': gamma_raw}
    _L0_xattn_all = _L0_xattn_setup()
    _L0_xattn_in = {k: v for k, v in _L0_xattn_all.items() if k in ('Wq', 'Wk', 'gamma_raw')}
    del _L0_xattn_all

    def _L0_ffn_setup():
        import jax, jax.numpy as jnp
        import numpy as np
        B, S, D = (2, 512, 512)
        E, TOP_K, H = (8, 2, 256)
        HS = 512
        key = jax.random.key(seed)
        ks = jax.random.split(key, 8)
        sc_d = 1.0 / np.sqrt(D)
        sc_h = 1.0 / np.sqrt(H)
        sc_hs = 1.0 / np.sqrt(HS)
        return {'hidden_states': jax.random.normal(ks[0], (B, S, D), jnp.float32), 'router_w': jax.random.normal(ks[1], (D, E), jnp.float32) * sc_d, 'w_gate': jax.random.normal(ks[2], (E, D, H), jnp.float32) * sc_d, 'w_up': jax.random.normal(ks[3], (E, D, H), jnp.float32) * sc_d, 'w_down': jax.random.normal(ks[4], (E, H, D), jnp.float32) * sc_h, 'sw_gate': jax.random.normal(ks[5], (D, HS), jnp.float32) * sc_d, 'sw_up': jax.random.normal(ks[6], (D, HS), jnp.float32) * sc_d, 'sw_down': jax.random.normal(ks[7], (HS, D), jnp.float32) * sc_hs}
    _L0_ffn_all = _L0_ffn_setup()
    _L0_ffn_in = {k: v for k, v in _L0_ffn_all.items() if k in ('router_w', 'w_gate', 'w_up', 'w_down', 'sw_gate', 'sw_up', 'sw_down')}
    del _L0_ffn_all

    def _L1_xattn_setup():
        import jax, jax.numpy as jnp
        import numpy as np
        EPS = 1e-06
        IMAGE_DIMS = 512
        key = jax.random.key(seed)
        k1, k2, k3 = jax.random.split(key, 3)
        B, I, J, D = (16, 512, 512, 128)
        p = jax.random.normal(k1, (B, I, J), dtype=jnp.float32)
        k_v = jax.random.normal(k2, (B, J, D), dtype=jnp.float32)
        W_k = jax.random.normal(k3, (D, D), dtype=jnp.float32) * (1.0 / np.sqrt(D))
        b_k = jnp.zeros((D,), dtype=jnp.float32)
        ln_gamma = jnp.ones((J,), dtype=jnp.float32)
        ln_beta = jnp.zeros((J,), dtype=jnp.float32)
        return {'p': p, 'k_v': k_v, 'W_k': W_k, 'b_k': b_k, 'ln_gamma': ln_gamma, 'ln_beta': ln_beta}
    _L1_xattn_all = _L1_xattn_setup()
    _L1_xattn_in = {k: v for k, v in _L1_xattn_all.items() if k in ('W_k', 'b_k', 'ln_gamma', 'ln_beta')}
    del _L1_xattn_all

    def _L1_ffn_setup():
        import jax, jax.numpy as jnp
        import numpy as np
        B_, S, D = (2, 512, 512)
        F_ = 2048
        R = 16
        H = 16
        HD = D // H
        MOD_SCALE = 0.1
        EPS = 1e-06

        def _rmsnorm(x, w):
            v = jnp.mean(x * x, axis=-1, keepdims=True)
            return x * jax.lax.rsqrt(v + EPS) * w

        def _attention(x, Wq, Wk, Wv, Wo):
            b, s, d = x.shape
            q = (x @ Wq.T).reshape(b, s, H, HD)
            k = (x @ Wk.T).reshape(b, s, H, HD)
            v = (x @ Wv.T).reshape(b, s, H, HD)
            scores = jnp.einsum('bqhd,bkhd->bhqk', q, k) / np.sqrt(HD).astype(np.float32)
            causal = jnp.tril(jnp.ones((s, s), bool))
            scores = jnp.where(causal, scores, jnp.finfo(scores.dtype).min)
            probs = jax.nn.softmax(scores, axis=-1)
            out = jnp.einsum('bhqk,bkhd->bqhd', probs, v).reshape(b, s, d)
            return out @ Wo.T
        key = jax.random.key(seed)
        ks = jax.random.split(key, 12)
        sd = 0.02
        return {'hidden_states': jax.random.normal(ks[0], (B_, S, D), jnp.float32), 'ln1_w': jnp.ones((D,), jnp.float32), 'ln2_w': jnp.ones((D,), jnp.float32), 'Wq': jax.random.normal(ks[1], (D, D), jnp.float32) * sd, 'Wk': jax.random.normal(ks[2], (D, D), jnp.float32) * sd, 'Wv': jax.random.normal(ks[3], (D, D), jnp.float32) * sd, 'Wo': jax.random.normal(ks[4], (D, D), jnp.float32) * sd, 'A': jax.random.normal(ks[5], (D, R), jnp.float32) * (0.01 / np.sqrt(D)), 'B': jax.random.normal(ks[6], (R, F_), jnp.float32) * (0.01 / np.sqrt(R)), 'W_in_base': jax.random.normal(ks[7], (F_, D), jnp.float32) * sd, 'W_up_base': jax.random.normal(ks[8], (F_, D), jnp.float32) * sd, 'W_down': jax.random.normal(ks[9], (D, F_), jnp.float32) * sd}
    _L1_ffn_all = _L1_ffn_setup()
    _L1_ffn_in = {k: v for k, v in _L1_ffn_all.items() if k in ('ln1_w', 'ln2_w', 'Wq', 'Wk', 'Wv', 'Wo', 'A', 'B', 'W_in_base', 'W_up_base', 'W_down')}
    del _L1_ffn_all
    return {'x': x, 'ctx_512': ctx_512, 'g_xattn': g_xattn, 'g_ffn': g_ffn, 'L0_xattn_Wq': _L0_xattn_in['Wq'], 'L0_xattn_Wk': _L0_xattn_in['Wk'], 'L0_xattn_gamma_raw': _L0_xattn_in['gamma_raw'], 'L0_ffn_router_w': _L0_ffn_in['router_w'], 'L0_ffn_w_gate': _L0_ffn_in['w_gate'], 'L0_ffn_w_up': _L0_ffn_in['w_up'], 'L0_ffn_w_down': _L0_ffn_in['w_down'], 'L0_ffn_sw_gate': _L0_ffn_in['sw_gate'], 'L0_ffn_sw_up': _L0_ffn_in['sw_up'], 'L0_ffn_sw_down': _L0_ffn_in['sw_down'], 'L1_xattn_W_k': _L1_xattn_in['W_k'], 'L1_xattn_b_k': _L1_xattn_in['b_k'], 'L1_xattn_ln_gamma': _L1_xattn_in['ln_gamma'], 'L1_xattn_ln_beta': _L1_xattn_in['ln_beta'], 'L1_ffn_ln1_w': _L1_ffn_in['ln1_w'], 'L1_ffn_ln2_w': _L1_ffn_in['ln2_w'], 'L1_ffn_Wq': _L1_ffn_in['Wq'], 'L1_ffn_Wk': _L1_ffn_in['Wk'], 'L1_ffn_Wv': _L1_ffn_in['Wv'], 'L1_ffn_Wo': _L1_ffn_in['Wo'], 'L1_ffn_A': _L1_ffn_in['A'], 'L1_ffn_B': _L1_ffn_in['B'], 'L1_ffn_W_in_base': _L1_ffn_in['W_in_base'], 'L1_ffn_W_up_base': _L1_ffn_in['W_up_base'], 'L1_ffn_W_down': _L1_ffn_in['W_down']}

def reference(x, ctx_512, g_xattn, g_ffn, L0_xattn_Wq, L0_xattn_Wk, L0_xattn_gamma_raw, L0_ffn_router_w, L0_ffn_w_gate, L0_ffn_w_up, L0_ffn_w_down, L0_ffn_sw_gate, L0_ffn_sw_up, L0_ffn_sw_down, L1_xattn_W_k, L1_xattn_b_k, L1_xattn_ln_gamma, L1_xattn_ln_beta, L1_ffn_ln1_w, L1_ffn_ln2_w, L1_ffn_Wq, L1_ffn_Wk, L1_ffn_Wv, L1_ffn_Wo, L1_ffn_A, L1_ffn_B, L1_ffn_W_in_base, L1_ffn_W_up_base, L1_ffn_W_down):
    import jax
    import jax.numpy as jnp

    def _L0_xattn_ref(h, adj_raw, Wq, Wk, gamma_raw):
        import jax, jax.numpy as jnp
        import numpy as np
        B, N, D = (16, 512, 128)
        H = 4
        TOP_K_RATIO = 0.3
        b, n, dm = h.shape
        d = dm // H
        Q = (h @ Wq.T).reshape(b, n, H, d).transpose(0, 2, 1, 3)
        K = (h @ Wk.T).reshape(b, n, H, d).transpose(0, 2, 1, 3)
        sim = jnp.einsum('bhnd,bhmd->bnm', Q, K) / (jnp.sqrt(jnp.float32(d)) * H)
        k = max(1, int(n * TOP_K_RATIO))
        topk_vals = jax.lax.top_k(sim, k)[0]
        threshold = topk_vals[:, :, -1:]
        sparse_mask = (sim >= threshold).astype(sim.dtype)
        A_learned = jax.nn.sigmoid(sim) * sparse_mask
        A_learned = (A_learned + jnp.swapaxes(A_learned, -1, -2)) * 0.5
        gamma = jax.nn.sigmoid(gamma_raw)
        return (1.0 - gamma) * adj_raw + gamma * A_learned

    def _L0_ffn_ref(hidden_states, router_w, w_gate, w_up, w_down, sw_gate, sw_up, sw_down):
        import jax, jax.numpy as jnp
        import numpy as np
        B, S, D = (2, 512, 512)
        E, TOP_K, H = (8, 2, 256)
        HS = 512
        b, s, d = hidden_states.shape
        x = hidden_states.reshape(-1, d)
        T = x.shape[0]
        logits = x @ router_w
        probs = jax.nn.softmax(logits, axis=-1)
        topk_w, topk_idx = jax.lax.top_k(probs, TOP_K)
        topk_w = topk_w / jnp.sum(topk_w, axis=-1, keepdims=True)
        g = jnp.einsum('td,edh->teh', x, w_gate)
        u = jnp.einsum('td,edh->teh', x, w_up)
        h = jax.nn.silu(g) * u
        y = jnp.einsum('teh,ehd->ted', h, w_down)
        combine = jnp.zeros((T, E), dtype=x.dtype)
        combine = combine.at[jnp.arange(T)[:, None], topk_idx].add(topk_w)
        routed = jnp.einsum('te,ted->td', combine, y)
        sh = jax.nn.silu(hidden_states @ sw_gate) * (hidden_states @ sw_up)
        shared = sh @ sw_down
        return routed.reshape(b, s, d) + shared

    def _L1_xattn_ref(p, k_v, W_k, b_k, ln_gamma, ln_beta):
        import jax, jax.numpy as jnp
        import numpy as np
        EPS = 1e-06
        IMAGE_DIMS = 512
        kv = k_v @ W_k.T + b_k
        out = jnp.einsum('bij,bjd->bid', p, kv)
        scale = IMAGE_DIMS ** (-0.5)
        sim = jnp.einsum('bid,bjd->bij', out, kv) * scale
        mu = jnp.mean(sim, axis=-1, keepdims=True)
        var = jnp.var(sim, axis=-1, keepdims=True)
        sim = (sim - mu) * jax.lax.rsqrt(var + EPS) * ln_gamma + ln_beta
        attn = jax.nn.softmax(sim, axis=-1)
        return attn

    def _L1_ffn_ref(hidden_states, ln1_w, ln2_w, Wq, Wk, Wv, Wo, A, B, W_in_base, W_up_base, W_down):
        import jax, jax.numpy as jnp
        import numpy as np
        B_, S, D = (2, 512, 512)
        F_ = 2048
        R = 16
        H = 16
        HD = D // H
        MOD_SCALE = 0.1
        EPS = 1e-06

        def _rmsnorm(x, w):
            v = jnp.mean(x * x, axis=-1, keepdims=True)
            return x * jax.lax.rsqrt(v + EPS) * w

        def _attention(x, Wq, Wk, Wv, Wo):
            b, s, d = x.shape
            q = (x @ Wq.T).reshape(b, s, H, HD)
            k = (x @ Wk.T).reshape(b, s, H, HD)
            v = (x @ Wv.T).reshape(b, s, H, HD)
            scores = jnp.einsum('bqhd,bkhd->bhqk', q, k) / np.sqrt(HD).astype(np.float32)
            causal = jnp.tril(jnp.ones((s, s), bool))
            scores = jnp.where(causal, scores, jnp.finfo(scores.dtype).min)
            probs = jax.nn.softmax(scores, axis=-1)
            out = jnp.einsum('bhqk,bkhd->bqhd', probs, v).reshape(b, s, d)
            return out @ Wo.T
        residual = hidden_states
        x = _rmsnorm(hidden_states, ln1_w)
        attn = _attention(x, Wq, Wk, Wv, Wo)
        mod = MOD_SCALE * jnp.tanh(attn @ A)
        h = _rmsnorm(residual, ln2_w)
        gate_pre = h @ W_in_base.T + mod * (h @ A) @ B
        gate = jax.nn.silu(gate_pre)
        up = h @ W_up_base.T
        mlp_out = gate * up @ W_down.T
        return residual + mlp_out
    x = x + jnp.tanh(g_xattn[0]) * _L0_xattn_ref(ctx_512, _layernorm(x, axis=-1), L0_xattn_Wq, L0_xattn_Wk, L0_xattn_gamma_raw)
    x = x + jnp.tanh(g_ffn[0]) * _L0_ffn_ref(_layernorm(x, axis=-1), L0_ffn_router_w, L0_ffn_w_gate, L0_ffn_w_up, L0_ffn_w_down, L0_ffn_sw_gate, L0_ffn_sw_up, L0_ffn_sw_down)
    x = x + jnp.tanh(g_xattn[1]) * _L1_xattn_ref(_layernorm(x, axis=-1), ctx_512, L1_xattn_W_k, L1_xattn_b_k, L1_xattn_ln_gamma, L1_xattn_ln_beta)
    x = x + jnp.tanh(g_ffn[1]) * _L1_ffn_ref(_layernorm(x, axis=-1), L1_ffn_ln1_w, L1_ffn_ln2_w, L1_ffn_Wq, L1_ffn_Wk, L1_ffn_Wv, L1_ffn_Wo, L1_ffn_A, L1_ffn_B, L1_ffn_W_in_base, L1_ffn_W_up_base, L1_ffn_W_down)
    return x

_drawn_inputs = setup_inputs


def setup_inputs(seed=0):
    import zlib

    import numpy as np

    out = dict(_drawn_inputs(seed))
    spreads = {'g_ffn': (-1.0, 0.2),
     'L1_xattn_b_k': (0.0, 2.0),
     'L1_xattn_ln_gamma': (1.0, 0.6),
     'L1_xattn_ln_beta': (0.0, 2.0),
     'L1_ffn_ln1_w': (1.0, 0.6),
     'L1_ffn_ln2_w': (1.0, 0.2)}
    factors = {'L1_xattn_W_k': 200.0,
     'L1_ffn_Wq': 200.0,
     'L1_ffn_Wk': 200.0,
     'L1_ffn_Wv': 200.0,
     'L1_ffn_Wo': 200.0,
     'L1_ffn_A': 200.0,
     'L1_ffn_B': 200.0}
    for name, (base, spread) in spreads.items():
        noise = np.random.default_rng([zlib.crc32(name.encode()), seed]).standard_normal(out[name].shape)
        drawn = base * np.exp(spread * noise) if base else spread * noise
        out[name] = jnp.asarray(drawn.astype(out[name].dtype))
    for name, factor in factors.items():
        out[name] = (out[name] * factor).astype(out[name].dtype)
    return out
```

```python
from contextlib import ExitStack

import concourse.bass as bass
from concourse import mybir

P = 128
F32 = mybir.dt.float32
F32R = mybir.dt.float32r
BF16 = mybir.dt.bfloat16
U32 = mybir.dt.uint32
I32 = mybir.dt.int32
ALU = mybir.AluOpType
ACT = mybir.ActivationFunctionType
AX = mybir.AxisListType.X

B, N, D = 4, 512, 512
C = 128
T = B * N // P
R = N // P
DC = D // P
LN_EPS = 1e-5

GRAPH_HEADS = 4
GRAPH_SCALE = 1.0 / ((C // GRAPH_HEADS) ** 0.5 * GRAPH_HEADS)
TOP = int(N * 0.3)
HALVINGS = 24
MEAN_TO_LOW = (N / (N - TOP + 1) - 1) ** 0.5
MEAN_TO_HIGH = (N / TOP - 1) ** 0.5
VT = 7
ST = T - VT

GROUPS = (slice(0, (ST + 1) // 2), slice((ST + 1) // 2, ST))

E_ = 8
UH = 256
HC = UH // P
MOE_UNITS = E_ + 2
KV_EPS = 1e-6
KV_SCALE = N ** -0.5
HEADS = 16
HD = D // HEADS
RK = 16
F_ = 2048
MLP_UNITS = F_ // UH
ATT_SCALE = 1.0 / HD ** 0.5
MOD_SCALE = 0.1
MASKED = -1e30
TB = B * N // 512

GU_LEAD = 2
Y_LEAD = 32
ACC_LEAD = 16


def chained(eng, sem, start):
    n = [0]

    def step(ins):
        n[0] += 1
        ins.then_inc(sem, 1)
        eng.wait_ge(sem, start + n[0])
    return step


def flamingo_kernel(nc, x_in, ctxT_in, g_xattn, g_ffn, gr_Wq, gr_Wk, gr_gamma, router_w, w_gate, w_up,
                    w_down, sw_gate, sw_up, sw_down, WkT, b_k, ln_gamma, ln_beta, ln1_w, ln2_w, WqT,
                    WkT1, Wv, Wo, A_in, B_in, W_inT, W_upT, W_downT, out, stop=99):
    with ExitStack() as ctx:
        def sb(name, shape, dt=F32, scope=ctx):
            return scope.enter_context(nc.sbuf_tensor(name, shape, dt))

        def sem(name):
            return ctx.enter_context(nc.semaphore(name))

        bank = ctx.enter_context(nc.psum_tensor("bank", [P, 8, 512], F32))
        x = sb("x", [P, T, D])
        ident = sb("ident", [P, P])
        gates = sb("gates", [P, 8])
        tg = sb("tg", [P, 4])
        gam = sb("gam", [P, 1])
        stats = sb("stats", [P, T, 6])
        mv = sb("mv", [P, T, 2])
        half = sb("half", [P, T])
        rstd = sb("rstd", [P, T])
        nmr = sb("nmr", [P, T])
        sm1 = sb("sm1", [P, T])
        x_dram = x_in.rearrange("b (r p) d -> p (b r) d", p=P)
        out_dram = out.rearrange("b (r p) d -> p (b r) d", p=P)

        phase_graph(nc, sb, sem, locals())
        if stop >= 2:
            phase_moe(nc, sb, sem, locals())
        if stop >= 3:
            phase_kv(nc, sb, sem, locals())
        if stop >= 4:
            phase_attention_mlp(nc, sb, sem, locals())
        s_out = sem("x_stored")
        with nc.Block() as block:
            @block.sync
            def _(sp):
                sp.dma_start(out_dram[:, 0:8, :], x[:, 0:8, :]).then_inc(s_out, 16)
                sp.dma_start(out_dram[:, 8:16, :], x[:, 8:16, :]).then_inc(s_out, 16)
                sp.wait_ge(s_out, 32)


def rstd_steps(pool, v, mv_, scale, eps, half, rstd, nmr, step):
    step(pool.tensor_scalar(v, mv_[:, :, 1], scale, eps, ALU.mult, ALU.add))
    step(pool.tensor_tensor(rstd, v, half, ALU.pow))
    step(pool.tensor_tensor(nmr, mv_[:, :, 0], rstd, ALU.mult))
    return pool.tensor_scalar(nmr, nmr, -1.0, None, ALU.mult)


def phase_graph(nc, sb, sem, g):
    x, bank, ident, gates, tg, gam = g["x"], g["bank"], g["ident"], g["gates"], g["tg"], g["gam"]
    stats, mv, half, rstd, nmr, sm1 = g["stats"], g["mv"], g["half"], g["rstd"], g["nmr"], g["sm1"]
    with ExitStack() as scope:
        def s_(name, shape, dt=F32):
            return sb(name, shape, dt, scope)
        S = s_("sim", [P, T, N])
        ctxT = s_("gr_ctxT", [P, B, N])
        wq = s_("gr_wq", [C, C])
        wk = s_("gr_wk", [C, C])
        M = s_("gr_M", [C, C])
        Z = s_("gr_Z", [P, B, N])
        sst = s_("sim_stats", [P, T, 6])
        smv = s_("sim_mv", [P, T, 2])
        sg = s_("sig", [P, 2, N])
        yb = s_("yb", [P, 2, N])
        tb = s_("tb", [P, 2, N])
        junk_v = s_("junk_v", [P, VT, N], BF16)
        junk_s = s_("junk_s", [P, ST, N], BF16)
        width = s_("width", [P, T])
        low = s_("low", [P, T])
        mid = s_("mid", [P, T])
        cnt = s_("cnt", [P, T])
        sel = s_("selc", [P, T])
        nlow = s_("nlow", [P, ST])
        nmid = s_("nmid", [P, ST])
        slack = s_("slack", [P, T])
        sigma = s_("sigma", [P, T])
        sc1 = s_("sc1", [P, T])
        bi1 = s_("bi1", [P, T])
        c1 = s_("c1", [P, 1])
        c2 = s_("c2", [P, 1])

        x_in_s = [sem(f"gr_x_arrived{b}") for b in range(B)]
        w_in = sem("gr_weights_arrived")
        c_in = sem("gr_ctx_arrived")
        g_in = sem("gr_gates_arrived")
        m_ps = sem("gr_M_done")
        m_sb = sem("gr_M_copied")
        z_ps = sem("gr_Z_done")
        z_sb = sem("gr_Z_copied")
        s_ps = sem("gr_sim_done")
        s_sb = sem("gr_sim_copied")
        cst = sem("gr_constants")
        vch = sem("gr_vector_chain")
        pch = sem("gr_pool_chain")
        lnst = sem("gr_ln_stats")
        sim_st = sem("gr_sim_stats")
        brk = sem("gr_bracket_ready")
        nmid_r = [sem(f"gr_negmid_ready{h}") for h in range(2)]
        cnt_s = sem("gr_signs_counted")
        gat = sem("gr_gates_ready")
        coef = sem("gr_coefs_ready")
        sig_r = sem("gr_sigmoid_ready")
        a_r = sem("gr_A_ready")
        at_r = sem("gr_AT_ready")
        y_r = sem("gr_y_ready")
        t_r = sem("gr_t_ready")
        x_r = sem("gr_x_ready")

        with nc.Block() as block:
            @block.sync
            def _(sp):
                sp.dma_start(wq[:], g["gr_Wq"]).then_inc(w_in, 16)
                sp.dma_start(wk[:], g["gr_Wk"]).then_inc(w_in, 16)
                sp.dma_start(ctxT[:], g["ctxT_in"].rearrange("c (b n) -> c b n", b=B)).then_inc(c_in, 16)
                for k, (src, n) in enumerate(((g["g_xattn"], 2), (g["g_ffn"], 2), (g["gr_gamma"], 1))):
                    sp.dma_start(gates[:, 2 * k:2 * k + n], src.partition_broadcast(P)).then_inc(g_in, 16)
                for b in range(B):
                    sp.dma_start(x[:, R * b:R * b + R, :], g["x_dram"][:, R * b:R * b + R, :])\
                      .then_inc(x_in_s[b], 16)

            @block.tensor
            def _(pe):
                pe.wait_ge(w_in, 32)
                pe.matmul(bank[:, 0, 0:C], wq[:], wk[:], start=True, stop=True).then_inc(m_ps, 1)
                pe.wait_ge(m_sb, 1)
                pe.wait_ge(c_in, 16)
                for b in range(B):
                    if b >= 2:
                        pe.wait_ge(z_sb, b - 1)
                    pe.matmul(bank[:, b % 2, :], M[:], ctxT[:, b, :], start=True, stop=True).then_inc(z_ps, 1)
                    pe.wait_ge(z_sb, b + 1)
                    for r in range(R):
                        t = R * b + r
                        if t >= 6:
                            pe.wait_ge(s_sb, t - 5)
                        pe.matmul(bank[:, 2 + t % 6, :], Z[:, b, r * P:(r + 1) * P], ctxT[:, b, :],
                                  start=True, stop=True).then_inc(s_ps, 1)
                pe.wait_ge(cst, 1)
                for b in range(B):
                    pe.wait_ge(a_r, R * (b + 1))
                    for r in range(R):
                        t = R * b + r
                        if t >= 8:
                            pe.wait_ge(t_r, t - 7)
                        if t == 0:
                            pe.wait_ge(s_sb, T)
                        for q in range(R):
                            last = pe.transpose(bank[:, t % 8, q * P:(q + 1) * P],
                                                S[:, R * b + q, r * P:(r + 1) * P], ident[:])
                        last.then_inc(at_r, 1)

            @block.scalar
            def _(act):
                act.wait_ge(g_in, 48)
                act.activation(tg[:], gates[:, 0:4], ACT.Tanh)
                act.activation(gam[:], gates[:, 4:5], ACT.Sigmoid).then_inc(gat, 1)
                act.wait_ge(m_ps, 1)
                act.activation(M[:], bank[:, 0, 0:C], ACT.Copy).then_inc(m_sb, 1)
                for b in range(B):
                    act.wait_ge(z_ps, b + 1)
                    act.activation(Z[:, b, :], bank[:, b % 2, :], ACT.Copy).then_inc(z_sb, 1)
                    for r in range(R):
                        t = R * b + r
                        act.wait_ge(s_ps, t + 1)
                        act.activation(S[:, t, :], bank[:, 2 + t % 6, :], ACT.Copy).then_inc(s_sb, 1)
                with act.Fori(0, HALVINGS) as i:
                    for h in range(2):
                        act.wait_ge(nmid_r[h], i + 1)
                        for j in range(GROUPS[h].start, GROUPS[h].stop):
                            last = act.activation(junk_s[:, j, :], S[:, VT + j, :], ACT.Sign, bias=nmid[:, j:j + 1],
                                                  accum_out=cnt[:, VT + j:VT + j + 1])
                        last.then_inc(cnt_s, 1)
                act.wait_ge(coef, 1)
                act.wait_ge(x_in_s[3], 16)
                for t in range(T):
                    if t >= 2:
                        act.wait_ge(a_r, t - 1)
                    act.activation(sg[:, t % 2, :], S[:, t, :], ACT.Sigmoid, scale=GRAPH_SCALE).then_inc(sig_r, 1)
                for t in range(T):
                    if t >= 2:
                        act.wait_ge(x_r, t - 1)
                    act.activation(yb[:, t % 2, :], x[:, t, :], ACT.Identity, bias=bi1[:, t:t + 1],
                                   scale=sc1[:, t:t + 1]).then_inc(y_r, 1)

            @block.gpsimd
            def _(pool):
                step = chained(pool, pch, 0)
                step(pool.memset(ident[:], 0.0))
                step(pool.memset(half[:], -0.5))
                pool.affine_select(out=ident[:], in_=ident[:], compare_op=ALU.not_equal, fill=1.0, base=0,
                                   pattern=[[-1, P]], channel_multiplier=1).then_inc(cst, 1)
                pool.wait_ge(lnst, 1)
                step(rstd_steps(pool, sm1[:], mv, 1.0, LN_EPS, half[:], rstd[:], nmr[:], step))
                pool.wait_ge(gat, 1)
                step(pool.tensor_scalar(c1[:], gam[:], -1.0, 1.0, ALU.mult, ALU.add))
                step(pool.tensor_tensor(c1[:], c1[:], tg[:, 0:1], ALU.mult))
                step(pool.tensor_tensor(c2[:], gam[:], tg[:, 0:1], ALU.mult))
                step(pool.tensor_scalar(c2[:], c2[:], 0.5, None, ALU.mult))
                step(pool.tensor_scalar(sc1[:], rstd[:], c1[:, 0:1], 1.0, ALU.mult, ALU.add))
                pool.tensor_scalar(bi1[:], nmr[:], c1[:, 0:1], 0.0, ALU.mult, ALU.add).then_inc(coef, 1)
                pool.wait_ge(sim_st, 1)
                mean, var = smv[:, :, 0], smv[:, :, 1]
                step(pool.tensor_scalar(half[:], half[:], -1.0, None, ALU.mult))
                step(pool.tensor_tensor(sigma[:], var, half[:], ALU.pow))
                step(pool.tensor_tensor(slack[:], mean, mean, ALU.mult))
                step(pool.tensor_tensor(slack[:], slack[:], var, ALU.add))
                step(pool.tensor_tensor(slack[:], slack[:], half[:], ALU.pow))
                step(pool.tensor_scalar(half[:], half[:], -1.0, None, ALU.mult))
                step(pool.tensor_scalar(slack[:], slack[:], 2.0 ** -18, None, ALU.mult))
                step(pool.tensor_scalar(low[:], sigma[:], -1.02 * MEAN_TO_LOW, None, ALU.mult))
                step(pool.tensor_tensor(low[:], low[:], mean, ALU.add))
                step(pool.tensor_tensor(low[:], low[:], slack[:], ALU.subtract))
                step(pool.tensor_scalar(width[:], sigma[:], 1.04 * (MEAN_TO_LOW + MEAN_TO_HIGH), None, ALU.mult))
                step(pool.tensor_tensor(width[:], width[:], slack[:], ALU.add))
                step(pool.tensor_tensor(width[:], width[:], slack[:], ALU.add))
                pool.tensor_scalar(width[:], width[:], 0.5, None, ALU.mult).then_inc(brk, 1)
                pool.wait_ge(brk, 1)
                step(pool.tensor_scalar(nlow[:], low[:, VT:T], -1.0, None, ALU.mult))
                for h, own in enumerate(GROUPS):
                    at = slice(VT + own.start, VT + own.stop)
                    pool.tensor_tensor(nmid[:, own], nlow[:, own], width[:, at], ALU.subtract).then_inc(nmid_r[h], 1)

            @block.vector
            def _(dve):
                step = chained(dve, vch, 0)
                for b in range(B):
                    dve.wait_ge(x_in_s[b], 16)
                    for t in range(R * b, R * b + R):
                        last = dve.bn_stats(stats[:, t, :], x[:, t, :])
                step(last)
                for t in range(T):
                    last = dve.bn_aggr(mv[:, t, :], stats[:, t, :])
                last.then_inc(lnst, 1)
                for t in range(T):
                    dve.wait_ge(s_sb, t + 1)
                    last = dve.bn_stats(sst[:, t, :], S[:, t, :])
                step(last)
                for t in range(T):
                    last = dve.bn_aggr(smv[:, t, :], sst[:, t, :])
                last.then_inc(sim_st, 1)
                own = slice(0, VT)
                dve.wait_ge(brk, 1)
                step(dve.tensor_tensor(mid[:, own], low[:, own], width[:, own], ALU.add))
                uch = sem("gr_vector_search_chain")
                with dve.Fori(0, HALVINGS) as i:
                    step = chained(dve, uch, 9 * i)

                    def renew(h):
                        own, at = GROUPS[h], slice(VT + GROUPS[h].start, VT + GROUPS[h].stop)
                        dve.wait_ge(cnt_s, 2 * i + h + 1)
                        step(dve.scalar_tensor_tensor(sel[:, at], cnt[:, at], float(2 * TOP - N), width[:, at],
                                                      ALU.is_ge, ALU.mult))
                        step(dve.tensor_tensor(nlow[:, own], nlow[:, own], sel[:, at], ALU.subtract))
                        dve.scalar_tensor_tensor(nmid[:, own], width[:, at], -0.5, nlow[:, own], ALU.mult, ALU.add)\
                           .then_inc(nmid_r[h], 1)

                    for t in range(VT):
                        last = dve.tensor_scalar(junk_v[:, t, :], S[:, t, :], mid[:, t:t + 1], None, ALU.is_ge,
                                                 ALU.add, accum_out=cnt[:, t:t + 1])
                        if t == VT // 2:
                            renew(0)
                    step(last)
                    step(dve.scalar_tensor_tensor(sel[:, own], cnt[:, own], float(TOP) - 0.5, width[:, own],
                                                  ALU.is_ge, ALU.mult))
                    step(dve.tensor_tensor(low[:, own], low[:, own], sel[:, own], ALU.add))
                    step(dve.scalar_tensor_tensor(mid[:, own], width[:, own], 0.5, low[:, own], ALU.mult, ALU.add))
                    renew(1)
                    for h in range(2):
                        dve.wait_ge(nmid_r[h], i + 2)
                    step(dve.tensor_scalar(width[:], width[:], 0.5, None, ALU.mult))
                step = chained(dve, vch, 2)
                step(dve.tensor_scalar(low[:, VT:T], nlow[:], -1.0, None, ALU.mult))
                for t in range(T):
                    dve.wait_ge(sig_r, t + 1)
                    dve.scalar_tensor_tensor(S[:, t, :], S[:, t, :], low[:, t:t + 1], sg[:, t % 2, :],
                                             ALU.is_ge, ALU.mult).then_inc(a_r, 1)
                for t in range(T):
                    dve.wait_ge(at_r, t + 1)
                    dve.tensor_tensor(tb[:, t % 2, :], bank[:, t % 8, :], S[:, t, :], ALU.add).then_inc(t_r, 1)
                    dve.wait_ge(t_r, t + 1)
                    dve.wait_ge(y_r, t + 1)
                    dve.scalar_tensor_tensor(x[:, t, :], tb[:, t % 2, :], c2[:, 0:1], yb[:, t % 2, :],
                                             ALU.mult, ALU.add).then_inc(x_r, 1)


def phase_moe(nc, sb, sem, g):
    x, bank, ident, tg, stats, mv = g["x"], g["bank"], g["ident"], g["tg"], g["stats"], g["mv"]
    half, rstd, nmr, sm1 = g["half"], g["rstd"], g["nmr"], g["sm1"]
    with ExitStack() as scope:
        def s_(name, shape, dt=F32):
            return sb(name, shape, dt, scope)
        xT_hi = s_("moe_xT_hi", [P, DC, B * N], F32R)
        xT_lo = s_("moe_xT_lo", [P, DC, B * N], F32R)
        coefs = s_("moe_coefs", [P, MOE_UNITS, T])
        with ExitStack() as inner:
            def i_(name, shape, dt=F32):
                return sb(name, shape, dt, inner)
            xn = i_("moe_xn", [P, 2, D])
            rw = i_("moe_rw", [P, DC, E_])
            rw_hi = i_("moe_rw_hi", [P, DC, E_], F32R)
            rw_lo = i_("moe_rw_lo", [P, DC, E_], F32R)
            logits = i_("moe_logits", [P, T, E_])
            best = i_("moe_best", [P, T, 8])
            best_at = i_("moe_best_at", [P, T, 8], U32)
            at_f = i_("moe_at_f", [P, 2, T])
            gap = i_("moe_gap", [P, T])
            w2 = i_("moe_w2", [P, T])
            w1 = i_("moe_w1", [P, T])
            eids = i_("moe_eids", [P, E_, T], I32)
            eids_f = i_("moe_eids_f", [P, E_, T])
            pick = i_("moe_pick", [P, E_, T])

            rw_in = sem("moe_router_arrived")
            rw_h = sem("moe_router_hi")
            rw_l = sem("moe_router_lo")
            st_r = sem("moe_stats_ready")
            ln_r = sem("moe_rstd_ready")
            xn_r = sem("moe_xn_ready")
            xt_p = sem("moe_xT_transposed")
            xt_h = sem("moe_xT_hi_ready")
            xt_l = sem("moe_xT_lo_ready")
            lg_p = sem("moe_logits_done")
            gp_r = sem("moe_gap_ready")
            ex_r = sem("moe_exp_ready")
            io_r = sem("moe_ids_ready")
            vch = sem("moe_vector_chain")
            pch = sem("moe_pool_chain")

            with nc.Block() as block:
                @block.sync
                def _(sp):
                    sp.dma_start(rw[:], g["router_w"].rearrange("(c p) e -> p c e", p=P)).then_inc(rw_in, 16)

                @block.gpsimd
                def _(pool):
                    step = chained(pool, pch, 0)
                    step(pool.iota(eids[:], pattern=[[1, E_], [0, T]], base=0, channel_multiplier=0))
                    pool.tensor_copy(eids_f[:], eids[:]).then_inc(io_r, 1)
                    pool.wait_ge(st_r, 1)
                    step(rstd_steps(pool, sm1[:], mv, 1.0, LN_EPS, half[:], rstd[:], nmr[:], step))
                    pool.tensor_copy(sm1[:], rstd[:]).then_inc(ln_r, 1)
                    pool.wait_ge(rw_h, 1)
                    pool.tensor_tensor(rw_lo[:], rw[:], rw_hi[:].bitcast(F32), ALU.subtract).then_inc(rw_l, 1)

                @block.scalar
                def _(act):
                    act.wait_ge(rw_in, 16)
                    act.activation(rw_hi[:], rw[:], ACT.Copy).then_inc(rw_h, 1)
                    act.wait_ge(ln_r, 1)

                    def normalise(t):
                        if t >= 2:
                            act.wait_ge(xt_p, t - 1)
                        act.activation(xn[:, t % 2, :], x[:, t, :], ACT.Identity, bias=nmr[:, t:t + 1],
                                       scale=rstd[:, t:t + 1]).then_inc(xn_r, 1)

                    normalise(0)
                    for t in range(T):
                        if t + 1 < T:
                            normalise(t + 1)
                        act.wait_ge(xt_p, t + 1)
                        act.activation(xT_hi[:, :, t * P:(t + 1) * P],
                                       bank[:, t % 4, :].rearrange("p (c n) -> p c n", c=DC), ACT.Copy)\
                           .then_inc(xt_h, 1)
                    act.wait_ge(gp_r, 1)
                    act.activation(w2[:], gap[:], ACT.Exp).then_inc(ex_r, 1)

                def router(pe, t):
                    pe.wait_ge(xt_l, t + 1)
                    at = slice(t * P, (t + 1) * P)
                    passes = [(a, w, c) for c in range(DC) for a, w in ((xT_hi, rw_hi), (xT_hi, rw_lo), (xT_lo, rw_hi))]
                    for k, (a, w, c) in enumerate(passes):
                        last = pe.matmul(bank[:, 4, t * E_:(t + 1) * E_], a[:, c, at], w[:, c, :],
                                         start=k == 0, stop=k == len(passes) - 1)
                    last.then_inc(lg_p, 1)

                @block.tensor
                def _(pe):
                    pe.wait_ge(rw_l, 1)
                    for t in range(T):
                        pe.wait_ge(xn_r, t + 1)
                        if t >= 4:
                            pe.wait_ge(xt_l, t - 3)
                        for c in range(DC):
                            last = pe.transpose(bank[:, t % 4, c * P:(c + 1) * P], xn[:, t % 2, c * P:(c + 1) * P],
                                                ident[:])
                        last.then_inc(xt_p, 1)
                        if t >= 1:
                            router(pe, t - 1)
                    router(pe, T - 1)

                @block.vector
                def _(dve):
                    step = chained(dve, vch, 0)
                    for t in range(T):
                        last = dve.bn_stats(stats[:, t, :], x[:, t, :])
                    step(last)
                    for t in range(T):
                        last = dve.bn_aggr(mv[:, t, :], stats[:, t, :])
                    last.then_inc(st_r, 1)
                    for t in range(T):
                        dve.wait_ge(xt_h, t + 1)
                        at = slice(t * P, (t + 1) * P)
                        dve.tensor_tensor(xT_lo[:, :, at], bank[:, t % 4, :].rearrange("p (c n) -> p c n", c=DC),
                                          xT_hi[:, :, at].bitcast(F32), ALU.subtract).then_inc(xt_l, 1)
                    dve.wait_ge(lg_p, T)
                    step(dve.tensor_copy(logits[:], bank[:, 4, 0:T * E_].rearrange("p (t e) -> p t e", e=E_)))
                    for t in range(T):
                        last = dve.max(best[:, t, :], logits[:, t, :])
                    step(last)
                    dve.tensor_tensor(gap[:], best[:, :, 1], best[:, :, 0], ALU.subtract).then_inc(gp_r, 1)
                    for t in range(T):
                        last = dve.max_index(best_at[:, t, :], best[:, t, :], logits[:, t, :])
                    step(last)
                    step(dve.tensor_copy(at_f[:], best_at[:, :, 0:2].rearrange("p t k -> p k t")))
                    dve.wait_ge(ex_r, 1)
                    step(dve.tensor_scalar(w1[:], w2[:], 1.0, None, ALU.add))
                    step(dve.reciprocal(w1[:], w1[:]))
                    step(dve.tensor_scalar(w1[:], w1[:], tg[:, 2:3], None, ALU.mult))
                    step(dve.tensor_tensor(w2[:], w2[:], w1[:], ALU.mult))
                    dve.wait_ge(io_r, 1)
                    for k, w in ((0, w1), (1, w2)):
                        dst = coefs[:, 0:E_, :] if k == 0 else pick[:]
                        each = at_f[:, k, :].unsqueeze(1).broadcast_to([P, E_, T])
                        step(dve.tensor_tensor(dst, eids_f[:], each, ALU.is_equal))
                        step(dve.tensor_tensor(dst, dst, w[:].unsqueeze(1).broadcast_to([P, E_, T]), ALU.mult))
                    step(dve.tensor_tensor(coefs[:, 0:E_, :], coefs[:, 0:E_, :], pick[:], ALU.add))
                    ones = coefs[:, E_:MOE_UNITS, :]
                    step(dve.memset(ones, 1.0))
                    step(dve.tensor_scalar(ones, ones, tg[:, 2:3], None, ALU.mult))

        def source(u, p, loop):
            if loop:
                return (g["w_gate"][u].rearrange("(c p) h -> p c h", p=P),
                        g["w_up"][u].rearrange("(c p) h -> p c h", p=P),
                        g["w_down"][u].rearrange("(k p) d -> p k d", p=P))
            at = slice(p * UH, (p + 1) * UH)
            return (g["sw_gate"][:, at].rearrange("(c p) h -> p c h", p=P),
                    g["sw_up"][:, at].rearrange("(c p) h -> p c h", p=P),
                    g["sw_down"][at, :].rearrange("(k p) d -> p k d", p=P))

        gated_units(nc, s_, sem, "moe", x, bank, xT_hi, xT_lo, MOE_UNITS, source, coefs=coefs)


def gated_units(nc, s_, sem, tag, x, bank, xT_hi, xT_lo, units, source, coefs=None, gate=None, mod=None):
    raw_g = s_(tag + "_raw_g", [P, DC, UH])
    raw_u = s_(tag + "_raw_u", [P, DC, UH])
    raw_d = s_(tag + "_raw_d", [P, HC, D])
    g_hi = s_(tag + "_g_hi", [P, 2, DC, UH], F32R)
    g_lo = s_(tag + "_g_lo", [P, 2, DC, UH], F32R)
    u_hi = s_(tag + "_u_hi", [P, 2, DC, UH], F32R)
    u_lo = s_(tag + "_u_lo", [P, 2, DC, UH], F32R)
    d_hi = s_(tag + "_d_hi", [P, 2, HC, D], F32R)
    d_lo = s_(tag + "_d_lo", [P, 2, HC, D], F32R)
    sil = s_(tag + "_silu", [P, HC, 512])
    hid = s_(tag + "_hidden", [P, HC, 512])
    h_hi = s_(tag + "_h_hi", [P, 2, HC, 512], F32R)
    h_lo = s_(tag + "_h_lo", [P, 2, HC, 512], F32R)
    if coefs is not None:
        coef = s_(tag + "_coef", [P, 2, T])
    if mod is not None:
        b_stack, m_stack = mod
        b_unit = s_(tag + "_b_unit", [96, 2, UH], F32R)

    w_in = sem(tag + "_w_arrived")
    w_hi = sem(tag + "_w_hi_ready")
    w_lo = sem(tag + "_w_lo_ready")
    g_ps = sem(tag + "_gate_done")
    u_ps = sem(tag + "_up_done")
    sil_r = sem(tag + "_silu_ready")
    hid_r = sem(tag + "_hidden_ready")
    hhi_r = sem(tag + "_h_hi_ready")
    hlo_r = sem(tag + "_h_lo_ready")
    y_ps = sem(tag + "_y_done")
    acc_r = sem(tag + "_y_added")
    loops = units // 2 - 1

    with nc.Block() as block:
        @block.sync
        def _(sp):
            def load(u, p, loop):
                sp.wait_ge(w_lo, u)
                for dst, src in zip((raw_g, raw_u, raw_d), source(u, p, loop)):
                    sp.dma_start(dst[:], src).then_inc(w_in, 16)
            with sp.Fori(0, loops) as i:
                for p in range(2):
                    load(2 * i + p, p, True)
            for p in range(2):
                load(2 * loops + p, p, False)

        @block.gpsimd
        def _(pool):
            def split_lo(u, p, first=False):
                if coefs is not None and not first:
                    pool.wait_ge(acc_r, 16 * u - 16 + ACC_LEAD)
                pool.wait_ge(w_hi, u + 1)
                pool.tensor_tensor(g_lo[:, p], raw_g[:], g_hi[:, p].bitcast(F32), ALU.subtract)
                if coefs is not None:
                    pool.tensor_copy(coef[:, p, :], coefs[:, u, :])
                if mod is not None:
                    pool.tensor_copy(b_unit[:, p, :], b_stack[:, bass.ds(u * UH, UH)].bitcast(F32))
                pool.tensor_tensor(u_lo[:, p], raw_u[:], u_hi[:, p].bitcast(F32), ALU.subtract)
                pool.tensor_tensor(d_lo[:, p], raw_d[:], d_hi[:, p].bitcast(F32), ALU.subtract).then_inc(w_lo, 1)

            split_lo(0, 0, first=True)
            with pool.Fori(0, loops) as i:
                for p in range(2):
                    split_lo(2 * i + p + 1, (p + 1) % 2)
            split_lo(2 * loops + 1, 1)

        @block.scalar
        def _(act):
            act.sem_inc(sil_r, GU_LEAD)

            def split_hi(u, p, first=False):
                act.wait_ge(w_in, 48 * (u + 1))
                if not first:
                    act.wait_ge(y_ps, 16 * u + Y_LEAD - 16)
                act.activation(g_hi[:, p], raw_g[:], ACT.Copy)
                act.activation(u_hi[:, p], raw_u[:], ACT.Copy)
                act.activation(d_hi[:, p], raw_d[:], ACT.Copy).then_inc(w_hi, 1)

            def hidden(n, tb):
                for c in range(HC):
                    act.wait_ge(g_ps, 2 * n + c + 1)
                    act.wait_ge(hid_r, 2 * n + c - 1 + GU_LEAD)
                    act.activation(sil[:, c, :], bank[:, 2 * c, :], ACT.Silu).then_inc(sil_r, 1)
                for c in range(HC):
                    act.wait_ge(hid_r, 2 * n + c + 1 + GU_LEAD)
                    if c == 0:
                        act.wait_ge(y_ps, 4 * n - 4 + Y_LEAD)
                    act.activation(h_hi[:, tb % 2, c, :], hid[:, c, :], ACT.Copy).then_inc(hhi_r, 1)

            def pair(i, last):
                for p in range(2):
                    for tb in range(TB):
                        n = 8 * i + 4 * p + tb
                        if not (last and p == 1 and tb == TB - 1):
                            hidden(n + 1, (tb + 1) % TB)
                        if tb == 0 and not (last and p == 1):
                            split_hi(2 * i + p + 1, (p + 1) % 2)

            split_hi(0, 0, first=True)
            hidden(0, 0)
            with act.Fori(0, loops) as i:
                pair(i, False)
            pair(loops, True)

        @block.tensor
        def _(pe):
            pe.sem_inc(y_ps, Y_LEAD)

            def gate_up(n, u, p, tb):
                if tb == 0:
                    pe.wait_ge(w_lo, u + 1)
                at = slice(tb * 512, (tb + 1) * 512)
                for c in range(HC):
                    hs = slice(c * P, (c + 1) * P)
                    for which, (w_h, w_l) in enumerate(((g_hi, g_lo), (u_hi, u_lo))):
                        pe.wait_ge((sil_r, hid_r)[which], 2 * n + c - 1 + GU_LEAD)
                        passes = [(w, a, k) for k in range(DC) for w, a in ((w_h, xT_hi), (w_h, xT_lo), (w_l, xT_hi))]
                        more = mod is not None and which == 0
                        for k, (w, a, d) in enumerate(passes):
                            last = pe.matmul(bank[:, 2 * c + which, :], w[:, p, d, hs], a[:, d, at], start=k == 0,
                                             stop=k == len(passes) - 1 and not more)
                        if more:
                            last = pe.matmul(bank[:, 2 * c, :], b_unit[:, p, hs], m_stack[:, at], start=False, stop=True)
                        last.then_inc((g_ps, u_ps)[which], 1)

            def down(n, p, tb):
                pe.wait_ge(hlo_r, 2 * n + 2 + GU_LEAD)
                for j in range(4):
                    js = slice(j * P, (j + 1) * P)
                    pe.wait_ge(acc_r, 4 * n + j - 3 + ACC_LEAD)
                    passes = [(h, w, k) for k in range(HC) for h, w in ((h_hi, d_hi), (h_hi, d_lo), (h_lo, d_hi))]
                    for k, (h, w, c) in enumerate(passes):
                        last = pe.matmul(bank[:, 4 + j, :], h[:, tb % 2, c, js], w[:, p, c, :], start=k == 0,
                                         stop=k == len(passes) - 1)
                    last.then_inc(y_ps, 1)

            def pair(i, last):
                for p in range(2):
                    for tb in range(TB):
                        n = 8 * i + 4 * p + tb
                        over = tb == TB - 1
                        if not (last and p == 1 and over):
                            gate_up(n + 1, 2 * i + p + over, (p + over) % 2, (tb + 1) % TB)
                        down(n, p, tb)

            gate_up(0, 0, 0, 0)
            with pe.Fori(0, loops) as i:
                pair(i, False)
            pair(loops, True)

        @block.vector
        def _(dve):
            dve.sem_inc(hid_r, GU_LEAD)
            dve.sem_inc(acc_r, ACC_LEAD)
            dve.sem_inc(hlo_r, GU_LEAD)

            def hidden(n, tb):
                for c in range(HC):
                    dve.wait_ge(sil_r, 2 * n + c + 1 + GU_LEAD)
                    dve.wait_ge(u_ps, 2 * n + c + 1)
                    dve.wait_ge(hlo_r, 2 * n + c - 1 + GU_LEAD)
                    dve.tensor_tensor(hid[:, c, :], bank[:, 2 * c + 1, :], sil[:, c, :], ALU.mult).then_inc(hid_r, 1)
                for c in range(HC):
                    dve.wait_ge(hhi_r, 2 * n + c + 1)
                    dve.tensor_tensor(h_lo[:, tb % 2, c, :], hid[:, c, :], h_hi[:, tb % 2, c, :].bitcast(F32),
                                      ALU.subtract).then_inc(hlo_r, 1)

            def add(n, p, tb):
                for j in range(4):
                    t = 4 * tb + j
                    dve.wait_ge(y_ps, 4 * n + j + 1 + Y_LEAD)
                    dve.wait_ge(acc_r, 4 * n + j - 15 + ACC_LEAD)
                    scalar = coef[:, p, t:t + 1] if coefs is not None else gate
                    dve.scalar_tensor_tensor(x[:, t, :], bank[:, 4 + j, :], scalar, x[:, t, :], ALU.mult, ALU.add)\
                       .then_inc(acc_r, 1)

            def pair(i, last):
                for p in range(2):
                    for tb in range(TB):
                        n = 8 * i + 4 * p + tb
                        if not (last and p == 1 and tb == TB - 1):
                            hidden(n + 1, (tb + 1) % TB)
                        add(n, p, tb)

            hidden(0, 0)
            with dve.Fori(0, loops) as i:
                pair(i, False)
            pair(loops, True)


def phase_kv(nc, sb, sem, g):
    x, bank, ident, tg, stats, mv = g["x"], g["bank"], g["ident"], g["tg"], g["stats"], g["mv"]
    half, rstd, nmr, sm1 = g["half"], g["rstd"], g["nmr"], g["sm1"]
    with ExitStack() as scope:
        def s_(name, shape, dt=F32):
            return sb(name, shape, dt, scope)
        ctxT = s_("kv_ctxT", [P, B, N])
        wk = s_("kv_wk", [C, C])
        bk = s_("kv_bk", [C, 1])
        gamma = s_("kv_gamma", [P, N])
        beta = s_("kv_beta", [P, N])
        kvT = s_("kvT", [C, 2, N])
        kv = s_("kv", [P, 2, R, C])
        xn = s_("kv_xn", [P, R, D])
        xnT = s_("kv_xnT", [P, DC, N])
        outT = s_("kv_outT", [C, 2, N])
        sst = s_("kv_sim_stats", [P, R, 6])
        smv = s_("kv_sim_mv", [P, R, 2])
        sr = s_("kv_sim_rstd", [P, R])
        sn = s_("kv_sim_nmr", [P, R])
        sv = s_("kv_sim_var", [P, R])
        y = s_("kv_y", [P, R, N])
        yb = s_("kv_yb", [P, R, N])
        nmax = s_("kv_nmax", [P, R])
        total = s_("kv_total", [P, R])
        share = s_("kv_share", [P, R])
        ex = s_("kv_exp", [P, R, N])

        w_in = sem("kv_weights_arrived")
        st_r = sem("kv_stats_ready")
        ln_r = sem("kv_rstd_ready")
        kvT_p = sem("kv_kvT_done")
        kvT_r = sem("kv_kvT_ready")
        kv_p = sem("kv_kv_transposed")
        kv_r = sem("kv_kv_ready")
        xn_r = sem("kv_xn_ready")
        xt_p = sem("kv_xnT_transposed")
        xt_r = sem("kv_xnT_ready")
        ot_p = sem("kv_outT_done")
        ot_r = sem("kv_outT_ready")
        sim_p = sem("kv_sim_done")
        sst_r = sem("kv_sim_stats_ready")
        srs_r = sem("kv_sim_rstd_ready")
        y_r = sem("kv_y_ready")
        yg_r = sem("kv_y_gamma_ready")
        yb_r = sem("kv_y_beta_ready")
        mx_r = sem("kv_max_ready")
        ex_r = sem("kv_exp_ready")
        x_r = sem("kv_x_ready")
        vch = sem("kv_vector_chain")
        vch2 = sem("kv_vector_loop_chain")
        pch = sem("kv_pool_chain")
        pch2 = sem("kv_pool_loop_chain")

        with nc.Block() as block:
            @block.sync
            def _(sp):
                sp.dma_start(ctxT[:], g["ctxT_in"].rearrange("c (b n) -> c b n", b=B)).then_inc(w_in, 16)
                sp.dma_start(wk[:], g["WkT"]).then_inc(w_in, 16)
                sp.dma_start(bk[:], g["b_k"].unsqueeze(1)).then_inc(w_in, 16)
                sp.dma_start(gamma[:], g["ln_gamma"].partition_broadcast(P)).then_inc(w_in, 16)
                sp.dma_start(beta[:], g["ln_beta"].partition_broadcast(P)).then_inc(w_in, 16)

            @block.tensor
            def _(pe):
                pe.wait_ge(w_in, 80)
                for b in range(B):
                    if b >= 1:
                        pe.wait_ge(xt_r, 4 * b - 2)
                    pe.matmul(bank[:, 0, :], wk[:], ctxT[:, b, :], start=True, stop=True).then_inc(kvT_p, 1)
                    pe.wait_ge(kvT_r, b + 1)
                    for j in range(R):
                        last = pe.transpose(bank[:, 1, j * C:(j + 1) * C], kvT[:, b % 2, j * P:(j + 1) * P], ident[:])
                    last.then_inc(kv_p, 1)
                    pe.wait_ge(xn_r, R * (b + 1))
                    for c in range(DC):
                        if b >= 1 or c >= 2:
                            pe.wait_ge(xt_r, 4 * b + c - 2)
                        if c == 2:
                            pe.wait_ge(kvT_r, b + 1)
                            pe.wait_ge(kv_r, b + 1)
                        for r in range(R):
                            last = pe.transpose(bank[:, (c + 2) % 4, r * P:(r + 1) * P], xn[:, r, c * P:(c + 1) * P],
                                                ident[:])
                        last.then_inc(xt_p, 1)
                    pe.wait_ge(kv_r, b + 1)
                    pe.wait_ge(xt_r, 4 * b + 4)
                    if b >= 1:
                        pe.wait_ge(ot_r, b)
                    for c in range(DC):
                        last = pe.matmul(bank[:, 2, :], kv[:, b % 2, c, :], xnT[:, c, :], start=c == 0, stop=c == DC - 1)
                    last.then_inc(ot_p, 1)
                    pe.wait_ge(ot_r, b + 1)
                    for r in range(R):
                        if b >= 1:
                            pe.wait_ge(y_r, R * (b - 1) + r + 1)
                        pe.matmul(bank[:, 4 + r, :], outT[:, b % 2, r * P:(r + 1) * P], kvT[:, b % 2, :],
                                  start=True, stop=True).then_inc(sim_p, 1)

            @block.scalar
            def _(act):
                act.wait_ge(ln_r, 1)
                act.wait_ge(w_in, 80)

                def prepare(b):
                    act.wait_ge(kvT_p, b + 1)
                    if b >= 2:
                        act.wait_ge(sim_p, R * (b - 1))
                    act.activation(kvT[:, b % 2, :], bank[:, 0, :], ACT.Identity, bias=bk[:, 0:1]).then_inc(kvT_r, 1)
                    act.wait_ge(kv_p, b + 1)
                    act.activation(kv[:, b % 2], bank[:, 1, :].rearrange("p (j c) -> p j c", j=R), ACT.Copy)\
                       .then_inc(kv_r, 1)
                    if b >= 1:
                        act.wait_ge(xt_p, DC * b)
                    for r in range(R):
                        t = R * b + r
                        act.activation(xn[:, r, :], x[:, t, :], ACT.Identity, bias=nmr[:, t:t + 1],
                                       scale=rstd[:, t:t + 1]).then_inc(xn_r, 1)
                    for c in range(DC):
                        act.wait_ge(xt_p, DC * b + c + 1)
                        if b >= 1:
                            act.wait_ge(ot_p, b)
                        act.activation(xnT[:, c, :], bank[:, (c + 2) % 4, :], ACT.Copy).then_inc(xt_r, 1)
                    act.wait_ge(ot_p, b + 1)
                    act.activation(outT[:, b % 2, :], bank[:, 2, :], ACT.Copy).then_inc(ot_r, 1)

                def soften(b):
                    act.wait_ge(srs_r, b + 1)
                    if b >= 1:
                        act.wait_ge(yb_r, R * b)
                    for r in range(R):
                        act.activation(y[:, r, :], bank[:, 4 + r, :], ACT.Identity, bias=sn[:, r:r + 1],
                                       scale=sr[:, r:r + 1]).then_inc(y_r, 1)
                    act.wait_ge(mx_r, b + 1)
                    if b >= 1:
                        act.wait_ge(x_r, R * b)
                    for r in range(R):
                        act.activation(ex[:, r, :], yb[:, r, :], ACT.Exp, bias=nmax[:, r:r + 1],
                                       accum_out=total[:, r:r + 1]).then_inc(ex_r, 1)

                for b in range(B):
                    prepare(b)
                    soften(b)

            @block.gpsimd
            def _(pool):
                step = chained(pool, pch, 0)
                pool.wait_ge(st_r, 1)
                step(rstd_steps(pool, sm1[:], mv, 1.0, LN_EPS, half[:], rstd[:], nmr[:], step))
                pool.tensor_copy(sm1[:], rstd[:]).then_inc(ln_r, 1)
                pool.wait_ge(w_in, 80)
                for b in range(B):
                    step = chained(pool, pch2, 4 * b)
                    pool.wait_ge(sst_r, b + 1)
                    if b >= 1:
                        pool.wait_ge(y_r, R * b)
                    step(pool.tensor_scalar(sv[:], smv[:, :, 1], KV_SCALE * KV_SCALE, KV_EPS, ALU.mult, ALU.add))
                    step(pool.tensor_tensor(sv[:], sv[:], half[:, 0:R], ALU.pow))
                    step(pool.tensor_scalar(sr[:], sv[:], KV_SCALE, None, ALU.mult))
                    step(pool.tensor_tensor(sn[:], smv[:, :, 0], sr[:], ALU.mult))
                    pool.tensor_scalar(sn[:], sn[:], -1.0, None, ALU.mult).then_inc(srs_r, 1)
                    for r in range(R):
                        pool.wait_ge(yg_r, R * b + r + 1)
                        if b >= 1 and r == 0:
                            pool.wait_ge(ex_r, R * b)
                        pool.tensor_tensor(yb[:, r, :], y[:, r, :], beta[:], ALU.add).then_inc(yb_r, 1)

            @block.vector
            def _(dve):
                step = chained(dve, vch, 0)
                for t in range(T):
                    last = dve.bn_stats(stats[:, t, :], x[:, t, :])
                step(last)
                for t in range(T):
                    last = dve.bn_aggr(mv[:, t, :], stats[:, t, :])
                last.then_inc(st_r, 1)
                dve.wait_ge(w_in, 80)
                for b in range(B):
                    step = chained(dve, vch2, 4 * b)
                    for r in range(R):
                        dve.wait_ge(sim_p, R * b + r + 1)
                        last = dve.bn_stats(sst[:, r, :], bank[:, 4 + r, :])
                    step(last)
                    for r in range(R):
                        last = dve.bn_aggr(smv[:, r, :], sst[:, r, :])
                    last.then_inc(sst_r, 1)
                    for r in range(R):
                        dve.wait_ge(y_r, R * b + r + 1)
                        dve.tensor_tensor(y[:, r, :], y[:, r, :], gamma[:], ALU.mult).then_inc(yg_r, 1)
                    for r in range(R):
                        dve.wait_ge(yb_r, R * b + r + 1)
                        if b >= 1 and r == 0:
                            dve.wait_ge(ex_r, R * b)
                        last = dve.reduce_max(nmax[:, r:r + 1], yb[:, r, :], AX)
                    step(last)
                    dve.tensor_scalar(nmax[:], nmax[:], -1.0, None, ALU.mult).then_inc(mx_r, 1)
                    dve.wait_ge(ex_r, R * b + R)
                    if b >= 1:
                        dve.wait_ge(x_r, R * b)
                    step(dve.reciprocal(share[:], total[:]))
                    step(dve.tensor_scalar(share[:], share[:], tg[:, 1:2], None, ALU.mult))
                    for r in range(R):
                        t = R * b + r
                        dve.scalar_tensor_tensor(x[:, t, :], ex[:, r, :], share[:, r:r + 1], x[:, t, :],
                                                 ALU.mult, ALU.add).then_inc(x_r, 1)


def phase_attention_mlp(nc, sb, sem, g):
    x, bank, ident, tg, stats, mv = g["x"], g["bank"], g["ident"], g["tg"], g["stats"], g["mv"]
    half, rstd, nmr, sm1 = g["half"], g["rstd"], g["nmr"], g["sm1"]
    with ExitStack() as scope:
        def s_(name, shape, dt=F32):
            return sb(name, shape, dt, scope)
        n_sc = s_("n_scale", [P, T])
        n_bi = s_("n_bias", [P, T])
        mod = s_("mod", [P, T, RK])
        r_sc = s_("r_scale", [P, T])
        r_bi = s_("r_bias", [P, T])
        with ExitStack() as inner:
            phase_attention(nc, lambda n, s, d=F32: sb(n, s, d, inner), sem, dict(g, **locals()))
        phase_mlp(nc, s_, sem, dict(g, **locals()))


def phase_attention(nc, s_, sem, g):
    x, bank, ident, tg, stats, mv = g["x"], g["bank"], g["ident"], g["tg"], g["stats"], g["mv"]
    half, rstd, nmr, sm1 = g["half"], g["rstd"], g["nmr"], g["sm1"]
    n_sc, n_bi, r_sc, r_bi, mod = g["n_sc"], g["n_bi"], g["r_sc"], g["r_bi"], g["mod"]
    raw = s_("at_raw", [P, 2, DC, D])
    wq_hi = s_("at_wq_hi", [P, DC, D], F32R)
    wq_lo = s_("at_wq_lo", [P, DC, D], F32R)
    wk_hi = s_("at_wk_hi", [P, DC, D], F32R)
    wk_lo = s_("at_wk_lo", [P, DC, D], F32R)
    wu_hi = s_("at_wu_hi", [P, DC, HEADS * RK], F32R)
    wu_lo = s_("at_wu_lo", [P, DC, HEADS * RK], F32R)
    A = s_("at_A", [P, DC, RK])
    woa = s_("at_woa", [P, DC, 4, RK])
    ln1 = s_("at_ln1", [P, DC])
    xn = s_("at_n", [P, R, D])
    xT_hi = s_("at_xT_hi", [P, DC, N], F32R)
    xT_lo = s_("at_xT_lo", [P, DC, N], F32R)
    qT = s_("at_qT", [P, DC, N])
    kT = s_("at_kT", [P, DC, N])
    U = s_("at_U", [P, R, HEADS * RK])
    mask_f = s_("at_mask_f", [P, P])
    mask = s_("at_mask", [P, P], F32R)
    ident_r = s_("at_ident", [P, P], F32R)
    mx = s_("at_max", [P, 4])
    nmx = s_("at_negmax", [P, 4])
    nscale = s_("at_negscale", [P, 1])
    red = s_("at_red", [P, RK])
    pr = s_("at_probs", [P, 4, N])
    pT = s_("at_probsT", [P, 2, N])
    tot = s_("at_total", [P, R, HEADS])
    rto = s_("at_rtotal", [P, 2, HEADS])
    ou = s_("at_out", [P, 2, HEADS, RK])

    w_in = sem("at_small_arrived")
    v_in = sem("at_values_arrived")
    q_in = sem("at_queries_arrived")
    st_r = sem("at_stats_ready")
    ln_r = sem("at_scales_ready")
    woa_p = sem("at_woa_done")
    woa_0 = sem("at_woa_cleared")
    woa_r = sem("at_woa_ready")
    wu_p = sem("at_wu_done")
    wu_h = sem("at_wu_hi_ready")
    wu_l = sem("at_wu_lo_ready")
    wqk_h = sem("at_wqk_hi_ready")
    wqk_l = sem("at_wqk_lo_ready")
    msk_r = sem("at_mask_ready")
    n_r = sem("at_n_ready")
    xt_p = sem("at_xT_transposed")
    xt_h = sem("at_xT_hi_ready")
    xt_l = sem("at_xT_lo_ready")
    pj_p = sem("at_projection_done")
    pj_r = sem("at_projection_ready")
    s_p = sem("at_scores_done")
    mx_r = sem("at_max_ready")
    nm_r = sem("at_negmax_ready")
    pr_r = sem("at_probs_ready")
    pT_p = sem("at_probsT_done")
    pT_r = sem("at_probsT_ready")
    o_p = sem("at_pv_done")
    o_r = sem("at_out_ready")
    vch = sem("at_vector_chain")
    och = sem("at_out_chain")
    pch = sem("at_pool_chain")

    UNITS = R * HEADS
    PROJ = 2 * DC + R
    LAG_T, LAG_V = 3, 4

    with nc.Block() as block:
        @block.sync
        def _(sp):
            sp.dma_start(raw[:, 0], g["Wo"].rearrange("(c p) o -> p c o", p=P)).then_inc(w_in, 16)
            sp.dma_start(A[:], g["A_in"].rearrange("(c p) r -> p c r", p=P)).then_inc(w_in, 16)
            sp.dma_start(ln1[:], g["ln1_w"]).then_inc(w_in, 16)
            sp.dma_start(raw[:, 1], g["Wv"].rearrange("(c p) d -> p c d", p=P)).then_inc(v_in, 16)
            sp.wait_ge(wu_p, DC)
            sp.dma_start(raw[:, 0], g["WqT"].rearrange("(c p) o -> p c o", p=P)).then_inc(q_in, 16)
            sp.dma_start(raw[:, 1], g["WkT1"].rearrange("(c p) o -> p c o", p=P)).then_inc(q_in, 16)

        @block.gpsimd
        def _(pool):
            step = chained(pool, pch, 0)
            pool.memset(woa[:], 0.0).then_inc(woa_0, 1)
            step(pool.memset(nscale[:], -ATT_SCALE))
            step(pool.memset(mask_f[:], 0.0))
            step(pool.affine_select(out=mask_f[:], in_=mask_f[:], compare_op=ALU.is_ge, fill=MASKED, base=0,
                                    pattern=[[-1, P]], channel_multiplier=1))
            step(pool.tensor_copy(mask[:], mask_f[:]))
            pool.tensor_copy(ident_r[:], ident[:]).then_inc(msk_r, 1)
            pool.wait_ge(st_r, 1)
            step(rstd_steps(pool, sm1[:], mv, 1.0, LN_EPS, half[:], rstd[:], nmr[:], step))
            step(pool.tensor_tensor(sm1[:], rstd[:], rstd[:], ALU.mult))
            step(pool.tensor_tensor(sm1[:], sm1[:], mv[:, :, 1], ALU.mult))
            step(pool.tensor_scalar(sm1[:], sm1[:], 1.0, KV_EPS, ALU.mult, ALU.add))
            step(pool.tensor_tensor(sm1[:], sm1[:], half[:], ALU.pow))
            step(pool.tensor_tensor(n_sc[:], rstd[:], sm1[:], ALU.mult))
            step(pool.tensor_tensor(n_bi[:], nmr[:], sm1[:], ALU.mult))
            step(pool.tensor_scalar(r_sc[:], rstd[:], tg[:, 3:4], 1.0, ALU.mult, ALU.add))
            pool.tensor_scalar(r_bi[:], nmr[:], tg[:, 3:4], 0.0, ALU.mult, ALU.add).then_inc(ln_r, 1)
            pool.wait_ge(wqk_h, 1)
            pool.tensor_tensor(wq_lo[:], raw[:, 0], wq_hi[:].bitcast(F32), ALU.subtract)
            pool.tensor_tensor(wk_lo[:], raw[:, 1], wk_hi[:].bitcast(F32), ALU.subtract).then_inc(wqk_l, 1)
            with pool.Fori(0, B) as b:
                for s in range(UNITS):
                    pool.wait_ge(mx_r, UNITS * b + s + 1)
                    pool.wait_ge(pr_r, UNITS * b + s - 3 + 4)
                    pool.tensor_tensor(nmx[:, s % 4:s % 4 + 1], mx[:, s % 4:s % 4 + 1], nscale[:], ALU.mult)\
                        .then_inc(nm_r, 1)

        @block.tensor
        def _(pe):
            pe.wait_ge(w_in, 48)
            for m in range(DC):
                for c in range(DC):
                    last = pe.matmul(bank[:, 0, m * RK:(m + 1) * RK], raw[:, 0, c, m * P:(m + 1) * P], A[:, c, :],
                                     start=c == 0, stop=c == DC - 1)
            last.then_inc(woa_p, 1)
            pe.wait_ge(v_in, 16)
            pe.wait_ge(woa_r, 1)
            for d in range(DC):
                for m in range(DC):
                    last = pe.matmul(bank[:, 1 + d, m * 4 * RK:(m + 1) * 4 * RK], raw[:, 1, m, d * P:(d + 1) * P],
                                     woa[:, m], start=True, stop=True)
                last.then_inc(wu_p, 1)
            pe.wait_ge(wu_l, DC)
            pe.wait_ge(wqk_l, 1)
            pe.wait_ge(msk_r, 1)

            def project(b):
                for c in range(DC):
                    if c == 0:
                        pe.wait_ge(n_r, R * b + R)
                        pe.wait_ge(o_r, R * b)
                    for r in range(R):
                        last = pe.transpose(bank[:, c, r * P:(r + 1) * P], xn[:, r, c * P:(c + 1) * P], ident[:])
                    last.then_inc(xt_p, 1)
                pe.wait_ge(xt_l, DC * b + DC)
                k = 0
                for w_h, w_l in ((wq_hi, wq_lo), (wk_hi, wk_lo)):
                    for o in range(DC):
                        if k >= 4:
                            pe.wait_ge(pj_r, PROJ * b + k - 3)
                        passes = [(w, a, c) for c in range(DC) for w, a in ((w_h, xT_hi), (w_h, xT_lo), (w_l, xT_hi))]
                        for q, (w, a, c) in enumerate(passes):
                            last = pe.matmul(bank[:, k % 4, :], w[:, c, o * P:(o + 1) * P], a[:, c, :], start=q == 0,
                                             stop=q == len(passes) - 1)
                        last.then_inc(pj_p, 1)
                        k += 1
                for r in range(R):
                    pe.wait_ge(pj_r, PROJ * b + k - 3)
                    passes = [(a, w, c) for c in range(DC) for a, w in ((xT_hi, wu_hi), (xT_hi, wu_lo), (xT_lo, wu_hi))]
                    for q, (a, w, c) in enumerate(passes):
                        last = pe.matmul(bank[:, k % 4, 0:HEADS * RK], a[:, c, r * P:(r + 1) * P], w[:, c, :],
                                         start=q == 0, stop=q == len(passes) - 1)
                    last.then_inc(pj_p, 1)
                    k += 1
                pe.wait_ge(pj_r, PROJ * b + PROJ)

            def scores(b, s):
                qt, h = s // HEADS, s % HEADS
                keys = (qt + 1) * P
                hp = slice(h % 4 * HD, (h % 4 + 1) * HD)
                pe.wait_ge(pr_r, UNITS * b + s - 3 + 4)
                slot = 2 + s % 4
                pe.matmul(bank[:, slot, 0:keys], qT[hp, h // 4, qt * P:(qt + 1) * P], kT[hp, h // 4, 0:keys],
                          start=True, stop=False)
                pe.matmul(bank[:, slot, qt * P:keys], ident_r[:], mask[:], start=False, stop=True)\
                  .then_inc(s_p, 1)

            def turn(b, s):
                qt = s // HEADS
                pe.wait_ge(pr_r, UNITS * b + s + 1 + 4)
                pe.wait_ge(pT_r, UNITS * b + s - 1 + 2)
                for k in range(qt + 1):
                    last = pe.transpose(bank[:, 6 + s % 2, k * P:(k + 1) * P], pr[:, s % 4, k * P:(k + 1) * P], ident[:])
                last.then_inc(pT_p, 1)

            def product(b, s):
                qt, h = s // HEADS, s % HEADS
                pe.wait_ge(pT_r, UNITS * b + s + 1 + 2)
                if h == 0 and qt >= 2:
                    pe.wait_ge(o_r, R * b + qt - 1)
                for k in range(qt + 1):
                    last = pe.matmul(bank[:, qt % 2, h * RK:(h + 1) * RK], pT[:, s % 2, k * P:(k + 1) * P],
                                     U[:, k, h * RK:(h + 1) * RK], start=k == 0, stop=k == qt)
                last.then_inc(o_p, 1)

            with pe.Fori(0, B) as b:
                project(b)
                for s in range(UNITS + LAG_V):
                    if s < UNITS:
                        scores(b, s)
                    if LAG_T <= s < UNITS + LAG_T:
                        turn(b, s - LAG_T)
                    if s >= LAG_V:
                        product(b, s - LAG_V)

        @block.scalar
        def _(act):
            act.sem_inc(pr_r, 4)
            for d in range(DC):
                act.wait_ge(wu_p, d + 1)
                act.activation(wu_hi[:, d, :], bank[:, 1 + d, 0:HEADS * RK], ACT.Copy).then_inc(wu_h, 1)
            act.wait_ge(q_in, 32)
            act.activation(wq_hi[:], raw[:, 0], ACT.Copy)
            act.activation(wk_hi[:], raw[:, 1], ACT.Copy).then_inc(wqk_h, 1)
            act.wait_ge(ln_r, 1)
            act.wait_ge(w_in, 48)

            def normalise(b):
                act.wait_ge(ln_r, 1)
                for r in range(R):
                    act.activation(xn[:, r, :], x[:, bass.ds(R * b + r, 1), :].rearrange("p o d -> p (o d)"),
                                   ACT.Identity, bias=n_bi[:, bass.ds(R * b + r, 1)],
                                   scale=n_sc[:, bass.ds(R * b + r, 1)]).then_inc(n_r, 1)

            with act.Fori(0, B) as b:
                act.wait_ge(xt_p, DC * b)
                normalise(b)
                for c in range(DC):
                    act.wait_ge(xt_p, DC * b + c + 1)
                    if c == 0:
                        act.wait_ge(pj_p, PROJ * b)
                    act.activation(xT_hi[:, c, :], bank[:, c, :], ACT.Copy, scale=ln1[:, c:c + 1]).then_inc(xt_h, 1)
                act.wait_ge(o_p, UNITS * b)
                for k in range(PROJ):
                    act.wait_ge(pj_p, PROJ * b + k + 1)
                    if k < 2 * DC:
                        act.activation((qT, kT)[k // DC][:, k % DC, :], bank[:, k % 4, :], ACT.Copy).then_inc(pj_r, 1)
                    else:
                        act.activation(U[:, k - 2 * DC, :], bank[:, k % 4, 0:HEADS * RK], ACT.Copy).then_inc(pj_r, 1)
                act.wait_ge(o_r, R * b)
                for s in range(UNITS):
                    qt, h = s // HEADS, s % HEADS
                    keys = (qt + 1) * P
                    act.wait_ge(nm_r, UNITS * b + s + 1 + 4)
                    act.wait_ge(pT_p, UNITS * b + s - 3 + 4)
                    act.activation(pr[:, s % 4, 0:keys], bank[:, 2 + s % 4, 0:keys], ACT.Exp,
                                   bias=nmx[:, s % 4:s % 4 + 1], scale=ATT_SCALE, accum_out=tot[:, qt, h:h + 1])\
                       .then_inc(pr_r, 1)

        @block.vector
        def _(dve):
            dve.sem_inc(pT_r, 2)
            dve.sem_inc(pT_p, 4)
            dve.sem_inc(nm_r, 4)
            step = chained(dve, vch, 0)
            for t in range(T):
                last = dve.bn_stats(stats[:, t, :], x[:, t, :])
            step(last)
            for t in range(T):
                last = dve.bn_aggr(mv[:, t, :], stats[:, t, :])
            last.then_inc(st_r, 1)
            dve.wait_ge(woa_p, 1)
            dve.wait_ge(woa_0, 1)
            for j in range(4):
                rows = slice(j * HD, (j + 1) * HD)
                last = dve.tensor_copy(woa[rows, :, j, :], bank[rows, 0, 0:DC * RK].rearrange("p (m r) -> p m r", r=RK))
            last.then_inc(woa_r, 1)
            for d in range(DC):
                dve.wait_ge(wu_h, d + 1)
                dve.tensor_tensor(wu_lo[:, d, :], bank[:, 1 + d, 0:HEADS * RK], wu_hi[:, d, :].bitcast(F32),
                                  ALU.subtract).then_inc(wu_l, 1)
            dve.wait_ge(w_in, 48)

            def finish(b, qt):
                step = chained(dve, och, 3 * R * b + 3 * qt)
                dve.wait_ge(o_p, UNITS * b + HEADS * (qt + 1))
                dve.wait_ge(o_r, R * b + qt)
                step(dve.reciprocal(rto[:, qt % 2, :], tot[:, qt, :]))
                step(dve.tensor_tensor(ou[:, qt % 2], bank[:, qt % 2, 0:HEADS * RK].rearrange("p (h r) -> p h r", r=RK),
                                       rto[:, qt % 2, :].unsqueeze(2).broadcast_to([P, HEADS, RK]), ALU.mult))
                step(dve.tensor_reduce(red[:], ou[:, qt % 2].rearrange("p h r -> p r h"), op=ALU.add, axis=AX))
                dve.tensor_scalar(mod[:, bass.ds(R * b + qt, 1), :].rearrange("p o r -> p (o r)"), red[:], 1.0, None,
                                  ALU.mult).then_inc(o_r, 1)

            with dve.Fori(0, B) as b:
                for c in range(DC):
                    dve.wait_ge(xt_h, DC * b + c + 1)
                    dve.scalar_tensor_tensor(xT_lo[:, c, :], bank[:, c, :], ln1[:, c:c + 1],
                                             xT_hi[:, c, :].bitcast(F32), ALU.mult, ALU.subtract).then_inc(xt_l, 1)
                for s in range(UNITS + LAG_T):
                    if s < UNITS:
                        keys = (s // HEADS + 1) * P
                        dve.wait_ge(s_p, UNITS * b + s + 1)
                        dve.wait_ge(nm_r, UNITS * b + s - 3 + 4)
                        dve.reduce_max(mx[:, s % 4:s % 4 + 1], bank[:, 2 + s % 4, 0:keys], AX).then_inc(mx_r, 1)
                    if s >= LAG_T:
                        v = s - LAG_T
                        keys = (v // HEADS + 1) * P
                        dve.wait_ge(pT_p, UNITS * b + v + 1 + 4)
                        if v >= 2:
                            dve.wait_ge(o_p, UNITS * b + v - 1)
                        else:
                            dve.wait_ge(o_p, UNITS * b)
                        dve.tensor_copy(pT[:, v % 2, 0:keys], bank[:, 6 + v % 2, 0:keys]).then_inc(pT_r, 1)
                        if v % HEADS == 2 and v > HEADS:
                            finish(b, v // HEADS - 1)
                finish(b, R - 1)


def phase_mlp(nc, s_, sem, g):
    x, bank, ident, tg = g["x"], g["bank"], g["ident"], g["tg"]
    n_sc, n_bi, r_sc, r_bi, mod = g["n_sc"], g["n_bi"], g["r_sc"], g["r_bi"], g["mod"]
    xT_hi = s_("ml_xT_hi", [P, DC, B * N], F32R)
    xT_lo = s_("ml_xT_lo", [P, DC, B * N], F32R)
    b_stack = s_("ml_b_stack", [96, F_], F32R)
    m_stack = s_("ml_m_stack", [96, B * N], F32R)
    with ExitStack() as inner:
        def i_(name, shape, dt=F32):
            return inner.enter_context(nc.sbuf_tensor(name, shape, dt))
        xn = i_("ml_n", [P, R, D])
        ln2 = i_("ml_ln2", [P, DC])
        A = i_("ml_A", [P, DC, RK])
        A_hi = i_("ml_A_hi", [P, DC, RK], F32R)
        A_lo = i_("ml_A_lo", [P, DC, RK], F32R)
        b_raw = i_("ml_b_raw", [96, F_])
        m_rows = i_("ml_m_rows", [P, T, 3, 32])
        m_hi = i_("ml_m_hi", [96, 512], F32R)

        w_in = sem("ml_small_arrived")
        b_0 = sem("ml_b_cleared")
        b_in = sem("ml_b_arrived")
        a_h = sem("ml_A_hi_ready")
        a_l = sem("ml_A_lo_ready")
        bst_h = sem("ml_b_hi_ready")
        bst_r = sem("ml_b_stack_ready")
        m_0 = sem("ml_m_cleared")
        n_r = sem("ml_n_ready")
        xt_p = sem("ml_xT_transposed")
        xt_h = sem("ml_xT_hi_ready")
        xt_l = sem("ml_xT_lo_ready")
        th_r = sem("ml_tanh_ready")
        ha_p = sem("ml_hA_done")
        m_r = sem("ml_m_ready")
        mt_p = sem("ml_mT_done")
        mh_r = sem("ml_m_hi_ready")
        ms_r = sem("ml_m_stack_ready")
        vch = sem("ml_vector_chain")

        with nc.Block() as block:
            @block.sync
            def _(sp):
                sp.dma_start(ln2[:], g["ln2_w"]).then_inc(w_in, 16)
                sp.dma_start(A[:], g["A_in"].rearrange("(c p) r -> p c r", p=P)).then_inc(w_in, 16)
                sp.wait_ge(b_0, 1)
                for k in range(3):
                    sp.dma_start(b_raw[32 * k:32 * k + RK, :], g["B_in"]).then_inc(b_in, 16)

            @block.gpsimd
            def _(pool):
                pool.memset(b_raw[:], 0.0).then_inc(b_0, 1)
                pool.memset(m_rows[:], 0.0).then_inc(m_0, 1)
                pool.wait_ge(a_h, 1)
                pool.tensor_tensor(A_lo[:], A[:], A_hi[:].bitcast(F32), ALU.subtract).then_inc(a_l, 1)

            @block.scalar
            def _(act):
                act.activation(mod[:], mod[:], ACT.Tanh).then_inc(th_r, 1)
                act.wait_ge(w_in, 32)
                act.activation(A_hi[:], A[:], ACT.Copy).then_inc(a_h, 1)
                act.wait_ge(b_in, 48)
                act.activation(b_stack[:], b_raw[:], ACT.Copy).then_inc(bst_h, 1)
                for b in range(B):
                    if b >= 1:
                        act.wait_ge(xt_p, DC * b)
                    for r in range(R):
                        t = R * b + r
                        act.activation(xn[:, r, :], x[:, t, :], ACT.Identity, bias=n_bi[:, t:t + 1],
                                       scale=n_sc[:, t:t + 1]).then_inc(n_r, 1)
                        act.wait_ge(n_r, t + 1)
                        act.activation(x[:, t, :], x[:, t, :], ACT.Identity, bias=r_bi[:, t:t + 1],
                                       scale=r_sc[:, t:t + 1])
                    for c in range(DC):
                        act.wait_ge(xt_p, DC * b + c + 1)
                        act.activation(xT_hi[:, c, b * N:(b + 1) * N], bank[:, c, :], ACT.Copy,
                                       scale=ln2[:, c:c + 1]).then_inc(xt_h, 1)
                for b in range(B):
                    act.wait_ge(mt_p, b + 1)
                    if b >= 1:
                        act.wait_ge(ms_r, b)
                    act.activation(m_hi[:], bank[0:96, 5 + b % 2, :], ACT.Copy).then_inc(mh_r, 1)

            @block.tensor
            def _(pe):
                for b in range(B):
                    pe.wait_ge(n_r, R * b + R)
                    for c in range(DC):
                        if b >= 1:
                            pe.wait_ge(xt_l, DC * b + c - 3)
                        for r in range(R):
                            last = pe.transpose(bank[:, c, r * P:(r + 1) * P], xn[:, r, c * P:(c + 1) * P], ident[:])
                        last.then_inc(xt_p, 1)
                    if b == 0:
                        pe.wait_ge(a_l, 1)
                    pe.wait_ge(xt_l, DC * b + DC)
                    for r in range(R):
                        t = R * b + r
                        at = slice(t * P, (t + 1) * P)
                        passes = [(a, w, c) for c in range(DC) for a, w in ((xT_hi, A_hi), (xT_hi, A_lo), (xT_lo, A_hi))]
                        for q, (a, w, c) in enumerate(passes):
                            last = pe.matmul(bank[:, 4, t * RK:(t + 1) * RK], a[:, c, at], w[:, c, :], start=q == 0,
                                             stop=q == len(passes) - 1)
                    last.then_inc(ha_p, 1)
                pe.wait_ge(m_r, 1)
                for b in range(B):
                    if b >= 2:
                        pe.wait_ge(ms_r, b - 1)
                    for r in range(R):
                        last = pe.transpose(bank[0:96, 5 + b % 2, r * P:(r + 1) * P],
                                            m_rows[:, R * b + r].rearrange("p k m -> p (k m)"), ident[:])
                    last.then_inc(mt_p, 1)

            @block.vector
            def _(dve):
                step = chained(dve, vch, 0)
                dve.wait_ge(w_in, 32)
                dve.wait_ge(bst_h, 1)
                dve.tensor_tensor(b_stack[32:64, :], b_raw[32:64, :], b_stack[32:64, :].bitcast(F32), ALU.subtract)\
                   .then_inc(bst_r, 1)
                for b in range(B):
                    for c in range(DC):
                        dve.wait_ge(xt_h, DC * b + c + 1)
                        at = slice(b * N, (b + 1) * N)
                        dve.scalar_tensor_tensor(xT_lo[:, c, at], bank[:, c, :], ln2[:, c:c + 1],
                                                 xT_hi[:, c, at].bitcast(F32), ALU.mult, ALU.subtract).then_inc(xt_l, 1)
                dve.wait_ge(th_r, 1)
                dve.wait_ge(ha_p, B)
                dve.wait_ge(m_0, 1)
                step(dve.scalar_tensor_tensor(m_rows[:, :, 0, 0:RK], mod[:], MOD_SCALE,
                                              bank[:, 4, 0:T * RK].rearrange("p (t r) -> p t r", r=RK),
                                              ALU.mult, ALU.mult))
                dve.tensor_copy(m_rows[:, :, 1, 0:RK], m_rows[:, :, 0, 0:RK])
                dve.tensor_copy(m_rows[:, :, 2, 0:RK], m_rows[:, :, 0, 0:RK]).then_inc(m_r, 1)
                for b in range(B):
                    dve.wait_ge(mh_r, b + 1)
                    at = slice(b * 512, (b + 1) * 512)
                    dve.tensor_copy(m_stack[0:64, at], m_hi[0:64, :].bitcast(F32))
                    dve.tensor_tensor(m_stack[64:96, at], bank[64:96, 5 + b % 2, :], m_hi[64:96, :].bitcast(F32),
                                      ALU.subtract).then_inc(ms_r, 1)

    def source(u, p, loop):
        at = bass.ds(u * UH, UH)
        return (g["W_inT"][:, at].rearrange("(c p) h -> p c h", p=P),
                g["W_upT"][:, at].rearrange("(c p) h -> p c h", p=P),
                g["W_downT"][at, :].rearrange("(k p) d -> p k d", p=P))

    gated_units(nc, s_, sem, "ml", x, bank, xT_hi, xT_lo, MLP_UNITS, source, gate=tg[:, 3:4], mod=(b_stack, m_stack))


def layout(inputs):
    import numpy as np
    a = {k: np.asarray(v) for k, v in inputs.items()}
    c = np.ascontiguousarray
    return {
        "x_in": a["x"], "ctxT_in": c(a["ctx_512"].reshape(B * N, C).T),
        "g_xattn": a["g_xattn"], "g_ffn": a["g_ffn"],
        "gr_Wq": a["L0_xattn_Wq"], "gr_Wk": a["L0_xattn_Wk"], "gr_gamma": a["L0_xattn_gamma_raw"].reshape(1),
        "router_w": a["L0_ffn_router_w"], "w_gate": a["L0_ffn_w_gate"], "w_up": a["L0_ffn_w_up"],
        "w_down": a["L0_ffn_w_down"], "sw_gate": a["L0_ffn_sw_gate"], "sw_up": a["L0_ffn_sw_up"],
        "sw_down": a["L0_ffn_sw_down"],
        "WkT": c(a["L1_xattn_W_k"].T), "b_k": a["L1_xattn_b_k"], "ln_gamma": a["L1_xattn_ln_gamma"],
        "ln_beta": a["L1_xattn_ln_beta"], "ln1_w": c(a["L1_ffn_ln1_w"].reshape(DC, P).T), "ln2_w": c(a["L1_ffn_ln2_w"].reshape(DC, P).T),
        "WqT": c(a["L1_ffn_Wq"].T), "WkT1": c(a["L1_ffn_Wk"].T), "Wv": a["L1_ffn_Wv"], "Wo": a["L1_ffn_Wo"],
        "A_in": a["L1_ffn_A"], "B_in": a["L1_ffn_B"], "W_inT": c(a["L1_ffn_W_in_base"].T),
        "W_upT": c(a["L1_ffn_W_up_base"].T), "W_downT": c(a["L1_ffn_W_down"].T),
    }


def kernel(**inputs):
    import numpy as _np
    import concourse.bacc as _bacc
    from concourse import mybir as _mybir
    from concourse.bass_utils import run_bass_kernel_spmd as _run

    nc = _bacc.Bacc("TRN2", target_bir_lowering=False, num_devices=1)
    arrays, args = {}, []
    for name, a in layout(inputs).items():
        arrays[f"in_{name}"] = _np.ascontiguousarray(a)
        args.append(nc.dram_tensor(f"in_{name}", a.shape, _mybir.dt.from_np(a.dtype), kind="ExternalInput").ap())
    out = nc.dram_tensor("out_0", (B, N, D), _mybir.dt.float32, kind="ExternalOutput").ap()
    flamingo_kernel(nc, *args, out)
    r = _run(nc, [arrays], core_ids=[0])
    return r.results[0]["out_0"]
```

```python
from contextlib import ExitStack

import concourse.bass as bass
from concourse import mybir

P = 128
F32 = mybir.dt.float32
F32R = mybir.dt.float32r
BF16 = mybir.dt.bfloat16
U32 = mybir.dt.uint32
I32 = mybir.dt.int32
ALU = mybir.AluOpType
ACT = mybir.ActivationFunctionType
AX = mybir.AxisListType.X

B, N, D = 4, 512, 512
C = 128
T = B * N // P
R = N // P
DC = D // P
LN_EPS = 1e-5

GRAPH_HEADS = 4
GRAPH_SCALE = 1.0 / ((C // GRAPH_HEADS) ** 0.5 * GRAPH_HEADS)
TOP = int(N * 0.3)
HALVINGS = 24
MEAN_TO_LOW = (N / (N - TOP + 1) - 1) ** 0.5
MEAN_TO_HIGH = (N / TOP - 1) ** 0.5
VT = 7
ST = T - VT

GROUPS = (slice(0, (ST + 1) // 2), slice((ST + 1) // 2, ST))

E_ = 8
UH = 256
HC = UH // P
MOE_UNITS = E_ + 2
KV_EPS = 1e-6
KV_SCALE = N ** -0.5
HEADS = 16
HD = D // HEADS
RK = 16
F_ = 2048
MLP_UNITS = F_ // UH
ATT_SCALE = 1.0 / HD ** 0.5
MOD_SCALE = 0.1
MASKED = -1e30
TB = B * N // 512

GU_LEAD = 2
Y_LEAD = 32
ACC_LEAD = 16


class Count:
    def __init__(self, sem):
        self.sem, self.value = sem, 0


def linked(eng, count):
    def step(ins):
        count.value += 1
        ins.then_inc(count.sem, 1)
        eng.wait_ge(count.sem, count.value)
    return step


def chained(eng, sem, start):
    count = [start]

    def step(ins):
        count[0] += 1
        ins.then_inc(sem, 1)
        eng.wait_ge(sem, count[0])
    return step


def flamingo_kernel(nc, x_in, ctxT_in, g_xattn, g_ffn, gr_Wq, gr_Wk, gr_gamma, router_w, w_gate, w_up,
                    w_down, sw_gate, sw_up, sw_down, WkT, b_k, ln_gamma, ln_beta, ln1_w, ln2_w, WqT,
                    WkT1, Wv, Wo, A_in, B_in, W_inT, W_upT, W_downT, out, stop=99):
    with ExitStack() as ctx:
        def sb(name, shape, dt=F32, scope=ctx):
            return scope.enter_context(nc.sbuf_tensor(name, shape, dt))

        def sem(name):
            return ctx.enter_context(nc.semaphore(name))

        bank = ctx.enter_context(nc.psum_tensor("bank", [P, 8, 512], F32))
        x = sb("x", [P, T, D])
        ident = sb("ident", [P, P])
        gates = sb("gates", [P, 8])
        tg = sb("tg", [P, 4])
        gam = sb("gam", [P, 1])
        stats = sb("stats", [P, T, 6])
        mv = sb("mv", [P, T, 2])
        half = sb("half", [P, T])
        rstd = sb("rstd", [P, T])
        nmr = sb("nmr", [P, T])
        sm1 = sb("sm1", [P, T])
        x_dram = x_in.rearrange("b (r p) d -> p (b r) d", p=P)
        out_dram = out.rearrange("b (r p) d -> p (b r) d", p=P)

        vector_chain, pool_chain = Count(sem("vector_chain")), Count(sem("pool_chain"))
        phase_graph(nc, sb, sem, locals())
        if stop >= 2:
            phase_moe(nc, sb, sem, locals())
        if stop >= 3:
            phase_kv(nc, sb, sem, locals())
        if stop >= 4:
            phase_attention_mlp(nc, sb, sem, locals())
        s_out = sem("x_stored")
        with nc.Block() as block:
            @block.sync
            def _(sp):
                sp.dma_start(out_dram[:, 0:8, :], x[:, 0:8, :]).then_inc(s_out, 16)
                sp.dma_start(out_dram[:, 8:16, :], x[:, 8:16, :]).then_inc(s_out, 16)
                sp.wait_ge(s_out, 32)


def rstd_steps(pool, v, mv_, scale, eps, half, rstd, nmr, step):
    step(pool.tensor_scalar(v, mv_[:, :, 1], scale, eps, ALU.mult, ALU.add))
    step(pool.tensor_tensor(rstd, v, half, ALU.pow))
    step(pool.tensor_tensor(nmr, mv_[:, :, 0], rstd, ALU.mult))
    return pool.tensor_scalar(nmr, nmr, -1.0, None, ALU.mult)


def phase_graph(nc, sb, sem, g):
    x, bank, ident, gates, tg, gam = g["x"], g["bank"], g["ident"], g["gates"], g["tg"], g["gam"]
    stats, mv, half, rstd, nmr, sm1 = g["stats"], g["mv"], g["half"], g["rstd"], g["nmr"], g["sm1"]
    with ExitStack() as scope:
        def s_(name, shape, dt=F32):
            return sb(name, shape, dt, scope)
        S = s_("sim", [P, T, N])
        ctxT = s_("gr_ctxT", [P, B, N])
        wq = s_("gr_wq", [C, C])
        wk = s_("gr_wk", [C, C])
        M = s_("gr_M", [C, C])
        Z = s_("gr_Z", [P, B, N])
        sst = s_("sim_stats", [P, T, 6])
        smv = s_("sim_mv", [P, T, 2])
        sg = s_("sig", [P, 2, N])
        yb = s_("yb", [P, 2, N])
        tb = s_("tb", [P, 2, N])
        junk_v = s_("junk_v", [P, VT, N], BF16)
        junk_s = s_("junk_s", [P, ST, N], BF16)
        width = s_("width", [P, T])
        low = s_("low", [P, T])
        mid = s_("mid", [P, T])
        cnt = s_("cnt", [P, T])
        sel = s_("selc", [P, T])
        nlow = s_("nlow", [P, ST])
        nmid = s_("nmid", [P, ST])
        slack = s_("slack", [P, T])
        sigma = s_("sigma", [P, T])
        sc1 = s_("sc1", [P, T])
        bi1 = s_("bi1", [P, T])
        c1 = s_("c1", [P, 1])
        c2 = s_("c2", [P, 1])

        x_in_s = [sem(f"gr_x_arrived{b}") for b in range(B)]
        w_in = sem("gr_weights_arrived")
        c_in = sem("gr_ctx_arrived")
        g_in = sem("gr_gates_arrived")
        m_ps = sem("gr_M_done")
        m_sb = sem("gr_M_copied")
        z_ps = sem("gr_Z_done")
        z_sb = sem("gr_Z_copied")
        s_ps = sem("gr_sim_done")
        s_sb = sem("gr_sim_copied")
        cst = sem("gr_constants")
        lnst = sem("gr_ln_stats")
        sim_st = sem("gr_sim_stats")
        brk = sem("gr_bracket_ready")
        nmid_r = [sem(f"gr_negmid_ready{h}") for h in range(2)]
        cnt_s = sem("gr_signs_counted")
        gat = sem("gr_gates_ready")
        coef = sem("gr_coefs_ready")
        sig_r = sem("gr_sigmoid_ready")
        a_r = sem("gr_A_ready")
        at_r = sem("gr_AT_ready")
        y_r = sem("gr_y_ready")
        t_r = sem("gr_t_ready")
        x_r = sem("gr_x_ready")

        with nc.Block() as block:
            @block.sync
            def _(sp):
                sp.dma_start(wq[:], g["gr_Wq"]).then_inc(w_in, 16)
                sp.dma_start(wk[:], g["gr_Wk"]).then_inc(w_in, 16)
                sp.dma_start(ctxT[:], g["ctxT_in"].rearrange("c (b n) -> c b n", b=B)).then_inc(c_in, 16)
                for k, (src, n) in enumerate(((g["g_xattn"], 2), (g["g_ffn"], 2), (g["gr_gamma"], 1))):
                    sp.dma_start(gates[:, 2 * k:2 * k + n], src.partition_broadcast(P)).then_inc(g_in, 16)
                for b in range(B):
                    sp.dma_start(x[:, R * b:R * b + R, :], g["x_dram"][:, R * b:R * b + R, :])\
                      .then_inc(x_in_s[b], 16)

            @block.tensor
            def _(pe):
                pe.wait_ge(w_in, 32)
                pe.matmul(bank[:, 0, 0:C], wq[:], wk[:], start=True, stop=True).then_inc(m_ps, 1)
                pe.wait_ge(m_sb, 1)
                pe.wait_ge(c_in, 16)
                for b in range(B):
                    if b >= 2:
                        pe.wait_ge(z_sb, b - 1)
                    pe.matmul(bank[:, b % 2, :], M[:], ctxT[:, b, :], start=True, stop=True).then_inc(z_ps, 1)
                    pe.wait_ge(z_sb, b + 1)
                    for r in range(R):
                        t = R * b + r
                        if t >= 6:
                            pe.wait_ge(s_sb, t - 5)
                        pe.matmul(bank[:, 2 + t % 6, :], Z[:, b, r * P:(r + 1) * P], ctxT[:, b, :],
                                  start=True, stop=True).then_inc(s_ps, 1)
                pe.wait_ge(cst, 1)
                for b in range(B):
                    pe.wait_ge(a_r, R * (b + 1))
                    for r in range(R):
                        t = R * b + r
                        if t >= 8:
                            pe.wait_ge(t_r, t - 7)
                        if t == 0:
                            pe.wait_ge(s_sb, T)
                        for q in range(R):
                            last = pe.transpose(bank[:, t % 8, q * P:(q + 1) * P],
                                                S[:, R * b + q, r * P:(r + 1) * P], ident[:])
                        last.then_inc(at_r, 1)

            @block.scalar
            def _(act):
                act.wait_ge(g_in, 48)
                act.activation(tg[:], gates[:, 0:4], ACT.Tanh)
                act.activation(gam[:], gates[:, 4:5], ACT.Sigmoid).then_inc(gat, 1)
                act.wait_ge(m_ps, 1)
                act.activation(M[:], bank[:, 0, 0:C], ACT.Copy).then_inc(m_sb, 1)
                for b in range(B):
                    act.wait_ge(z_ps, b + 1)
                    act.activation(Z[:, b, :], bank[:, b % 2, :], ACT.Copy).then_inc(z_sb, 1)
                    for r in range(R):
                        t = R * b + r
                        act.wait_ge(s_ps, t + 1)
                        act.activation(S[:, t, :], bank[:, 2 + t % 6, :], ACT.Copy).then_inc(s_sb, 1)
                with act.Fori(0, HALVINGS) as i:
                    for h in range(2):
                        act.wait_ge(nmid_r[h], i + 1)
                        for j in range(GROUPS[h].start, GROUPS[h].stop):
                            last = act.activation(junk_s[:, j, :], S[:, VT + j, :], ACT.Sign, bias=nmid[:, j:j + 1],
                                                  accum_out=cnt[:, VT + j:VT + j + 1])
                        last.then_inc(cnt_s, 1)
                act.wait_ge(coef, 1)
                act.wait_ge(x_in_s[3], 16)
                for t in range(T):
                    if t >= 2:
                        act.wait_ge(a_r, t - 1)
                    act.activation(sg[:, t % 2, :], S[:, t, :], ACT.Sigmoid, scale=GRAPH_SCALE).then_inc(sig_r, 1)
                for t in range(T):
                    if t >= 2:
                        act.wait_ge(x_r, t - 1)
                    act.activation(yb[:, t % 2, :], x[:, t, :], ACT.Identity, bias=bi1[:, t:t + 1],
                                   scale=sc1[:, t:t + 1]).then_inc(y_r, 1)

            @block.gpsimd
            def _(pool):
                step = linked(pool, g["pool_chain"])
                step(pool.memset(ident[:], 0.0))
                step(pool.memset(half[:], -0.5))
                pool.affine_select(out=ident[:], in_=ident[:], compare_op=ALU.not_equal, fill=1.0, base=0,
                                   pattern=[[-1, P]], channel_multiplier=1).then_inc(cst, 1)
                pool.wait_ge(lnst, 1)
                step(rstd_steps(pool, sm1[:], mv, 1.0, LN_EPS, half[:], rstd[:], nmr[:], step))
                pool.wait_ge(gat, 1)
                step(pool.tensor_scalar(c1[:], gam[:], -1.0, 1.0, ALU.mult, ALU.add))
                step(pool.tensor_tensor(c1[:], c1[:], tg[:, 0:1], ALU.mult))
                step(pool.tensor_tensor(c2[:], gam[:], tg[:, 0:1], ALU.mult))
                step(pool.tensor_scalar(c2[:], c2[:], 0.5, None, ALU.mult))
                step(pool.tensor_scalar(sc1[:], rstd[:], c1[:, 0:1], 1.0, ALU.mult, ALU.add))
                pool.tensor_scalar(bi1[:], nmr[:], c1[:, 0:1], 0.0, ALU.mult, ALU.add).then_inc(coef, 1)
                pool.wait_ge(sim_st, 1)
                mean, var = smv[:, :, 0], smv[:, :, 1]
                step(pool.tensor_scalar(half[:], half[:], -1.0, None, ALU.mult))
                step(pool.tensor_tensor(sigma[:], var, half[:], ALU.pow))
                step(pool.tensor_tensor(slack[:], mean, mean, ALU.mult))
                step(pool.tensor_tensor(slack[:], slack[:], var, ALU.add))
                step(pool.tensor_tensor(slack[:], slack[:], half[:], ALU.pow))
                step(pool.tensor_scalar(half[:], half[:], -1.0, None, ALU.mult))
                step(pool.tensor_scalar(slack[:], slack[:], 2.0 ** -18, None, ALU.mult))
                step(pool.tensor_scalar(low[:], sigma[:], -1.02 * MEAN_TO_LOW, None, ALU.mult))
                step(pool.tensor_tensor(low[:], low[:], mean, ALU.add))
                step(pool.tensor_tensor(low[:], low[:], slack[:], ALU.subtract))
                step(pool.tensor_scalar(width[:], sigma[:], 1.04 * (MEAN_TO_LOW + MEAN_TO_HIGH), None, ALU.mult))
                step(pool.tensor_tensor(width[:], width[:], slack[:], ALU.add))
                step(pool.tensor_tensor(width[:], width[:], slack[:], ALU.add))
                pool.tensor_scalar(width[:], width[:], 0.5, None, ALU.mult).then_inc(brk, 1)
                pool.wait_ge(brk, 1)
                step(pool.tensor_scalar(nlow[:], low[:, VT:T], -1.0, None, ALU.mult))
                for h, own in enumerate(GROUPS):
                    at = slice(VT + own.start, VT + own.stop)
                    pool.tensor_tensor(nmid[:, own], nlow[:, own], width[:, at], ALU.subtract).then_inc(nmid_r[h], 1)

            @block.vector
            def _(dve):
                step = linked(dve, g["vector_chain"])
                for b in range(B):
                    dve.wait_ge(x_in_s[b], 16)
                    for t in range(R * b, R * b + R):
                        last = dve.bn_stats(stats[:, t, :], x[:, t, :])
                step(last)
                for t in range(T):
                    last = dve.bn_aggr(mv[:, t, :], stats[:, t, :])
                last.then_inc(lnst, 1)
                for t in range(T):
                    dve.wait_ge(s_sb, t + 1)
                    last = dve.bn_stats(sst[:, t, :], S[:, t, :])
                step(last)
                for t in range(T):
                    last = dve.bn_aggr(smv[:, t, :], sst[:, t, :])
                last.then_inc(sim_st, 1)
                own = slice(0, VT)
                dve.wait_ge(brk, 1)
                step(dve.tensor_tensor(mid[:, own], low[:, own], width[:, own], ALU.add))
                uch = sem("gr_vector_search_chain")
                with dve.Fori(0, HALVINGS) as i:
                    step = chained(dve, uch, 9 * i)

                    def renew(h):
                        own, at = GROUPS[h], slice(VT + GROUPS[h].start, VT + GROUPS[h].stop)
                        dve.wait_ge(cnt_s, 2 * i + h + 1)
                        step(dve.scalar_tensor_tensor(sel[:, at], cnt[:, at], float(2 * TOP - N), width[:, at],
                                                      ALU.is_ge, ALU.mult))
                        step(dve.tensor_tensor(nlow[:, own], nlow[:, own], sel[:, at], ALU.subtract))
                        dve.scalar_tensor_tensor(nmid[:, own], width[:, at], -0.5, nlow[:, own], ALU.mult, ALU.add)\
                           .then_inc(nmid_r[h], 1)

                    for t in range(VT):
                        last = dve.tensor_scalar(junk_v[:, t, :], S[:, t, :], mid[:, t:t + 1], None, ALU.is_ge,
                                                 ALU.add, accum_out=cnt[:, t:t + 1])
                        if t == VT // 2:
                            renew(0)
                    step(last)
                    step(dve.scalar_tensor_tensor(sel[:, own], cnt[:, own], float(TOP) - 0.5, width[:, own],
                                                  ALU.is_ge, ALU.mult))
                    step(dve.tensor_tensor(low[:, own], low[:, own], sel[:, own], ALU.add))
                    step(dve.scalar_tensor_tensor(mid[:, own], width[:, own], 0.5, low[:, own], ALU.mult, ALU.add))
                    renew(1)
                    for h in range(2):
                        dve.wait_ge(nmid_r[h], i + 2)
                    step(dve.tensor_scalar(width[:], width[:], 0.5, None, ALU.mult))
                step = linked(dve, g["vector_chain"])
                step(dve.tensor_scalar(low[:, VT:T], nlow[:], -1.0, None, ALU.mult))
                for t in range(T):
                    dve.wait_ge(sig_r, t + 1)
                    dve.scalar_tensor_tensor(S[:, t, :], S[:, t, :], low[:, t:t + 1], sg[:, t % 2, :],
                                             ALU.is_ge, ALU.mult).then_inc(a_r, 1)
                for t in range(T):
                    dve.wait_ge(at_r, t + 1)
                    dve.tensor_tensor(tb[:, t % 2, :], bank[:, t % 8, :], S[:, t, :], ALU.add).then_inc(t_r, 1)
                    dve.wait_ge(t_r, t + 1)
                    dve.wait_ge(y_r, t + 1)
                    dve.scalar_tensor_tensor(x[:, t, :], tb[:, t % 2, :], c2[:, 0:1], yb[:, t % 2, :],
                                             ALU.mult, ALU.add).then_inc(x_r, 1)


def phase_moe(nc, sb, sem, g):
    x, bank, ident, tg, stats, mv = g["x"], g["bank"], g["ident"], g["tg"], g["stats"], g["mv"]
    half, rstd, nmr, sm1 = g["half"], g["rstd"], g["nmr"], g["sm1"]
    with ExitStack() as scope:
        def s_(name, shape, dt=F32):
            return sb(name, shape, dt, scope)
        xT_hi = s_("moe_xT_hi", [P, DC, B * N], F32R)
        xT_lo = s_("moe_xT_lo", [P, DC, B * N], F32R)
        coefs = s_("moe_coefs", [P, MOE_UNITS, T])
        with ExitStack() as inner:
            def i_(name, shape, dt=F32):
                return sb(name, shape, dt, inner)
            xn = i_("moe_xn", [P, 2, D])
            rw = i_("moe_rw", [P, DC, E_])
            rw_hi = i_("moe_rw_hi", [P, DC, E_], F32R)
            rw_lo = i_("moe_rw_lo", [P, DC, E_], F32R)
            logits = i_("moe_logits", [P, T, E_])
            best = i_("moe_best", [P, T, 8])
            best_at = i_("moe_best_at", [P, T, 8], U32)
            at_f = i_("moe_at_f", [P, 2, T])
            gap = i_("moe_gap", [P, T])
            w2 = i_("moe_w2", [P, T])
            w1 = i_("moe_w1", [P, T])
            eids = i_("moe_eids", [P, E_, T], I32)
            eids_f = i_("moe_eids_f", [P, E_, T])
            pick = i_("moe_pick", [P, E_, T])

            rw_in = sem("moe_router_arrived")
            rw_h = sem("moe_router_hi")
            rw_l = sem("moe_router_lo")
            st_r = sem("moe_stats_ready")
            ln_r = sem("moe_rstd_ready")
            xn_r = sem("moe_xn_ready")
            xt_p = sem("moe_xT_transposed")
            xt_h = sem("moe_xT_hi_ready")
            xt_l = sem("moe_xT_lo_ready")
            lg_p = sem("moe_logits_done")
            gp_r = sem("moe_gap_ready")
            ex_r = sem("moe_exp_ready")
            io_r = sem("moe_ids_ready")

            with nc.Block() as block:
                @block.sync
                def _(sp):
                    sp.dma_start(rw[:], g["router_w"].rearrange("(c p) e -> p c e", p=P)).then_inc(rw_in, 16)

                @block.gpsimd
                def _(pool):
                    step = linked(pool, g["pool_chain"])
                    step(pool.iota(eids[:], pattern=[[1, E_], [0, T]], base=0, channel_multiplier=0))
                    pool.tensor_copy(eids_f[:], eids[:]).then_inc(io_r, 1)
                    pool.wait_ge(st_r, 1)
                    step(rstd_steps(pool, sm1[:], mv, 1.0, LN_EPS, half[:], rstd[:], nmr[:], step))
                    pool.tensor_copy(sm1[:], rstd[:]).then_inc(ln_r, 1)
                    pool.wait_ge(rw_h, 1)
                    pool.tensor_tensor(rw_lo[:], rw[:], rw_hi[:].bitcast(F32), ALU.subtract).then_inc(rw_l, 1)

                @block.scalar
                def _(act):
                    act.wait_ge(rw_in, 16)
                    act.activation(rw_hi[:], rw[:], ACT.Copy).then_inc(rw_h, 1)
                    act.wait_ge(ln_r, 1)

                    def normalise(t):
                        if t >= 2:
                            act.wait_ge(xt_p, t - 1)
                        act.activation(xn[:, t % 2, :], x[:, t, :], ACT.Identity, bias=nmr[:, t:t + 1],
                                       scale=rstd[:, t:t + 1]).then_inc(xn_r, 1)

                    normalise(0)
                    for t in range(T):
                        if t + 1 < T:
                            normalise(t + 1)
                        act.wait_ge(xt_p, t + 1)
                        act.activation(xT_hi[:, :, t * P:(t + 1) * P],
                                       bank[:, t % 4, :].rearrange("p (c n) -> p c n", c=DC), ACT.Copy)\
                           .then_inc(xt_h, 1)
                    act.wait_ge(gp_r, 1)
                    act.activation(w2[:], gap[:], ACT.Exp).then_inc(ex_r, 1)

                def router(pe, t):
                    pe.wait_ge(xt_l, t + 1)
                    at = slice(t * P, (t + 1) * P)
                    passes = [(a, w, c) for c in range(DC) for a, w in ((xT_hi, rw_hi), (xT_hi, rw_lo), (xT_lo, rw_hi))]
                    for k, (a, w, c) in enumerate(passes):
                        last = pe.matmul(bank[:, 4, t * E_:(t + 1) * E_], a[:, c, at], w[:, c, :],
                                         start=k == 0, stop=k == len(passes) - 1)
                    last.then_inc(lg_p, 1)

                @block.tensor
                def _(pe):
                    pe.wait_ge(rw_l, 1)
                    for t in range(T):
                        pe.wait_ge(xn_r, t + 1)
                        if t >= 4:
                            pe.wait_ge(xt_l, t - 3)
                        for c in range(DC):
                            last = pe.transpose(bank[:, t % 4, c * P:(c + 1) * P], xn[:, t % 2, c * P:(c + 1) * P],
                                                ident[:])
                        last.then_inc(xt_p, 1)
                        if t >= 1:
                            router(pe, t - 1)
                    router(pe, T - 1)

                @block.vector
                def _(dve):
                    step = linked(dve, g["vector_chain"])
                    for t in range(T):
                        last = dve.bn_stats(stats[:, t, :], x[:, t, :])
                    step(last)
                    for t in range(T):
                        last = dve.bn_aggr(mv[:, t, :], stats[:, t, :])
                    last.then_inc(st_r, 1)
                    for t in range(T):
                        dve.wait_ge(xt_h, t + 1)
                        at = slice(t * P, (t + 1) * P)
                        dve.tensor_tensor(xT_lo[:, :, at], bank[:, t % 4, :].rearrange("p (c n) -> p c n", c=DC),
                                          xT_hi[:, :, at].bitcast(F32), ALU.subtract).then_inc(xt_l, 1)
                    dve.wait_ge(lg_p, T)
                    step(dve.tensor_copy(logits[:], bank[:, 4, 0:T * E_].rearrange("p (t e) -> p t e", e=E_)))
                    for t in range(T):
                        last = dve.max(best[:, t, :], logits[:, t, :])
                    step(last)
                    dve.tensor_tensor(gap[:], best[:, :, 1], best[:, :, 0], ALU.subtract).then_inc(gp_r, 1)
                    for t in range(T):
                        last = dve.max_index(best_at[:, t, :], best[:, t, :], logits[:, t, :])
                    step(last)
                    step(dve.tensor_copy(at_f[:], best_at[:, :, 0:2].rearrange("p t k -> p k t")))
                    dve.wait_ge(ex_r, 1)
                    step(dve.tensor_scalar(w1[:], w2[:], 1.0, None, ALU.add))
                    step(dve.reciprocal(w1[:], w1[:]))
                    step(dve.tensor_scalar(w1[:], w1[:], tg[:, 2:3], None, ALU.mult))
                    step(dve.tensor_tensor(w2[:], w2[:], w1[:], ALU.mult))
                    dve.wait_ge(io_r, 1)
                    for k, w in ((0, w1), (1, w2)):
                        dst = coefs[:, 0:E_, :] if k == 0 else pick[:]
                        each = at_f[:, k, :].unsqueeze(1).broadcast_to([P, E_, T])
                        step(dve.tensor_tensor(dst, eids_f[:], each, ALU.is_equal))
                        step(dve.tensor_tensor(dst, dst, w[:].unsqueeze(1).broadcast_to([P, E_, T]), ALU.mult))
                    step(dve.tensor_tensor(coefs[:, 0:E_, :], coefs[:, 0:E_, :], pick[:], ALU.add))
                    ones = coefs[:, E_:MOE_UNITS, :]
                    step(dve.memset(ones, 1.0))
                    step(dve.tensor_scalar(ones, ones, tg[:, 2:3], None, ALU.mult))

        def source(u, p, loop):
            if loop:
                return (g["w_gate"][u].rearrange("(c p) h -> p c h", p=P),
                        g["w_up"][u].rearrange("(c p) h -> p c h", p=P),
                        g["w_down"][u].rearrange("(k p) d -> p k d", p=P))
            at = slice(p * UH, (p + 1) * UH)
            return (g["sw_gate"][:, at].rearrange("(c p) h -> p c h", p=P),
                    g["sw_up"][:, at].rearrange("(c p) h -> p c h", p=P),
                    g["sw_down"][at, :].rearrange("(k p) d -> p k d", p=P))

        gated_units(nc, s_, sem, "moe", x, bank, xT_hi, xT_lo, MOE_UNITS, source, coefs=coefs)


def gated_units(nc, s_, sem, tag, x, bank, xT_hi, xT_lo, units, source, coefs=None, gate=None, mod=None):
    raw_g = s_(tag + "_raw_g", [P, DC, UH])
    raw_u = s_(tag + "_raw_u", [P, DC, UH])
    raw_d = s_(tag + "_raw_d", [P, HC, D])
    g_hi = s_(tag + "_g_hi", [P, 2, DC, UH], F32R)
    g_lo = s_(tag + "_g_lo", [P, 2, DC, UH], F32R)
    u_hi = s_(tag + "_u_hi", [P, 2, DC, UH], F32R)
    u_lo = s_(tag + "_u_lo", [P, 2, DC, UH], F32R)
    d_hi = s_(tag + "_d_hi", [P, 2, HC, D], F32R)
    d_lo = s_(tag + "_d_lo", [P, 2, HC, D], F32R)
    sil = s_(tag + "_silu", [P, HC, 512])
    hid = s_(tag + "_hidden", [P, HC, 512])
    h_hi = s_(tag + "_h_hi", [P, 2, HC, 512], F32R)
    h_lo = s_(tag + "_h_lo", [P, 2, HC, 512], F32R)
    if coefs is not None:
        coef = s_(tag + "_coef", [P, 2, T])
    if mod is not None:
        b_stack, m_stack = mod
        b_unit = s_(tag + "_b_unit", [96, 2, UH], F32R)

    w_in = sem(tag + "_w_arrived")
    w_hi = sem(tag + "_w_hi_ready")
    w_lo = sem(tag + "_w_lo_ready")
    g_ps = sem(tag + "_gate_done")
    u_ps = sem(tag + "_up_done")
    sil_r = sem(tag + "_silu_ready")
    hid_r = sem(tag + "_hidden_ready")
    hhi_r = sem(tag + "_h_hi_ready")
    hlo_r = sem(tag + "_h_lo_ready")
    y_ps = sem(tag + "_y_done")
    acc_r = sem(tag + "_y_added")
    loops = units // 2 - 1

    with nc.Block() as block:
        @block.sync
        def _(sp):
            def load(u, p, loop):
                sp.wait_ge(w_lo, u)
                for dst, src in zip((raw_g, raw_u, raw_d), source(u, p, loop)):
                    sp.dma_start(dst[:], src).then_inc(w_in, 16)
            with sp.Fori(0, loops) as i:
                for p in range(2):
                    load(2 * i + p, p, True)
            for p in range(2):
                load(2 * loops + p, p, False)

        @block.gpsimd
        def _(pool):
            def split_lo(u, p, first=False):
                if coefs is not None and not first:
                    pool.wait_ge(acc_r, 16 * u - 16 + ACC_LEAD)
                pool.wait_ge(w_hi, u + 1)
                pool.tensor_tensor(g_lo[:, p], raw_g[:], g_hi[:, p].bitcast(F32), ALU.subtract)
                if coefs is not None:
                    pool.tensor_copy(coef[:, p, :], coefs[:, u, :])
                if mod is not None:
                    pool.tensor_copy(b_unit[:, p, :], b_stack[:, bass.ds(u * UH, UH)].bitcast(F32))
                pool.tensor_tensor(u_lo[:, p], raw_u[:], u_hi[:, p].bitcast(F32), ALU.subtract)
                pool.tensor_tensor(d_lo[:, p], raw_d[:], d_hi[:, p].bitcast(F32), ALU.subtract).then_inc(w_lo, 1)

            split_lo(0, 0, first=True)
            with pool.Fori(0, loops) as i:
                for p in range(2):
                    split_lo(2 * i + p + 1, (p + 1) % 2)
            split_lo(2 * loops + 1, 1)

        @block.scalar
        def _(act):
            act.sem_inc(sil_r, GU_LEAD)

            def split_hi(u, p, first=False):
                act.wait_ge(w_in, 48 * (u + 1))
                if not first:
                    act.wait_ge(y_ps, 16 * u + Y_LEAD - 16)
                act.activation(g_hi[:, p], raw_g[:], ACT.Copy)
                act.activation(u_hi[:, p], raw_u[:], ACT.Copy)
                act.activation(d_hi[:, p], raw_d[:], ACT.Copy).then_inc(w_hi, 1)

            def hidden(n, tb):
                for c in range(HC):
                    act.wait_ge(g_ps, 2 * n + c + 1)
                    act.wait_ge(hid_r, 2 * n + c - 1 + GU_LEAD)
                    act.activation(sil[:, c, :], bank[:, 2 * c, :], ACT.Silu).then_inc(sil_r, 1)
                for c in range(HC):
                    act.wait_ge(hid_r, 2 * n + c + 1 + GU_LEAD)
                    if c == 0:
                        act.wait_ge(y_ps, 4 * n - 4 + Y_LEAD)
                    act.activation(h_hi[:, tb % 2, c, :], hid[:, c, :], ACT.Copy).then_inc(hhi_r, 1)

            def pair(i, last):
                for p in range(2):
                    for tb in range(TB):
                        n = 8 * i + 4 * p + tb
                        if not (last and p == 1 and tb == TB - 1):
                            hidden(n + 1, (tb + 1) % TB)
                        if tb == 0 and not (last and p == 1):
                            split_hi(2 * i + p + 1, (p + 1) % 2)

            split_hi(0, 0, first=True)
            hidden(0, 0)
            with act.Fori(0, loops) as i:
                pair(i, False)
            pair(loops, True)

        @block.tensor
        def _(pe):
            pe.sem_inc(y_ps, Y_LEAD)

            def gate_up(n, u, p, tb):
                if tb == 0:
                    pe.wait_ge(w_lo, u + 1)
                at = slice(tb * 512, (tb + 1) * 512)
                for c in range(HC):
                    hs = slice(c * P, (c + 1) * P)
                    for which, (w_h, w_l) in enumerate(((g_hi, g_lo), (u_hi, u_lo))):
                        pe.wait_ge((sil_r, hid_r)[which], 2 * n + c - 1 + GU_LEAD)
                        passes = [(w, a, k) for k in range(DC) for w, a in ((w_h, xT_hi), (w_h, xT_lo), (w_l, xT_hi))]
                        more = mod is not None and which == 0
                        for k, (w, a, d) in enumerate(passes):
                            last = pe.matmul(bank[:, 2 * c + which, :], w[:, p, d, hs], a[:, d, at], start=k == 0,
                                             stop=k == len(passes) - 1 and not more)
                        if more:
                            last = pe.matmul(bank[:, 2 * c, :], b_unit[:, p, hs], m_stack[:, at], start=False, stop=True)
                        last.then_inc((g_ps, u_ps)[which], 1)

            def down(n, p, tb):
                pe.wait_ge(hlo_r, 2 * n + 2 + GU_LEAD)
                for j in range(4):
                    js = slice(j * P, (j + 1) * P)
                    pe.wait_ge(acc_r, 4 * n + j - 3 + ACC_LEAD)
                    passes = [(h, w, k) for k in range(HC) for h, w in ((h_hi, d_hi), (h_hi, d_lo), (h_lo, d_hi))]
                    for k, (h, w, c) in enumerate(passes):
                        last = pe.matmul(bank[:, 4 + j, :], h[:, tb % 2, c, js], w[:, p, c, :], start=k == 0,
                                         stop=k == len(passes) - 1)
                    last.then_inc(y_ps, 1)

            def pair(i, last):
                for p in range(2):
                    for tb in range(TB):
                        n = 8 * i + 4 * p + tb
                        over = tb == TB - 1
                        if not (last and p == 1 and over):
                            gate_up(n + 1, 2 * i + p + over, (p + over) % 2, (tb + 1) % TB)
                        down(n, p, tb)

            gate_up(0, 0, 0, 0)
            with pe.Fori(0, loops) as i:
                pair(i, False)
            pair(loops, True)

        @block.vector
        def _(dve):
            dve.sem_inc(hid_r, GU_LEAD)
            dve.sem_inc(acc_r, ACC_LEAD)
            dve.sem_inc(hlo_r, GU_LEAD)

            def hidden(n, tb):
                for c in range(HC):
                    dve.wait_ge(sil_r, 2 * n + c + 1 + GU_LEAD)
                    dve.wait_ge(u_ps, 2 * n + c + 1)
                    dve.wait_ge(hlo_r, 2 * n + c - 1 + GU_LEAD)
                    dve.tensor_tensor(hid[:, c, :], bank[:, 2 * c + 1, :], sil[:, c, :], ALU.mult).then_inc(hid_r, 1)
                for c in range(HC):
                    dve.wait_ge(hhi_r, 2 * n + c + 1)
                    dve.tensor_tensor(h_lo[:, tb % 2, c, :], hid[:, c, :], h_hi[:, tb % 2, c, :].bitcast(F32),
                                      ALU.subtract).then_inc(hlo_r, 1)

            def add(n, p, tb):
                for j in range(4):
                    t = 4 * tb + j
                    dve.wait_ge(y_ps, 4 * n + j + 1 + Y_LEAD)
                    dve.wait_ge(acc_r, 4 * n + j - 15 + ACC_LEAD)
                    scalar = coef[:, p, t:t + 1] if coefs is not None else gate
                    dve.scalar_tensor_tensor(x[:, t, :], bank[:, 4 + j, :], scalar, x[:, t, :], ALU.mult, ALU.add)\
                       .then_inc(acc_r, 1)

            def pair(i, last):
                for p in range(2):
                    for tb in range(TB):
                        n = 8 * i + 4 * p + tb
                        if not (last and p == 1 and tb == TB - 1):
                            hidden(n + 1, (tb + 1) % TB)
                        add(n, p, tb)

            hidden(0, 0)
            with dve.Fori(0, loops) as i:
                pair(i, False)
            pair(loops, True)


def phase_kv(nc, sb, sem, g):
    x, bank, ident, tg, stats, mv = g["x"], g["bank"], g["ident"], g["tg"], g["stats"], g["mv"]
    half, rstd, nmr, sm1 = g["half"], g["rstd"], g["nmr"], g["sm1"]
    with ExitStack() as scope:
        def s_(name, shape, dt=F32):
            return sb(name, shape, dt, scope)
        ctxT = s_("kv_ctxT", [P, B, N])
        wk = s_("kv_wk", [C, C])
        bk = s_("kv_bk", [C, 1])
        gamma = s_("kv_gamma", [P, N])
        beta = s_("kv_beta", [P, N])
        kvT = s_("kvT", [C, 2, N])
        kv = s_("kv", [P, 2, R, C])
        xn = s_("kv_xn", [P, R, D])
        xnT = s_("kv_xnT", [P, DC, N])
        outT = s_("kv_outT", [C, 2, N])
        sst = s_("kv_sim_stats", [P, R, 6])
        smv = s_("kv_sim_mv", [P, R, 2])
        sr = s_("kv_sim_rstd", [P, R])
        sn = s_("kv_sim_nmr", [P, R])
        sv = s_("kv_sim_var", [P, R])
        y = s_("kv_y", [P, R, N])
        yb = s_("kv_yb", [P, R, N])
        nmax = s_("kv_nmax", [P, R])
        total = s_("kv_total", [P, R])
        share = s_("kv_share", [P, R])
        ex = s_("kv_exp", [P, R, N])

        w_in = sem("kv_weights_arrived")
        st_r = sem("kv_stats_ready")
        ln_r = sem("kv_rstd_ready")
        kvT_p = sem("kv_kvT_done")
        kvT_r = sem("kv_kvT_ready")
        kv_p = sem("kv_kv_transposed")
        kv_r = sem("kv_kv_ready")
        xn_r = sem("kv_xn_ready")
        xt_p = sem("kv_xnT_transposed")
        xt_r = sem("kv_xnT_ready")
        ot_p = sem("kv_outT_done")
        ot_r = sem("kv_outT_ready")
        sim_p = sem("kv_sim_done")
        sst_r = sem("kv_sim_stats_ready")
        srs_r = sem("kv_sim_rstd_ready")
        y_r = sem("kv_y_ready")
        yg_r = sem("kv_y_gamma_ready")
        yb_r = sem("kv_y_beta_ready")
        mx_r = sem("kv_max_ready")
        ex_r = sem("kv_exp_ready")
        x_r = sem("kv_x_ready")

        with nc.Block() as block:
            @block.sync
            def _(sp):
                sp.dma_start(ctxT[:], g["ctxT_in"].rearrange("c (b n) -> c b n", b=B)).then_inc(w_in, 16)
                sp.dma_start(wk[:], g["WkT"]).then_inc(w_in, 16)
                sp.dma_start(bk[:], g["b_k"].unsqueeze(1)).then_inc(w_in, 16)
                sp.dma_start(gamma[:], g["ln_gamma"].partition_broadcast(P)).then_inc(w_in, 16)
                sp.dma_start(beta[:], g["ln_beta"].partition_broadcast(P)).then_inc(w_in, 16)

            @block.tensor
            def _(pe):
                pe.wait_ge(w_in, 80)
                for b in range(B):
                    if b >= 1:
                        pe.wait_ge(xt_r, 4 * b - 2)
                    pe.matmul(bank[:, 0, :], wk[:], ctxT[:, b, :], start=True, stop=True).then_inc(kvT_p, 1)
                    pe.wait_ge(kvT_r, b + 1)
                    for j in range(R):
                        last = pe.transpose(bank[:, 1, j * C:(j + 1) * C], kvT[:, b % 2, j * P:(j + 1) * P], ident[:])
                    last.then_inc(kv_p, 1)
                    pe.wait_ge(xn_r, R * (b + 1))
                    for c in range(DC):
                        if b >= 1 or c >= 2:
                            pe.wait_ge(xt_r, 4 * b + c - 2)
                        if c == 2:
                            pe.wait_ge(kvT_r, b + 1)
                            pe.wait_ge(kv_r, b + 1)
                        for r in range(R):
                            last = pe.transpose(bank[:, (c + 2) % 4, r * P:(r + 1) * P], xn[:, r, c * P:(c + 1) * P],
                                                ident[:])
                        last.then_inc(xt_p, 1)
                    pe.wait_ge(kv_r, b + 1)
                    pe.wait_ge(xt_r, 4 * b + 4)
                    if b >= 1:
                        pe.wait_ge(ot_r, b)
                    for c in range(DC):
                        last = pe.matmul(bank[:, 2, :], kv[:, b % 2, c, :], xnT[:, c, :], start=c == 0, stop=c == DC - 1)
                    last.then_inc(ot_p, 1)
                    pe.wait_ge(ot_r, b + 1)
                    for r in range(R):
                        if b >= 1:
                            pe.wait_ge(y_r, R * (b - 1) + r + 1)
                        pe.matmul(bank[:, 4 + r, :], outT[:, b % 2, r * P:(r + 1) * P], kvT[:, b % 2, :],
                                  start=True, stop=True).then_inc(sim_p, 1)

            @block.scalar
            def _(act):
                act.wait_ge(ln_r, 1)
                act.wait_ge(w_in, 80)

                def prepare(b):
                    act.wait_ge(kvT_p, b + 1)
                    if b >= 2:
                        act.wait_ge(sim_p, R * (b - 1))
                    act.activation(kvT[:, b % 2, :], bank[:, 0, :], ACT.Identity, bias=bk[:, 0:1]).then_inc(kvT_r, 1)
                    act.wait_ge(kv_p, b + 1)
                    act.activation(kv[:, b % 2], bank[:, 1, :].rearrange("p (j c) -> p j c", j=R), ACT.Copy)\
                       .then_inc(kv_r, 1)
                    if b >= 1:
                        act.wait_ge(xt_p, DC * b)
                    for r in range(R):
                        t = R * b + r
                        act.activation(xn[:, r, :], x[:, t, :], ACT.Identity, bias=nmr[:, t:t + 1],
                                       scale=rstd[:, t:t + 1]).then_inc(xn_r, 1)
                    for c in range(DC):
                        act.wait_ge(xt_p, DC * b + c + 1)
                        if b >= 1:
                            act.wait_ge(ot_p, b)
                        act.activation(xnT[:, c, :], bank[:, (c + 2) % 4, :], ACT.Copy).then_inc(xt_r, 1)
                    act.wait_ge(ot_p, b + 1)
                    act.activation(outT[:, b % 2, :], bank[:, 2, :], ACT.Copy).then_inc(ot_r, 1)

                def soften(b):
                    act.wait_ge(srs_r, b + 1)
                    if b >= 1:
                        act.wait_ge(yb_r, R * b)
                    for r in range(R):
                        act.activation(y[:, r, :], bank[:, 4 + r, :], ACT.Identity, bias=sn[:, r:r + 1],
                                       scale=sr[:, r:r + 1]).then_inc(y_r, 1)
                    act.wait_ge(mx_r, b + 1)
                    if b >= 1:
                        act.wait_ge(x_r, R * b)
                    for r in range(R):
                        act.activation(ex[:, r, :], yb[:, r, :], ACT.Exp, bias=nmax[:, r:r + 1],
                                       accum_out=total[:, r:r + 1]).then_inc(ex_r, 1)

                for b in range(B):
                    prepare(b)
                    soften(b)

            @block.gpsimd
            def _(pool):
                step = linked(pool, g["pool_chain"])
                pool.wait_ge(st_r, 1)
                step(rstd_steps(pool, sm1[:], mv, 1.0, LN_EPS, half[:], rstd[:], nmr[:], step))
                pool.tensor_copy(sm1[:], rstd[:]).then_inc(ln_r, 1)
                pool.wait_ge(w_in, 80)
                for b in range(B):
                    step = linked(pool, g["pool_chain"])
                    pool.wait_ge(sst_r, b + 1)
                    if b >= 1:
                        pool.wait_ge(y_r, R * b)
                    step(pool.tensor_scalar(sv[:], smv[:, :, 1], KV_SCALE * KV_SCALE, KV_EPS, ALU.mult, ALU.add))
                    step(pool.tensor_tensor(sv[:], sv[:], half[:, 0:R], ALU.pow))
                    step(pool.tensor_scalar(sr[:], sv[:], KV_SCALE, None, ALU.mult))
                    step(pool.tensor_tensor(sn[:], smv[:, :, 0], sr[:], ALU.mult))
                    pool.tensor_scalar(sn[:], sn[:], -1.0, None, ALU.mult).then_inc(srs_r, 1)
                    for r in range(R):
                        pool.wait_ge(yg_r, R * b + r + 1)
                        if b >= 1 and r == 0:
                            pool.wait_ge(ex_r, R * b)
                        pool.tensor_tensor(yb[:, r, :], y[:, r, :], beta[:], ALU.add).then_inc(yb_r, 1)

            @block.vector
            def _(dve):
                step = linked(dve, g["vector_chain"])
                for t in range(T):
                    last = dve.bn_stats(stats[:, t, :], x[:, t, :])
                step(last)
                for t in range(T):
                    last = dve.bn_aggr(mv[:, t, :], stats[:, t, :])
                last.then_inc(st_r, 1)
                dve.wait_ge(w_in, 80)
                for b in range(B):
                    step = linked(dve, g["vector_chain"])
                    for r in range(R):
                        dve.wait_ge(sim_p, R * b + r + 1)
                        last = dve.bn_stats(sst[:, r, :], bank[:, 4 + r, :])
                    step(last)
                    for r in range(R):
                        last = dve.bn_aggr(smv[:, r, :], sst[:, r, :])
                    last.then_inc(sst_r, 1)
                    for r in range(R):
                        dve.wait_ge(y_r, R * b + r + 1)
                        dve.tensor_tensor(y[:, r, :], y[:, r, :], gamma[:], ALU.mult).then_inc(yg_r, 1)
                    for r in range(R):
                        dve.wait_ge(yb_r, R * b + r + 1)
                        if b >= 1 and r == 0:
                            dve.wait_ge(ex_r, R * b)
                        last = dve.reduce_max(nmax[:, r:r + 1], yb[:, r, :], AX)
                    step(last)
                    dve.tensor_scalar(nmax[:], nmax[:], -1.0, None, ALU.mult).then_inc(mx_r, 1)
                    dve.wait_ge(ex_r, R * b + R)
                    if b >= 1:
                        dve.wait_ge(x_r, R * b)
                    step(dve.reciprocal(share[:], total[:]))
                    step(dve.tensor_scalar(share[:], share[:], tg[:, 1:2], None, ALU.mult))
                    for r in range(R):
                        t = R * b + r
                        dve.scalar_tensor_tensor(x[:, t, :], ex[:, r, :], share[:, r:r + 1], x[:, t, :],
                                                 ALU.mult, ALU.add).then_inc(x_r, 1)


def phase_attention_mlp(nc, sb, sem, g):
    x, bank, ident, tg, stats, mv = g["x"], g["bank"], g["ident"], g["tg"], g["stats"], g["mv"]
    half, rstd, nmr, sm1 = g["half"], g["rstd"], g["nmr"], g["sm1"]
    with ExitStack() as scope:
        def s_(name, shape, dt=F32):
            return sb(name, shape, dt, scope)
        n_sc = s_("n_scale", [P, T])
        n_bi = s_("n_bias", [P, T])
        mod = s_("mod", [P, T, RK])
        r_sc = s_("r_scale", [P, T])
        r_bi = s_("r_bias", [P, T])
        with ExitStack() as inner:
            phase_attention(nc, lambda n, s, d=F32: sb(n, s, d, inner), sem, dict(g, **locals()))
        phase_mlp(nc, s_, sem, dict(g, **locals()))


def phase_attention(nc, s_, sem, g):
    x, bank, ident, tg, stats, mv = g["x"], g["bank"], g["ident"], g["tg"], g["stats"], g["mv"]
    half, rstd, nmr, sm1 = g["half"], g["rstd"], g["nmr"], g["sm1"]
    n_sc, n_bi, r_sc, r_bi, mod = g["n_sc"], g["n_bi"], g["r_sc"], g["r_bi"], g["mod"]
    GH = P // HD
    GB = HEADS // GH
    US = GH * R
    KQ = 3 * HD
    raw = s_("at_raw", [P, 2, DC, D])
    wq_hi = s_("at_wq_hi", [P, DC, D], F32R)
    wq_lo = s_("at_wq_lo", [P, DC, D], F32R)
    wk_hi = s_("at_wk_hi", [P, DC, D], F32R)
    wk_lo = s_("at_wk_lo", [P, DC, D], F32R)
    wu_hi = s_("at_wu_hi", [P, DC, HEADS * RK], F32R)
    wu_lo = s_("at_wu_lo", [P, DC, HEADS * RK], F32R)
    A = s_("at_A", [P, DC, RK])
    woa = s_("at_woa", [P, DC, GH, RK])
    ln1 = s_("at_ln1", [P, DC])
    xn = s_("at_n", [P, R, D])
    xT_hi = s_("at_xT_hi", [P, DC, N], F32R)
    xT_lo = s_("at_xT_lo", [P, DC, N], F32R)
    q_hi = s_("at_q_hi", [P, N], F32R)
    q_lo = s_("at_q_lo", [P, N], F32R)
    k_hi = s_("at_k_hi", [P, N], F32R)
    k_lo = s_("at_k_lo", [P, N], F32R)
    Q = s_("at_Q", [KQ + 2, 2, GH, N], F32R)
    K = s_("at_K", [KQ + 2, 2, GH, N], F32R)
    U = s_("at_U", [P, R, HEADS, RK])
    UC = 2 * RK + 1
    OC = RK + 1
    V = s_("at_V", [P, 2, R, GH, 2 * UC], F32R)
    ones = s_("at_ones", [P, N])
    sel = s_("at_sel", [2 * UC, 2 * OC])
    mask_f = s_("at_mask_f", [P, P])
    mask = s_("at_mask", [P, P], F32R)
    maskT = s_("at_maskT", [P, P], F32R)
    ident_r = s_("at_ident", [P, P], F32R)
    mx = s_("at_max", [P, 2, US // 2])
    m_hi = s_("at_m_hi", [US // 2, 2, P], F32R)
    m_lo = s_("at_m_lo", [US // 2, 2, P], F32R)
    pT = s_("at_probsT", [P, 4, N])
    p_hi = s_("at_probsT_hi", [P, 4, N], F32R)
    p_lo = s_("at_probsT_lo", [P, 4, N], F32R)
    oT = s_("at_outT", [2 * UC, 2, N])
    rto = s_("at_rtotal", [P, R, 2])
    ou = s_("at_out", [P, R, 2, RK])
    red = s_("at_red", [P, R, RK])

    w_in, v_in, q_in = sem("at_small_arrived"), sem("at_values_arrived"), sem("at_queries_arrived")
    st_r, ln_r = sem("at_stats_ready"), sem("at_scales_ready")
    woa_p, woa_r = sem("at_woa_done"), sem("at_woa_ready")
    wu_p, wu_h, wu_l = sem("at_wu_done"), sem("at_wu_hi_ready"), sem("at_wu_lo_ready")
    wqk_h, wqk_l = sem("at_wqk_hi_ready"), sem("at_wqk_lo_ready")
    cst = sem("at_constants_ready")
    n_r = sem("at_n_ready")
    xt_p, xt_h, xt_l = sem("at_xT_transposed"), sem("at_xT_hi_ready"), sem("at_xT_lo_ready")
    q_p, q_h, q_l = sem("at_q_done"), sem("at_q_hi_ready"), sem("at_q_lo_ready")
    k_p, k_h, k_l = sem("at_k_done"), sem("at_k_hi_ready"), sem("at_k_lo_ready")
    u_p, u_r = sem("at_U_done"), sem("at_U_ready")
    qk_in = [sem(f"at_qk_of_head{j}_placed") for j in range(GH)]
    s_p, mx_r = sem("at_scores_done"), sem("at_max_ready")
    mt_p, m_h, m_l = sem("at_maxT_done"), sem("at_m_hi_ready"), sem("at_m_lo_ready")
    m_in = [sem(f"at_m_of_half{h}_placed") for h in range(2)]
    st_p, ex_r = sem("at_scoresT_done"), sem("at_probsT_ready")
    pl_r = sem("at_probs_lo_ready")
    v_h, v_r = sem("at_V_hi_ready"), sem("at_V_ready")
    o_p, ot_r, sl_p, o_r = sem("at_pv_done"), sem("at_outT_ready"), sem("at_out_turned"), sem("at_out_ready")
    och = sem("at_out_chain")
    ST_LEAD, EX_LEAD, O_LEAD, OR_LEAD, PL_LEAD, SL_LEAD, M_LEAD = 1, 2, 4, 2, 4, 2, 16
    TAIL = 8

    def at_least(eng, s, value):
        if not isinstance(value, int) or value > 0:
            eng.wait_ge(s, value)

    def each_step(step):
        step(-2, 2, True, False, False)
        step(-1, 3, True, True, False)
        return lambda b, last: [step(GB * b + oc, oc, not (last and oc >= 2), not (last and oc == 3), True)
                                for oc in range(GB)]

    def run(eng, step):
        batch = each_step(step)
        with eng.Fori(0, B - 1) as b:
            batch(b, False)
        batch(B - 1, True)

    def late(G, oc, s, lag):
        u = s - lag
        if 0 <= u < US:
            return G, oc, u
        return (G - 1, oc - 1, u + US) if u < 0 and oc > 0 else None

    BANK = {"m1": 1, "x0": 0, "x1": 1, "x2": 0, "x3": 1, "q": 0, "k": 1, "m0": 0, "u0": 1, "u1": 0}

    with nc.Block() as block:
        @block.sync
        def _(sp):
            sp.sem_inc(m_in[0], M_LEAD)
            sp.sem_inc(m_in[1], M_LEAD)
            sp.dma_start(raw[:, 0], g["Wo"].rearrange("(c p) o -> p c o", p=P)).then_inc(w_in, 16)
            sp.dma_start(A[:], g["A_in"].rearrange("(c p) r -> p c r", p=P)).then_inc(w_in, 16)
            sp.dma_start(ln1[:], g["ln1_w"]).then_inc(w_in, 16)
            sp.dma_start(raw[:, 1], g["Wv"].rearrange("(c p) d -> p c d", p=P)).then_inc(v_in, 16)
            sp.wait_ge(wu_p, DC)
            sp.dma_start(raw[:, 0], g["WqT"].rearrange("(c p) o -> p c o", p=P)).then_inc(q_in, 16)
            sp.dma_start(raw[:, 1], g["WkT1"].rearrange("(c p) o -> p c o", p=P)).then_inc(q_in, 16)

            def place_max(group, par, h):
                at_least(sp, m_l, 2 * group + h + 1)
                rows = slice(GH // 2 * h, GH // 2 * (h + 1))
                for row, part in ((KQ, m_hi), (KQ + 1, m_lo)):
                    sp.dma_start(Q[row:row + 1, par, rows, :].rearrange("o j t -> o (j t)").bitcast(F32),
                                 part[:, h, :].bitcast(F32)).then_inc(m_in[h], 16)

            def place_qk(G, oc, probs, j):
                if j == 0:
                    at_least(sp, q_l, G + 3)
                    at_least(sp, k_l, G + 3)
                if probs:
                    at_least(sp, st_p, US * G + R * (j + 1) + ST_LEAD)
                hp = slice(j * HD, (j + 1) * HD)
                for k, (pq, pk) in enumerate(((q_hi, k_hi), (q_lo, k_hi), (q_hi, k_lo))):
                    rows = slice(k * HD, (k + 1) * HD)
                    sp.dma_start(Q[rows, oc % 2, j, :].bitcast(F32), pq[hp, :].bitcast(F32)).then_inc(qk_in[j], 16)
                    sp.dma_start(K[rows, oc % 2, j, :].bitcast(F32), pk[hp, :].bitcast(F32)).then_inc(qk_in[j], 16)

            def step(G, oc, project, maxima, probs):
                if probs:
                    place_max(G, oc % 2, 1)
                if maxima:
                    place_max(G + 1, (oc + 1) % 2, 0)
                if project:
                    for j in range(GH):
                        place_qk(G, oc, probs, j)
            run(sp, step)

        @block.gpsimd
        def _(pool):
            step = linked(pool, g["pool_chain"])
            pool.memset(woa[:], 0.0).then_inc(cst, 1)
            step(pool.memset(mod[:], 0.0))
            step(pool.memset(ones[:], 1.0))
            for par in range(2):
                for j in range(GH):
                    step(pool.tensor_copy(K[KQ:KQ + 2, par, j, :], ones[KQ:KQ + 2, :]))
            pool.sem_inc(cst, 1)
            zeros = pT[:].rearrange("p s n -> p (s n)")
            step(pool.memset(zeros, 0.0))
            for par in range(2):
                step(pool.tensor_copy(V[:, par].rearrange("p r h c -> p (r h c)"), zeros[:, 0:R * GH * 2 * UC]))
                for h in range(GH):
                    at = UC * (h % 2) + RK
                    step(pool.tensor_copy(V[:, par, :, h, at:at + 1], ones[:, 0:R].unsqueeze(2)))
            step(pool.memset(sel[:], 0.0))
            for h in range(2):
                for row, cols in ((UC * h, OC), (UC * h + OC, RK)):
                    at = sel[:, OC * h:OC * h + cols]
                    step(pool.affine_select(out=at, in_=at, compare_op=ALU.not_equal, fill=1.0, base=-row,
                                            pattern=[[-1, cols]], channel_multiplier=1))
            pool.sem_inc(cst, 1)
            for dst, sign in ((mask, 1), (maskT, -1)):
                step(pool.memset(mask_f[:], 0.0))
                step(pool.affine_select(out=mask_f[:], in_=mask_f[:], compare_op=ALU.is_ge, fill=MASKED, base=0,
                                        pattern=[[-sign, P]], channel_multiplier=sign))
                step(pool.tensor_copy(dst[:], mask_f[:]))
            pool.tensor_copy(ident_r[:], ident[:]).then_inc(cst, 1)
            pool.wait_ge(st_r, 1)
            step(rstd_steps(pool, sm1[:], mv, 1.0, LN_EPS, half[:], rstd[:], nmr[:], step))
            step(pool.tensor_tensor(sm1[:], rstd[:], rstd[:], ALU.mult))
            step(pool.tensor_tensor(sm1[:], sm1[:], mv[:, :, 1], ALU.mult))
            step(pool.tensor_scalar(sm1[:], sm1[:], 1.0, KV_EPS, ALU.mult, ALU.add))
            step(pool.tensor_tensor(sm1[:], sm1[:], half[:], ALU.pow))
            step(pool.tensor_tensor(n_sc[:], rstd[:], sm1[:], ALU.mult))
            step(pool.tensor_tensor(n_bi[:], nmr[:], sm1[:], ALU.mult))
            step(pool.tensor_scalar(r_sc[:], rstd[:], tg[:, 3:4], 1.0, ALU.mult, ALU.add))
            pool.tensor_scalar(r_bi[:], nmr[:], tg[:, 3:4], 0.0, ALU.mult, ALU.add).then_inc(ln_r, 1)
            pool.wait_ge(wqk_h, 1)
            pool.tensor_tensor(wq_lo[:], raw[:, 0], wq_hi[:].bitcast(F32), ALU.subtract)
            pool.tensor_tensor(wk_lo[:], raw[:, 1], wk_hi[:].bitcast(F32), ALU.subtract).then_inc(wqk_l, 1)

            def values(G, oc):
                one = ones[:, 0:R * RK].rearrange("p (r k) -> p r k", r=R)
                of, par = (oc + 1) % GB, (oc + 1) % 2
                if of == 0:
                    at_least(pool, u_r, G + 1 + R)
                at_least(pool, o_p, US * G + O_LEAD)
                for part in range(2):
                    for j in range(GH):
                        own = U[:, :, of * GH + j, :]
                        hi = V[:, par, :, j, UC * (j % 2):UC * (j % 2) + RK]
                        lo = V[:, par, :, j, UC * (j % 2) + OC:UC * (j % 2) + UC]
                        if part == 0:
                            last = pool.tensor_tensor(hi, own, one, ALU.mult)
                        else:
                            last = pool.tensor_tensor(lo, own, hi.bitcast(F32), ALU.subtract)
                    last.then_inc((v_h, v_r)[part], 1)
                    if part == 0:
                        at_least(pool, v_h, G + 2)

            def group(G, oc, project, maxima, probs):
                if maxima:
                    values(G, oc)
            run(pool, group)

        @block.tensor
        def _(pe):
            pe.sem_inc(st_p, ST_LEAD)
            pe.sem_inc(o_p, O_LEAD)
            pe.sem_inc(sl_p, SL_LEAD)
            pe.wait_ge(w_in, 48)
            for m in range(DC):
                for c in range(DC):
                    last = pe.matmul(bank[:, 2, m * RK:(m + 1) * RK], raw[:, 0, c, m * P:(m + 1) * P], A[:, c, :],
                                     start=c == 0, stop=c == DC - 1)
            last.then_inc(woa_p, 1)
            pe.wait_ge(v_in, 16)
            pe.wait_ge(woa_r, 1)
            for d in range(DC):
                for m in range(DC):
                    last = pe.matmul(bank[:, 3 + d, m * GH * RK:(m + 1) * GH * RK], raw[:, 1, m, d * P:(d + 1) * P],
                                     woa[:, m], start=True, stop=True)
                last.then_inc(wu_p, 1)
            pe.wait_ge(wu_l, DC)
            pe.wait_ge(wqk_l, 1)
            pe.wait_ge(cst, 4)

            def turn_x(G, c):
                at_least(pe, n_r, G + 2 + R)
                at_least(pe, *((m_l, 2 * G + 1), (m_l, 2 * G + 2), (xt_l, G + 3), (xt_l, G + 4))[c])
                for r in range(R):
                    last = pe.transpose(bank[:, BANK[f"x{c}"], r * P:(r + 1) * P], xn[:, r, c * P:(c + 1) * P], ident[:])
                last.then_inc(xt_p, 1)

            def project(G, oc, which, part, parts):
                heads = (oc + 2) % GB
                if part == 0 and which == "q":
                    if oc == 2:
                        at_least(pe, xt_l, G + 2 + DC)
                    elif oc == 3:
                        at_least(pe, u_r, G + 1 + R)
                    else:
                        at_least(pe, m_l, 2 * G + 1)
                if part == 0 and which == "k" and oc != 2:
                    at_least(pe, m_l, 2 * G + 2)
                w_h, w_l = (wq_hi, wq_lo) if which == "q" else (wk_hi, wk_lo)
                passes = [(w, a, c) for c in range(DC) for w, a in ((w_h, xT_hi), (w_h, xT_lo), (w_l, xT_hi))]
                for n in range(part * 12 // parts, (part + 1) * 12 // parts):
                    w, a, c = passes[n]
                    last = pe.matmul(bank[:, BANK[which], :], w[:, c, heads * P:(heads + 1) * P], a[:, c, :],
                                     start=n == 0, stop=n == 11)
                if part == parts - 1:
                    last.then_inc(q_p if which == "q" else k_p, 1)

            def project_values(G, r):
                if r == 0:
                    at_least(pe, k_l, G + 3)
                if r == 2:
                    at_least(pe, m_l, 2 * G + 3)
                for n, (a, w, c) in enumerate([(a, w, c) for c in range(DC)
                                               for a, w in ((xT_hi, wu_hi), (xT_hi, wu_lo), (xT_lo, wu_hi))]):
                    last = pe.matmul(bank[:, BANK[f"u{r // 2}"], r % 2 * 256:(r % 2 + 1) * 256],
                                     a[:, c, r * P:(r + 1) * P], w[:, c, :], start=n == 0, stop=n == 11)
                last.then_inc(u_p, 1)

            def scores(G, oc, s):
                h, qt = s // R, s % R
                keys, par = (qt + 1) * P, (oc + 1) % 2
                if qt == 0:
                    at_least(pe, qk_in[h], 96 * (G + 2))
                at_least(pe, mx_r, US * (G + 1) + s - 1)
                pe.matmul(bank[:, 2 + s % 2, 0:keys], Q[0:KQ, par, h, qt * P:keys], K[0:KQ, par, h, 0:keys],
                          start=True, stop=False)
                pe.matmul(bank[:, 2 + s % 2, qt * P:keys], ident_r[:], mask[:], start=False, stop=True).then_inc(s_p, 1)

            def turn_max(group, hf, last_use):
                at_least(pe, *last_use)
                at_least(pe, mx_r, US * group + US // 2 * (hf + 1))
                pe.transpose(bank[0:US // 2, BANK[f"m{hf}"], 0:P], mx[:, hf, :], ident[:]).then_inc(mt_p, 1)

            def scores_T(G, oc, s):
                h, k = s // R, s % R
                par, at = oc % 2, slice(k * P, (k + 1) * P)
                if s % (US // 2) == 0:
                    at_least(pe, m_in[s // (US // 2)], 32 * (G + 1) + M_LEAD)
                at_least(pe, ex_r, US * G + s - 1 + EX_LEAD)
                pe.matmul(bank[:, 4 + s % 2, k * P:], K[:, par, h, at], Q[:, par, h, k * P:], start=True, stop=False)
                pe.matmul(bank[:, 4 + s % 2, at], ident_r[:], maskT[:], start=False, stop=True).then_inc(st_p, 1)

            def product(G, oc, s):
                h, k = s // R, s % R
                hf, of = s // (US // 2), s % (US // 2)
                if s == 0:
                    at_least(pe, v_r, G + 1)
                if of == 0:
                    at_least(pe, o_r, 2 * (G - 1) + hf + 1 + OR_LEAD)
                at_least(pe, pl_r, US * G + s + 1 + PL_LEAD)
                for n, part in enumerate((p_hi, p_lo)):
                    last = pe.matmul(bank[0:2 * UC, 6 + hf, k * P:], V[:, oc % 2, k, h, :], part[:, s % 4, k * P:],
                                     start=of == 0 and n == 0, stop=of == US // 2 - 1 and n == 1)
                last.then_inc(o_p, 1)

            def turn_out(G, hf):
                at_least(pe, ot_r, 2 * G + hf + 1)
                for r in range(R):
                    last = pe.matmul(bank[:, 6 + hf, r * 2 * OC:(r + 1) * 2 * OC], oT[:, hf, r * P:(r + 1) * P], sel[:],
                                     start=True, stop=True)
                last.then_inc(sl_p, 1)

            def step(G, oc, project_, maxima, probs):
                for s in range(US + (TAIL if probs and oc == 3 else 0)):
                    if maxima and s < US:
                        scores(G, oc, s)
                    if probs and s < US:
                        scores_T(G, oc, s)
                    if probs and late(G, oc, s, 3):
                        product(*late(G, oc, s, 3))
                    if probs and late(G, oc, s, 14) and late(G, oc, s, 14)[2] % (US // 2) == 0:
                        group, _, of = late(G, oc, s, 14)
                        turn_out(group, of // (US // 2))
                    if probs and s == 1:
                        turn_max(G, 1, (k_l, G + 2) if oc != 3 else (u_r, G + 3) if project_ else (m_l, 2 * G))
                    if project_:
                        start = 4 if oc == 2 else 1
                        if oc == 2 and s < 4:
                            turn_x(G, s)
                        if start <= s < start + 4:
                            project(G, oc, "q", s - start, 4)
                        elif start + 4 <= s < start + 8:
                            project(G, oc, "k", s - start - 4, 4)
                    if maxima and s == (12 if project_ and oc == 2 else 10):
                        turn_max(G + 1, 0, (q_l, G + 3) if project_ else (m_l, 2 * G + 1))
                    if project_ and oc == 2 and 12 <= s < US:
                        project_values(G, s - 12)
            run(pe, step)

        @block.scalar
        def _(act):
            act.sem_inc(ex_r, EX_LEAD)
            for d in range(DC):
                act.wait_ge(wu_p, d + 1)
                act.activation(wu_hi[:, d, :], bank[:, 3 + d, 0:HEADS * RK], ACT.Copy).then_inc(wu_h, 1)
            act.wait_ge(q_in, 32)
            act.activation(wq_hi[:], raw[:, 0], ACT.Copy)
            act.activation(wk_hi[:], raw[:, 1], ACT.Copy).then_inc(wqk_h, 1)
            act.wait_ge(w_in, 48)

            def normalise(b):
                at_least(act, xt_p, DC * b)
                act.wait_ge(ln_r, 1)
                for r in range(R):
                    act.activation(xn[:, r, :], x[:, bass.ds(R * b + r, 1), :].rearrange("p o d -> p (o d)"),
                                   ACT.Identity, bias=n_bi[:, bass.ds(R * b + r, 1)],
                                   scale=n_sc[:, bass.ds(R * b + r, 1)]).then_inc(n_r, 1)

            def x_hi(G, oc, c):
                at_least(act, xt_p, G + 2 + c + 1)
                if c == 0:
                    at_least(act, k_p, G + 2)
                act.activation(xT_hi[:, c, :], bank[:, BANK[f"x{c}"], :], ACT.Copy,
                               scale=ln1[:, c:c + 1]).then_inc(xt_h, 1)

            def qk_hi(G, oc, which):
                done, dst, ready = (q_p, q_hi, q_h) if which == "q" else (k_p, k_hi, k_h)
                for j in range(GH):
                    at_least(act, qk_in[j], 96 * (G + 2))
                at_least(act, done, G + 3)
                act.activation(dst[:], bank[:, BANK[which], :], ACT.Copy).then_inc(ready, 1)

            def u_copy(G, hf):
                if hf == 0:
                    at_least(act, v_r, G + 2)
                at_least(act, u_p, G + 4 + 2 * hf)
                act.activation(U[:, 2 * hf:2 * hf + 2].rearrange("p r h k -> p (r h k)"), bank[:, BANK[f"u{hf}"], :],
                               ACT.Copy).then_inc(u_r, 2)

            def max_hi(group, hf):
                at_least(act, m_in[hf], 32 * group + M_LEAD)
                at_least(act, mt_p, 2 * group + hf + 1)
                act.activation(m_hi[:, hf, :], bank[0:US // 2, BANK[f"m{hf}"], 0:P], ACT.Copy, scale=-1.0)\
                   .then_inc(m_h, 1)

            def probs_T(G, oc, s):
                k = s % R
                at_least(act, o_p, US * G + s - 3 + O_LEAD)
                at_least(act, st_p, US * G + s + 1 + ST_LEAD)
                act.activation(p_hi[:, s % 4, k * P:], bank[:, 4 + s % 2, k * P:], ACT.Exp, scale=ATT_SCALE)
                act.activation(pT[:, s % 4, k * P:], bank[:, 4 + s % 2, k * P:], ACT.Exp, scale=ATT_SCALE)\
                   .then_inc(ex_r, 1)

            def out_copy(G, hf):
                at_least(act, sl_p, 2 * (G - 1) + hf + 1 + SL_LEAD)
                at_least(act, o_p, US * G + US // 2 * (hf + 1) + O_LEAD)
                act.activation(oT[:, hf, :], bank[0:2 * UC, 6 + hf, :], ACT.Copy).then_inc(ot_r, 1)

            def step(G, oc, project_, maxima, probs):
                after = 3 if oc == 2 else 0
                for s in range(US + (TAIL if probs and oc == 3 else 0)):
                    if probs and s < US:
                        probs_T(G, oc, s)
                    if probs and late(G, oc, s, 12) and late(G, oc, s, 12)[2] % (US // 2) == 0:
                        group, _, of = late(G, oc, s, 12)
                        out_copy(group, of // (US // 2))
                    if probs and s == 1:
                        max_hi(G, 1)
                    if project_:
                        if oc == 2 and s < 4:
                            x_hi(G, oc, s)
                        if s == 5 + after:
                            qk_hi(G, oc, "q")
                        if s == 9 + after:
                            qk_hi(G, oc, "k")
                    if maxima and s == (12 if project_ and oc == 2 else 10):
                        max_hi(G + 1, 0)
                    if oc == 1 and s == 13 and not isinstance(G, int):
                        normalise(turn[0] + 1)
                    if project_ and oc == 2 and s in (14, 15):
                        u_copy(G, s - 14)

            normalise(0)
            turn = [0]
            batch = each_step(step)
            with act.Fori(0, B - 1) as b:
                turn[0] = b
                batch(b, False)
            batch(B - 1, True)

        @block.vector
        def _(dve):
            dve.sem_inc(o_r, OR_LEAD)
            dve.sem_inc(pl_r, PL_LEAD)
            step_ = linked(dve, g["vector_chain"])
            for t in range(T):
                last = dve.bn_stats(stats[:, t, :], x[:, t, :])
            step_(last)
            for t in range(T):
                last = dve.bn_aggr(mv[:, t, :], stats[:, t, :])
            last.then_inc(st_r, 1)
            dve.wait_ge(woa_p, 1)
            dve.wait_ge(cst, 1)
            for j in range(GH):
                rows = slice(j * HD, (j + 1) * HD)
                last = dve.tensor_copy(woa[rows, :, j, :], bank[rows, 2, 0:DC * RK].rearrange("p (m r) -> p m r", r=RK))
            last.then_inc(woa_r, 1)
            for d in range(DC):
                dve.wait_ge(wu_h, d + 1)
                dve.tensor_tensor(wu_lo[:, d, :], bank[:, 3 + d, 0:HEADS * RK], wu_hi[:, d, :].bitcast(F32),
                                  ALU.subtract).then_inc(wu_l, 1)
            dve.wait_ge(w_in, 48)

            def x_lo(G, oc, c):
                at_least(dve, xt_h, G + 2 + c + 1)
                dve.scalar_tensor_tensor(xT_lo[:, c, :], bank[:, BANK[f"x{c}"], :], ln1[:, c:c + 1],
                                         xT_hi[:, c, :].bitcast(F32), ALU.mult, ALU.subtract).then_inc(xt_l, 1)

            def qk_lo(G, oc, which):
                ready, hi, lo, done = (q_h, q_hi, q_lo, q_l) if which == "q" else (k_h, k_hi, k_lo, k_l)
                at_least(dve, ready, G + 3)
                dve.tensor_tensor(lo[:], bank[:, BANK[which], :], hi[:].bitcast(F32), ALU.subtract)\
                   .then_inc(done, 1)

            def max_lo(group, hf):
                at_least(dve, m_h, 2 * group + hf + 1)
                dve.scalar_tensor_tensor(m_lo[:, hf, :], bank[0:US // 2, BANK[f"m{hf}"], 0:P], -1.0,
                                         m_hi[:, hf, :].bitcast(F32), ALU.mult, ALU.subtract).then_inc(m_l, 1)

            def maximum(G, oc, s):
                hf, at, keys = s // (US // 2), s % (US // 2), (s % R + 1) * P
                if at == 0:
                    at_least(dve, mt_p, 2 * (G + 1) + hf - 1)
                at_least(dve, s_p, US * (G + 1) + s + 1)
                dve.reduce_max(mx[:, hf, at:at + 1], bank[:, 2 + s % 2, 0:keys], AX).then_inc(mx_r, 1)

            def probs_lo(G, s):
                k = s % R
                at_least(dve, ex_r, US * G + s + 1 + EX_LEAD)
                dve.tensor_tensor(p_lo[:, s % 4, k * P:], pT[:, s % 4, k * P:], p_hi[:, s % 4, k * P:].bitcast(F32),
                                  ALU.subtract).then_inc(pl_r, 1)

            def finish(G, hf):
                link = chained(dve, och, 8 * G + 4 * hf)
                at_least(dve, sl_p, 2 * G + hf + 1 + SL_LEAD)
                out = bank[:, 6 + hf, 0:R * 2 * OC].rearrange("p (r h c) -> p r h c", r=R, h=2)
                link(dve.reciprocal(rto[:], out[:, :, :, RK]))
                link(dve.tensor_tensor(ou[:], out[:, :, :, 0:RK], rto[:].unsqueeze(3).broadcast_to([P, R, 2, RK]),
                                       ALU.mult))
                dve.sem_inc(o_r, 1)
                link(dve.tensor_tensor(red[:], ou[:, :, 0, :], ou[:, :, 1, :], ALU.add))
                own = mod[:, bass.ds(R * now[0], R), :]
                link(dve.tensor_tensor(own, own, red[:], ALU.add))

            def step(G, oc, project_, maxima, probs):
                after = 3 if oc == 2 else 0
                for s in range(US + (TAIL if probs and oc == 3 else 0)):
                    if maxima and s < US:
                        maximum(G, oc, s)
                    if probs and late(G, oc, s, 2):
                        group, _, of = late(G, oc, s, 2)
                        probs_lo(group, of)
                    if probs and late(G, oc, s, 15) and late(G, oc, s, 15)[2] % (US // 2) == 0:
                        group, _, of = late(G, oc, s, 15)
                        finish(group, of // (US // 2))
                    if probs and s == 1:
                        max_lo(G, 1)
                    if project_:
                        if oc == 2 and s < 4:
                            x_lo(G, oc, s)
                        if s == 5 + after:
                            qk_lo(G, oc, "q")
                        if s == 9 + after:
                            qk_lo(G, oc, "k")
                    if maxima and s == (12 if project_ and oc == 2 else 10):
                        max_lo(G + 1, 0)

            now = [0]
            batch = each_step(step)
            with dve.Fori(0, B - 1) as b:
                now[0] = b
                batch(b, False)
            now[0] = B - 1
            batch(B - 1, True)


def phase_mlp(nc, s_, sem, g):
    x, bank, ident, tg = g["x"], g["bank"], g["ident"], g["tg"]
    n_sc, n_bi, r_sc, r_bi, mod = g["n_sc"], g["n_bi"], g["r_sc"], g["r_bi"], g["mod"]
    xT_hi = s_("ml_xT_hi", [P, DC, B * N], F32R)
    xT_lo = s_("ml_xT_lo", [P, DC, B * N], F32R)
    b_stack = s_("ml_b_stack", [96, F_], F32R)
    m_stack = s_("ml_m_stack", [96, B * N], F32R)
    with ExitStack() as inner:
        def i_(name, shape, dt=F32):
            return inner.enter_context(nc.sbuf_tensor(name, shape, dt))
        xn = i_("ml_n", [P, R, D])
        ln2 = i_("ml_ln2", [P, DC])
        A = i_("ml_A", [P, DC, RK])
        A_hi = i_("ml_A_hi", [P, DC, RK], F32R)
        A_lo = i_("ml_A_lo", [P, DC, RK], F32R)
        b_raw = i_("ml_b_raw", [96, F_])
        m_rows = i_("ml_m_rows", [P, T, 3, 32])
        m_hi = i_("ml_m_hi", [96, 512], F32R)

        w_in = sem("ml_small_arrived")
        b_0 = sem("ml_rows_cleared")
        b_in = sem("ml_b_arrived")
        a_h = sem("ml_A_hi_ready")
        a_l = sem("ml_A_lo_ready")
        bst_h = sem("ml_b_hi_ready")
        bst_r = sem("ml_b_stack_ready")
        n_r = sem("ml_n_ready")
        xt_p = sem("ml_xT_transposed")
        xt_h = sem("ml_xT_hi_ready")
        xt_l = sem("ml_xT_lo_ready")
        th_r = sem("ml_tanh_ready")
        ha_p = sem("ml_hA_done")
        m_r = sem("ml_m_ready")
        mt_p = sem("ml_mT_done")
        mh_r = sem("ml_m_hi_ready")
        ms_r = sem("ml_m_stack_ready")

        with nc.Block() as block:
            @block.sync
            def _(sp):
                sp.dma_start(ln2[:], g["ln2_w"]).then_inc(w_in, 16)
                sp.dma_start(A[:], g["A_in"].rearrange("(c p) r -> p c r", p=P)).then_inc(w_in, 16)
                sp.wait_ge(b_0, 1)
                for k in range(3):
                    sp.dma_start(b_raw[32 * k:32 * k + RK, :], g["B_in"]).then_inc(b_in, 16)

            @block.gpsimd
            def _(pool):
                pool.memset(b_raw[:], 0.0).then_inc(b_0, 1)
                pool.memset(m_rows[:], 0.0).then_inc(b_0, 1)
                pool.wait_ge(a_h, 1)
                pool.tensor_tensor(A_lo[:], A[:], A_hi[:].bitcast(F32), ALU.subtract).then_inc(a_l, 1)

            @block.scalar
            def _(act):
                act.activation(mod[:], mod[:], ACT.Tanh).then_inc(th_r, 1)
                act.wait_ge(w_in, 32)
                act.activation(A_hi[:], A[:], ACT.Copy).then_inc(a_h, 1)
                act.wait_ge(b_in, 48)
                act.activation(b_stack[:], b_raw[:], ACT.Copy).then_inc(bst_h, 1)
                for b in range(B):
                    if b >= 1:
                        act.wait_ge(xt_p, DC * b)
                    for r in range(R):
                        t = R * b + r
                        act.activation(xn[:, r, :], x[:, t, :], ACT.Identity, bias=n_bi[:, t:t + 1],
                                       scale=n_sc[:, t:t + 1]).then_inc(n_r, 1)
                        act.wait_ge(n_r, t + 1)
                        act.activation(x[:, t, :], x[:, t, :], ACT.Identity, bias=r_bi[:, t:t + 1],
                                       scale=r_sc[:, t:t + 1])
                    for c in range(DC):
                        act.wait_ge(xt_p, DC * b + c + 1)
                        act.activation(xT_hi[:, c, b * N:(b + 1) * N], bank[:, c, :], ACT.Copy,
                                       scale=ln2[:, c:c + 1]).then_inc(xt_h, 1)
                for b in range(B):
                    act.wait_ge(mt_p, b + 1)
                    if b >= 1:
                        act.wait_ge(ms_r, b)
                    act.activation(m_hi[:], bank[0:96, 5 + b % 2, :], ACT.Copy).then_inc(mh_r, 1)

            @block.tensor
            def _(pe):
                for b in range(B):
                    pe.wait_ge(n_r, R * b + R)
                    for c in range(DC):
                        if b >= 1:
                            pe.wait_ge(xt_l, DC * b + c - 3)
                        for r in range(R):
                            last = pe.transpose(bank[:, c, r * P:(r + 1) * P], xn[:, r, c * P:(c + 1) * P], ident[:])
                        last.then_inc(xt_p, 1)
                    if b == 0:
                        pe.wait_ge(a_l, 1)
                    pe.wait_ge(xt_l, DC * b + DC)
                    for r in range(R):
                        t = R * b + r
                        at = slice(t * P, (t + 1) * P)
                        passes = [(a, w, c) for c in range(DC) for a, w in ((xT_hi, A_hi), (xT_hi, A_lo), (xT_lo, A_hi))]
                        for q, (a, w, c) in enumerate(passes):
                            last = pe.matmul(bank[:, 4, t * RK:(t + 1) * RK], a[:, c, at], w[:, c, :], start=q == 0,
                                             stop=q == len(passes) - 1)
                    last.then_inc(ha_p, 1)
                pe.wait_ge(m_r, 1)
                for b in range(B):
                    if b >= 2:
                        pe.wait_ge(ms_r, b - 1)
                    for r in range(R):
                        last = pe.transpose(bank[0:96, 5 + b % 2, r * P:(r + 1) * P],
                                            m_rows[:, R * b + r].rearrange("p k m -> p (k m)"), ident[:])
                    last.then_inc(mt_p, 1)

            @block.vector
            def _(dve):
                step = linked(dve, g["vector_chain"])
                dve.wait_ge(w_in, 32)
                dve.wait_ge(bst_h, 1)
                dve.tensor_tensor(b_stack[32:64, :], b_raw[32:64, :], b_stack[32:64, :].bitcast(F32), ALU.subtract)\
                   .then_inc(bst_r, 1)
                for b in range(B):
                    for c in range(DC):
                        dve.wait_ge(xt_h, DC * b + c + 1)
                        at = slice(b * N, (b + 1) * N)
                        dve.scalar_tensor_tensor(xT_lo[:, c, at], bank[:, c, :], ln2[:, c:c + 1],
                                                 xT_hi[:, c, at].bitcast(F32), ALU.mult, ALU.subtract).then_inc(xt_l, 1)
                dve.wait_ge(th_r, 1)
                dve.wait_ge(ha_p, B)
                dve.wait_ge(b_0, 2)
                step(dve.scalar_tensor_tensor(m_rows[:, :, 0, 0:RK], mod[:], MOD_SCALE,
                                              bank[:, 4, 0:T * RK].rearrange("p (t r) -> p t r", r=RK),
                                              ALU.mult, ALU.mult))
                dve.tensor_copy(m_rows[:, :, 1, 0:RK], m_rows[:, :, 0, 0:RK])
                dve.tensor_copy(m_rows[:, :, 2, 0:RK], m_rows[:, :, 0, 0:RK]).then_inc(m_r, 1)
                for b in range(B):
                    dve.wait_ge(mh_r, b + 1)
                    at = slice(b * 512, (b + 1) * 512)
                    dve.tensor_copy(m_stack[0:64, at], m_hi[0:64, :].bitcast(F32))
                    dve.tensor_tensor(m_stack[64:96, at], bank[64:96, 5 + b % 2, :], m_hi[64:96, :].bitcast(F32),
                                      ALU.subtract).then_inc(ms_r, 1)

    def source(u, p, loop):
        at = bass.ds(u * UH, UH)
        return (g["W_inT"][:, at].rearrange("(c p) h -> p c h", p=P),
                g["W_upT"][:, at].rearrange("(c p) h -> p c h", p=P),
                g["W_downT"][at, :].rearrange("(k p) d -> p k d", p=P))

    gated_units(nc, s_, sem, "ml", x, bank, xT_hi, xT_lo, MLP_UNITS, source, gate=tg[:, 3:4], mod=(b_stack, m_stack))


def layout(inputs):
    import numpy as np
    a = {k: np.asarray(v) for k, v in inputs.items()}
    c = np.ascontiguousarray
    return {
        "x_in": a["x"], "ctxT_in": c(a["ctx_512"].reshape(B * N, C).T),
        "g_xattn": a["g_xattn"], "g_ffn": a["g_ffn"],
        "gr_Wq": a["L0_xattn_Wq"], "gr_Wk": a["L0_xattn_Wk"], "gr_gamma": a["L0_xattn_gamma_raw"].reshape(1),
        "router_w": a["L0_ffn_router_w"], "w_gate": a["L0_ffn_w_gate"], "w_up": a["L0_ffn_w_up"],
        "w_down": a["L0_ffn_w_down"], "sw_gate": a["L0_ffn_sw_gate"], "sw_up": a["L0_ffn_sw_up"],
        "sw_down": a["L0_ffn_sw_down"],
        "WkT": c(a["L1_xattn_W_k"].T), "b_k": a["L1_xattn_b_k"], "ln_gamma": a["L1_xattn_ln_gamma"],
        "ln_beta": a["L1_xattn_ln_beta"], "ln1_w": c(a["L1_ffn_ln1_w"].reshape(DC, P).T), "ln2_w": c(a["L1_ffn_ln2_w"].reshape(DC, P).T),
        "WqT": c(a["L1_ffn_Wq"].T), "WkT1": c(a["L1_ffn_Wk"].T), "Wv": a["L1_ffn_Wv"], "Wo": a["L1_ffn_Wo"],
        "A_in": a["L1_ffn_A"], "B_in": a["L1_ffn_B"], "W_inT": c(a["L1_ffn_W_in_base"].T),
        "W_upT": c(a["L1_ffn_W_up_base"].T), "W_downT": c(a["L1_ffn_W_down"].T),
    }


def kernel(**inputs):
    import numpy as _np
    import concourse.bacc as _bacc
    from concourse import mybir as _mybir
    from concourse.bass_utils import run_bass_kernel_spmd as _run

    nc = _bacc.Bacc("TRN2", target_bir_lowering=False, num_devices=1)
    arrays, args = {}, []
    for name, a in layout(inputs).items():
        arrays[f"in_{name}"] = _np.ascontiguousarray(a)
        args.append(nc.dram_tensor(f"in_{name}", a.shape, _mybir.dt.from_np(a.dtype), kind="ExternalInput").ap())
    out = nc.dram_tensor("out_0", (B, N, D), _mybir.dt.float32, kind="ExternalOutput").ap()
    flamingo_kernel(nc, *args, out)
    r = _run(nc, [arrays], core_ids=[0])
    return r.results[0]["out_0"]
```

```python
from contextlib import ExitStack

import concourse.bass as bass
from concourse import mybir

P = 128
F32 = mybir.dt.float32
F32R = mybir.dt.float32r
BF16 = mybir.dt.bfloat16
U32 = mybir.dt.uint32
I32 = mybir.dt.int32
ALU = mybir.AluOpType
ACT = mybir.ActivationFunctionType
AX = mybir.AxisListType.X

B, N, D = 4, 512, 512
C = 128
T = B * N // P
R = N // P
DC = D // P
LN_EPS = 1e-5

GRAPH_HEADS = 4
GRAPH_SCALE = 1.0 / ((C // GRAPH_HEADS) ** 0.5 * GRAPH_HEADS)
TOP = int(N * 0.3)
HALVINGS = 24
MEAN_TO_LOW = (N / (N - TOP + 1) - 1) ** 0.5
MEAN_TO_HIGH = (N / TOP - 1) ** 0.5
SEARCH = ((slice(0, 4), slice(4, 8)), (slice(8, 12), slice(12, 16)))

E_ = 8
UH = 256
HC = UH // P
MOE_UNITS = E_ + 2
KV_EPS = 1e-6
KV_SCALE = N ** -0.5
HEADS = 16
HD = D // HEADS
RK = 16
F_ = 2048
MLP_UNITS = F_ // UH
ATT_SCALE = 1.0 / HD ** 0.5
MOD_SCALE = 0.1
MASKED = -1e30
TB = B * N // 512

GU_LEAD = 2
Y_LEAD = 32
ACC_LEAD = 16


class Count:
    def __init__(self, sem):
        self.sem, self.value = sem, 0


def linked(eng, count):
    def step(ins):
        count.value += 1
        ins.then_inc(count.sem, 1)
        eng.wait_ge(count.sem, count.value)
    return step


def flamingo_kernel(nc, x_in, ctxT_in, g_xattn, g_ffn, gr_Wq, gr_Wk, gr_gamma, router_w, w_gate, w_up,
                    w_down, sw_gate, sw_up, sw_down, WkT, b_k, ln_gamma, ln_beta, ln1_w, ln2_w, WqT,
                    WkT1, Wv, Wo, A_in, B_in, W_inT, W_upT, W_downT, out):
    with ExitStack() as ctx:
        def sb(name, shape, dt=F32, scope=ctx):
            return scope.enter_context(nc.sbuf_tensor(name, shape, dt))

        def sem(name):
            return ctx.enter_context(nc.semaphore(name))

        bank = ctx.enter_context(nc.psum_tensor("bank", [P, 8, 512], F32))
        x = sb("x", [P, T, D])
        ident = sb("ident", [P, P])
        gates = sb("gates", [P, 8])
        tg = sb("tg", [P, 4])
        gam = sb("gam", [P, 1])
        stats = sb("stats", [P, T, 6])
        mv = sb("mv", [P, T, 2])
        half = sb("half", [P, T])
        rstd = sb("rstd", [P, T])
        nmr = sb("nmr", [P, T])
        sm1 = sb("sm1", [P, T])
        x_dram = x_in.rearrange("b (r p) d -> p (b r) d", p=P)
        out_dram = out.rearrange("b (r p) d -> p (b r) d", p=P)

        vector_chain, pool_chain = Count(sem("vector_chain")), Count(sem("pool_chain"))
        n_sc = sb("n_scale", [P, T])
        n_bi = sb("n_bias", [P, T])
        mod = sb("mod", [P, T, RK])
        r_sc = sb("r_scale", [P, T])
        r_bi = sb("r_bias", [P, T])
        early = sb("early", [P, B * N + 2 * N])
        ctxT = early[:, 0:B * N].rearrange("p (b n) -> p b n", b=B)
        kv_gamma, kv_beta = early[:, B * N:B * N + N], early[:, B * N + N:B * N + 2 * N]
        third_raw = (early[:, 0:DC * UH].rearrange("p (c h) -> p c h", c=DC),
                     early[:, DC * UH:2 * DC * UH].rearrange("p (c h) -> p c h", c=DC),
                     early[:, 2 * DC * UH:2 * DC * UH + HC * D].rearrange("p (k d) -> p k d", k=HC))
        kv_wk = sb("kv_wk", [C, C])
        kv_bk = sb("kv_bk", [C, 1])
        rw = sb("moe_rw", [P, DC, E_])
        kv_in, rw_in, first_w = sem("kv_weights_arrived"), sem("moe_router_arrived"), sem("moe_first_unit_arrived")
        third_w = sem("ml_w_arrived")
        with ExitStack() as first:
            first_raw = raw_unit(lambda n, s: sb(n, s, F32, first)[:], "moe")
            phase_graph(nc, sb, sem, locals())
            phase_moe(nc, sb, sem, locals())
        with ExitStack() as second:
            att = AttentionOperands(lambda n, s, d=F32: sb(n, s, d, second), sem, locals())
            phase_kv(nc, sb, sem, locals())
            phase_attention(nc, lambda n, s, d=F32: sb(n, s, d, second), sem, locals())
        with ExitStack() as third:
            phase_mlp(nc, lambda n, s, d=F32: sb(n, s, d, third), sem, locals())


def rstd_steps(pool, v, mv_, scale, eps, half, rstd, nmr, step):
    step(pool.tensor_scalar(v, mv_[:, :, 1], scale, eps, ALU.mult, ALU.add))
    step(pool.tensor_tensor(rstd, v, half, ALU.pow))
    step(pool.tensor_tensor(nmr, mv_[:, :, 0], rstd, ALU.mult))
    return pool.tensor_scalar(nmr, nmr, -1.0, None, ALU.mult)


def raw_unit(alloc, tag):
    return alloc(tag + "_raw_g", [P, DC, UH]), alloc(tag + "_raw_u", [P, DC, UH]), alloc(tag + "_raw_d", [P, HC, D])


def expert(g, u):
    return (g["w_gate"][u].rearrange("(c p) h -> p c h", p=P), g["w_up"][u].rearrange("(c p) h -> p c h", p=P),
            g["w_down"][u].rearrange("(k p) d -> p k d", p=P))


def layer_norm_stats(dve, g, t, written, st_r, step):
    dve.wait_ge(*written)
    last = dve.bn_stats(g["stats"][:, t, :], g["x"][:, t, :])
    if t % R == R - 1:
        step(last)
        for q in range(t - R + 1, t + 1):
            last = dve.bn_aggr(g["mv"][:, q, :], g["stats"][:, q, :])
        last.then_inc(st_r, 1)


def layer_norm_scales(pool, g, b, st_r, step):
    own = slice(R * b, R * b + R)
    pool.wait_ge(st_r, b + 1)
    step(rstd_steps(pool, g["sm1"][:, own], g["mv"][:, own, :], 1.0, LN_EPS, g["half"][:, own], g["rstd"][:, own],
                    g["nmr"][:, own], step))


def phase_graph(nc, sb, sem, g):
    x, bank, ident, gates, tg, gam = g["x"], g["bank"], g["ident"], g["gates"], g["tg"], g["gam"]
    stats, mv, half, rstd, nmr, sm1 = g["stats"], g["mv"], g["half"], g["rstd"], g["nmr"], g["sm1"]
    with ExitStack() as scope:
        def s_(name, shape, dt=F32):
            return sb(name, shape, dt, scope)
        S = s_("sim", [P, T, N])
        ctxT = g["ctxT"]
        wq = s_("gr_wq", [C, C])
        wk = s_("gr_wk", [C, C])
        M = s_("gr_M", [C, C])
        Z = s_("gr_Z", [P, B, N])
        sst = s_("sim_stats", [P, T, 6])
        smv = s_("sim_mv", [P, T, 2])
        sg = s_("sig", [P, 4, N])
        tb = s_("tb", [P, 4, N])
        junk = s_("junk", [P, T, N], BF16)
        width = s_("width", [P, 2, T])
        halves = s_("halves", [P, T])
        low = s_("low", [P, T])
        mid = s_("mid", [P, T])
        cnt = s_("cnt", [P, T])
        sel = s_("chosen", [P, T])
        slack = s_("slack", [P, T])
        sigma = s_("sigma", [P, T])
        sc1 = s_("sc1", [P, T])
        bi1 = s_("bi1", [P, T])
        c1 = s_("c1", [P, 1])
        c2 = s_("c2", [P, 1])

        x_in_s = [sem(f"gr_x_arrived{b}") for b in range(B)]
        w_in = sem("gr_weights_arrived")
        c_in = sem("gr_ctx_arrived")
        g_in = sem("gr_gates_arrived")
        m_ps = sem("gr_M_done")
        m_sb = sem("gr_M_copied")
        z_ps = sem("gr_Z_done")
        z_sb = sem("gr_Z_copied")
        s_ps = sem("gr_sim_done")
        s_sb = sem("gr_sim_copied")
        cst = sem("gr_constants")
        lnst = sem("gr_ln_stats")
        sim_st = sem("gr_sim_stats")
        mid_r = [sem(f"gr_mid_ready{h}") for h in range(2)]
        cnt_v = sem("gr_values_counted")
        cnt_s = sem("gr_signs_counted")
        sch = sem("gr_search_chain")
        gat = sem("gr_gates_ready")
        coef = sem("gr_coefs_ready")
        sig_0 = sem("gr_sigmoid_made")
        sig_r = sem("gr_sigmoid_scaled")
        a_r = sem("gr_A_ready")
        at_r = sem("gr_AT_ready")
        y_r = sem("gr_x_scaled")
        t_r = sem("gr_A_plus_x_ready")
        x_r = sem("gr_x_ready")
        new_st = sem("gr_new_stats_ready")

        with nc.Block() as block:
            @block.sync
            def _(sp):
                sp.dma_start(wq[:], g["gr_Wq"]).then_inc(w_in, 16)
                sp.dma_start(wk[:], g["gr_Wk"]).then_inc(w_in, 16)
                sp.dma_start(ctxT, g["ctxT_in"].rearrange("c (b n) -> c b n", b=B)).then_inc(c_in, 16)
                for k, (src, n) in enumerate(((g["g_xattn"], 2), (g["g_ffn"], 2), (g["gr_gamma"], 1))):
                    sp.dma_start(gates[:, 2 * k:2 * k + n], src.partition_broadcast(P)).then_inc(g_in, 16)
                for b in range(B):
                    sp.dma_start(x[:, R * b:R * b + R, :], g["x_dram"][:, R * b:R * b + R, :])\
                      .then_inc(x_in_s[b], 16)
                sp.dma_start(g["rw"][:], g["router_w"].rearrange("(c p) e -> p c e", p=P)).then_inc(g["rw_in"], 16)
                for dst, src in zip(g["first_raw"], expert(g, 0)):
                    sp.dma_start(dst, src).then_inc(g["first_w"], 16)
                sp.dma_start(g["kv_wk"][:], g["WkT"]).then_inc(g["kv_in"], 16)
                sp.dma_start(g["kv_bk"][:], g["b_k"].unsqueeze(1)).then_inc(g["kv_in"], 16)
                sp.dma_start(g["kv_gamma"], g["ln_gamma"].partition_broadcast(P)).then_inc(g["kv_in"], 16)
                sp.dma_start(g["kv_beta"], g["ln_beta"].partition_broadcast(P)).then_inc(g["kv_in"], 16)

            @block.tensor
            def _(pe):
                pe.wait_ge(w_in, 32)
                pe.matmul(bank[:, 0, 0:C], wq[:], wk[:], start=True, stop=True).then_inc(m_ps, 1)
                pe.wait_ge(m_sb, 1)
                pe.wait_ge(c_in, 16)
                for b in range(B):
                    if b >= 2:
                        pe.wait_ge(z_sb, b - 1)
                    pe.matmul(bank[:, b % 2, :], M[:], ctxT[:, b, :], start=True, stop=True).then_inc(z_ps, 1)
                    pe.wait_ge(z_sb, b + 1)
                    for r in range(R):
                        t = R * b + r
                        if t >= 6:
                            pe.wait_ge(s_sb, t - 5)
                        pe.matmul(bank[:, 2 + t % 6, :], Z[:, b, r * P:(r + 1) * P], ctxT[:, b, :],
                                  start=True, stop=True).then_inc(s_ps, 1)
                pe.wait_ge(cst, 1)
                for b in range(B):
                    pe.wait_ge(a_r, R * (b + 1))
                    for r in range(R):
                        t = R * b + r
                        if t >= 8:
                            pe.wait_ge(x_r, t - 7)
                        if t == 0:
                            pe.wait_ge(s_sb, T)
                        for q in range(R):
                            last = pe.transpose(bank[:, t % 8, q * P:(q + 1) * P],
                                                S[:, R * b + q, r * P:(r + 1) * P], ident[:])
                        last.then_inc(at_r, 1)

            @block.scalar
            def _(act):
                act.wait_ge(g_in, 48)
                act.activation(tg[:], gates[:, 0:4], ACT.Tanh)
                act.activation(gam[:], gates[:, 4:5], ACT.Sigmoid).then_inc(gat, 1)
                act.wait_ge(m_ps, 1)
                act.activation(M[:], bank[:, 0, 0:C], ACT.Copy).then_inc(m_sb, 1)
                for b in range(B):
                    act.wait_ge(z_ps, b + 1)
                    act.activation(Z[:, b, :], bank[:, b % 2, :], ACT.Copy).then_inc(z_sb, 1)
                    for r in range(R):
                        t = R * b + r
                        act.wait_ge(s_ps, t + 1)
                        act.activation(S[:, t, :], bank[:, 2 + t % 6, :], ACT.Copy).then_inc(s_sb, 1)
                act.wait_ge(coef, 1)
                act.wait_ge(x_in_s[3], 16)
                for t in range(T):
                    act.activation(x[:, t, :], x[:, t, :], ACT.Identity, bias=bi1[:, t:t + 1],
                                   scale=sc1[:, t:t + 1]).then_inc(y_r, 1)
                with act.Fori(0, HALVINGS) as i:
                    for h, (_, own) in enumerate(SEARCH):
                        act.wait_ge(mid_r[h], i + 1)
                        for t in range(own.start, own.stop):
                            last = act.activation(junk[:, t, :], S[:, t, :], ACT.Sign, bias=mid[:, t:t + 1],
                                                  scale=-1.0, accum_out=cnt[:, t:t + 1])
                        last.then_inc(cnt_s, 1)
                for t in range(T + 1):
                    if t < T:
                        if t >= 4:
                            act.wait_ge(a_r, t - 3)
                        act.activation(sg[:, t % 4, :], S[:, t, :], ACT.Sigmoid, scale=GRAPH_SCALE).then_inc(sig_0, 1)
                    if t >= 1:
                        act.wait_ge(sig_0, t)
                        own = sg[:, (t - 1) % 4, :]
                        act.activation(own, own, ACT.Copy, scale=c2[:, 0:1]).then_inc(sig_r, 1)

            @block.gpsimd
            def _(pool):
                step = linked(pool, g["pool_chain"])
                step(pool.memset(ident[:], 0.0))
                step(pool.memset(half[:], -0.5))
                pool.affine_select(out=ident[:], in_=ident[:], compare_op=ALU.not_equal, fill=1.0, base=0,
                                   pattern=[[-1, P]], channel_multiplier=1).then_inc(cst, 1)
                pool.wait_ge(lnst, 1)
                step(rstd_steps(pool, sm1[:], mv, 1.0, LN_EPS, half[:], rstd[:], nmr[:], step))
                pool.wait_ge(gat, 1)
                step(pool.tensor_scalar(c1[:], gam[:], -1.0, 1.0, ALU.mult, ALU.add))
                step(pool.tensor_tensor(c1[:], c1[:], tg[:, 0:1], ALU.mult))
                step(pool.tensor_tensor(c2[:], gam[:], tg[:, 0:1], ALU.mult))
                step(pool.tensor_scalar(c2[:], c2[:], 0.5, None, ALU.mult))
                step(pool.tensor_scalar(sc1[:], rstd[:], c1[:, 0:1], 1.0, ALU.mult, ALU.add))
                pool.tensor_scalar(bi1[:], nmr[:], c1[:, 0:1], 0.0, ALU.mult, ALU.add).then_inc(coef, 1)
                pool.wait_ge(sim_st, 1)
                mean, var = smv[:, :, 0], smv[:, :, 1]
                step(pool.tensor_scalar(half[:], half[:], -1.0, None, ALU.mult))
                step(pool.tensor_tensor(sigma[:], var, half[:], ALU.pow))
                step(pool.tensor_tensor(slack[:], mean, mean, ALU.mult))
                step(pool.tensor_tensor(slack[:], slack[:], var, ALU.add))
                step(pool.tensor_tensor(slack[:], slack[:], half[:], ALU.pow))
                step(pool.tensor_scalar(half[:], half[:], -1.0, None, ALU.mult))
                step(pool.tensor_scalar(slack[:], slack[:], 2.0 ** -18, None, ALU.mult))
                step(pool.tensor_scalar(low[:], sigma[:], -1.02 * MEAN_TO_LOW, None, ALU.mult))
                step(pool.tensor_tensor(low[:], low[:], mean, ALU.add))
                step(pool.tensor_tensor(low[:], low[:], slack[:], ALU.subtract))
                wide = width[:, 0, :]
                step(pool.tensor_scalar(wide, sigma[:], 1.04 * (MEAN_TO_LOW + MEAN_TO_HIGH), None, ALU.mult))
                step(pool.tensor_tensor(wide, wide, slack[:], ALU.add))
                step(pool.tensor_tensor(wide, wide, slack[:], ALU.add))
                step(pool.tensor_scalar(wide, wide, 0.5, None, ALU.mult))
                step(pool.memset(halves[:], 0.5))
                for h, (vec, sca) in enumerate(SEARCH):
                    own = slice(vec.start, sca.stop)
                    step(pool.tensor_tensor(mid[:, own], low[:, own], width[:, 0, own], ALU.add))
                    pool.sem_inc(mid_r[h], 1)
                with pool.Fori(0, HALVINGS // 2) as i:
                    for par in range(2):
                        for h, (vec, sca) in enumerate(SEARCH):
                            own = slice(vec.start, sca.stop)
                            done = 20 * i + 10 * par + 5 * h
                            now, then = width[:, par, :], width[:, 1 - par, :]
                            pool.wait_ge(cnt_v, 4 * i + 2 * par + h + 1)
                            pool.wait_ge(cnt_s, 4 * i + 2 * par + h + 1)
                            pool.tensor_tensor(then[:, own], now[:, own], halves[:, own], ALU.mult).then_inc(sch, 1)
                            pool.tensor_scalar(sel[:, vec], cnt[:, vec], float(TOP) - 0.5, None, ALU.is_ge)\
                                .then_inc(sch, 1)
                            pool.tensor_scalar(sel[:, sca], cnt[:, sca], float(N - 2 * TOP), None, ALU.is_le)\
                                .then_inc(sch, 1)
                            pool.wait_ge(sch, done + 3)
                            pool.tensor_tensor(sel[:, own], sel[:, own], now[:, own], ALU.mult).then_inc(sch, 1)
                            pool.wait_ge(sch, done + 4)
                            pool.tensor_tensor(low[:, own], low[:, own], sel[:, own], ALU.add).then_inc(sch, 1)
                            pool.wait_ge(sch, done + 5)
                            pool.tensor_tensor(mid[:, own], low[:, own], then[:, own], ALU.add).then_inc(mid_r[h], 1)
                for t in range(T):
                    if t >= 4:
                        pool.wait_ge(x_r, t - 3)
                    pool.wait_ge(a_r, t + 1)
                    pool.wait_ge(y_r, t + 1)
                    pool.tensor_tensor(tb[:, t % 4, :], S[:, t, :], x[:, t, :], ALU.add).then_inc(t_r, 1)
                    if t % R == 2 and t > R:
                        layer_norm_scales(pool, g, t // R - 1, new_st, step)
                layer_norm_scales(pool, g, B - 1, new_st, step)

            @block.vector
            def _(dve):
                step = linked(dve, g["vector_chain"])
                for b in range(B):
                    dve.wait_ge(x_in_s[b], 16)
                    for t in range(R * b, R * b + R):
                        last = dve.bn_stats(stats[:, t, :], x[:, t, :])
                step(last)
                for t in range(T):
                    last = dve.bn_aggr(mv[:, t, :], stats[:, t, :])
                last.then_inc(lnst, 1)
                for t in range(T):
                    dve.wait_ge(s_sb, t + 1)
                    last = dve.bn_stats(sst[:, t, :], S[:, t, :])
                step(last)
                for t in range(T):
                    last = dve.bn_aggr(smv[:, t, :], sst[:, t, :])
                last.then_inc(sim_st, 1)
                with dve.Fori(0, HALVINGS) as i:
                    for h, (own, _) in enumerate(SEARCH):
                        dve.wait_ge(mid_r[h], i + 1)
                        for t in range(own.start, own.stop):
                            last = dve.tensor_scalar(junk[:, t, :], S[:, t, :], mid[:, t:t + 1], None, ALU.is_ge,
                                                     ALU.add, accum_out=cnt[:, t:t + 1])
                        last.then_inc(cnt_v, 1)
                for h in range(2):
                    dve.wait_ge(mid_r[h], HALVINGS + 1)
                for b in range(B + 1):
                    for t in range(R * b, R * b + R) if b < B else ():
                        dve.wait_ge(sig_r, t + 1)
                        dve.scalar_tensor_tensor(S[:, t, :], S[:, t, :], low[:, t:t + 1], sg[:, t % 4, :],
                                                 ALU.is_ge, ALU.mult).then_inc(a_r, 1)
                    for t in range(R * b - R, R * b) if b else ():
                        dve.wait_ge(at_r, t + 1)
                        dve.wait_ge(t_r, t + 1)
                        dve.tensor_tensor(x[:, t, :], bank[:, t % 8, :], tb[:, t % 4, :], ALU.add).then_inc(x_r, 1)
                        if t >= 1:
                            layer_norm_stats(dve, g, t - 1, (x_r, t), new_st, step)
                layer_norm_stats(dve, g, T - 1, (x_r, T), new_st, step)


def phase_moe(nc, sb, sem, g):
    x, bank, ident, tg, rstd, nmr = g["x"], g["bank"], g["ident"], g["tg"], g["rstd"], g["nmr"]
    with ExitStack() as scope:
        def s_(name, shape, dt=F32):
            return sb(name, shape, dt, scope)
        xT_hi = s_("moe_xT_hi", [P, DC, B * N], F32R)
        xT_lo = s_("moe_xT_lo", [P, DC, B * N], F32R)
        coefs = s_("moe_coefs", [P, MOE_UNITS, T])
        scratch = s_("moe_scratch", [P, 2, HC, 512])
        xn = scratch[:].rearrange("p a c n -> p (a c) n")
        rw, rw_in = g["rw"], g["rw_in"]
        rw_split = s_("moe_rw_split", [P, DC, 2, E_], F32R)
        logits = s_("moe_logits", [P, T, E_])
        best = s_("moe_best", [P, T, 8])
        best_at = s_("moe_best_at", [P, T, 8], U32)
        at_f = s_("moe_at_f", [P, 2, T])
        gap = s_("moe_gap", [P, T])
        w2 = s_("moe_w2", [P, T])
        w1 = s_("moe_w1", [P, T])
        eids = s_("moe_eids", [P, E_, T], I32)
        eids_f = s_("moe_eids_f", [P, E_, T])
        pick = s_("moe_pick", [P, E_, T])
        coef = s_("moe_coef", [P, 2, T])
        h_hi = s_("moe_h_hi", [P, 2, HC, 512], F32R)
        h_lo = s_("moe_h_lo", [P, 2, HC, 512], F32R)

        rw_h = sem("moe_router_hi")
        rw_l = sem("moe_router_lo")
        xn_r = sem("moe_xn_ready")
        xt_p = sem("moe_xT_transposed")
        xt_h = sem("moe_xT_hi_ready")
        xt_l = sem("moe_xT_lo_ready")
        lg_p = sem("moe_logits_done")
        lg_r = sem("moe_logits_ready")
        gp_r = sem("moe_gap_ready")
        ex_r = sem("moe_exp_ready")
        io_r = sem("moe_ids_ready")
        cf_r = sem("moe_coefs_ready")

        def constants(pool):
            step = linked(pool, g["pool_chain"])
            pool.wait_ge(rw_h, 1)
            pool.tensor_tensor(rw_split[:, :, 1, :], rw[:], rw_split[:, :, 0, :].bitcast(F32), ALU.subtract)\
                .then_inc(rw_l, 1)
            step(pool.iota(eids[:], pattern=[[1, E_], [0, T]], base=0, channel_multiplier=0))
            pool.tensor_copy(eids_f[:], eids[:]).then_inc(io_r, 1)

        def coefs_made(pool):
            pool.wait_ge(cf_r, 1)

        def x_hi(act, split_first):
            act.wait_ge(rw_in, 16)
            act.activation(rw_split[:, :, 0, :], rw[:], ACT.Copy).then_inc(rw_h, 1)

            def normalise(t):
                if t >= 4:
                    act.wait_ge(xt_p, t - 3)
                act.activation(xn[:, t % 4, :], x[:, t, :], ACT.Identity, bias=nmr[:, t:t + 1],
                               scale=rstd[:, t:t + 1]).then_inc(xn_r, 1)

            for t in range(3):
                normalise(t)
            for t in range(T):
                if t + 3 < T:
                    normalise(t + 3)
                act.wait_ge(xt_p, t + 1)
                act.activation(xT_hi[:, :, t * P:(t + 1) * P], bank[:, t % 4, :].rearrange("p (c n) -> p c n", c=DC),
                               ACT.Copy).then_inc(xt_h, 1)
                if t == T // 2:
                    split_first()

        def gap_exp(act):
            act.wait_ge(gp_r, 1)
            act.activation(w2[:], gap[:], ACT.Exp).then_inc(ex_r, 1)

        def x_turned(pe):
            def router(t):
                pe.wait_ge(xt_l, t + 1)
                at = slice(t * P, (t + 1) * P)
                for c in range(DC):
                    pe.matmul(bank[:, 4, t * 2 * E_:(t + 1) * 2 * E_], xT_hi[:, c, at],
                              rw_split[:, c].rearrange("p k e -> p (k e)"), start=c == 0, stop=False)
                for c in range(DC):
                    last = pe.matmul(bank[:, 4, t * 2 * E_:t * 2 * E_ + E_], xT_lo[:, c, at], rw_split[:, c, 0, :],
                                     start=False, stop=c == DC - 1)
                last.then_inc(lg_p, 1)

            for t in range(T):
                pe.wait_ge(xn_r, t + 1)
                if t >= 4:
                    pe.wait_ge(xt_l, t - 3)
                for c in range(DC):
                    last = pe.transpose(bank[:, t % 4, c * P:(c + 1) * P], xn[:, t % 4, c * P:(c + 1) * P], ident[:])
                last.then_inc(xt_p, 1)
                if t == 2:
                    pe.wait_ge(rw_l, 1)
                if t >= 2:
                    router(t - 2)
            router(T - 2)
            router(T - 1)
            pe.wait_ge(xt_l, T)
            pe.wait_ge(lg_r, 1)

        def x_lo(dve):
            for t in range(T):
                dve.wait_ge(xt_h, t + 1)
                at = slice(t * P, (t + 1) * P)
                dve.tensor_tensor(xT_lo[:, :, at], bank[:, t % 4, :].rearrange("p (c n) -> p c n", c=DC),
                                  xT_hi[:, :, at].bitcast(F32), ALU.subtract).then_inc(xt_l, 1)
            step = linked(dve, g["vector_chain"])
            both = bank[:, 4, 0:T * 2 * E_].rearrange("p (t k e) -> p t k e", k=2, e=E_)
            dve.wait_ge(lg_p, T)
            step(dve.tensor_copy(logits[:], both[:, :, 0, :]))
            dve.tensor_tensor(logits[:], logits[:], both[:, :, 1, :], ALU.add).then_inc(lg_r, 1)

        def two_best(dve):
            step = linked(dve, g["vector_chain"])
            dve.wait_ge(lg_r, 1)
            for t in range(T):
                last = dve.max(best[:, t, :], logits[:, t, :])
            step(last)
            dve.tensor_tensor(gap[:], best[:, :, 1], best[:, :, 0], ALU.subtract).then_inc(gp_r, 1)
            for t in range(T):
                last = dve.max_index(best_at[:, t, :], best[:, t, :], logits[:, t, :])
            step(last)
            step(dve.tensor_copy(at_f[:], best_at[:, :, 0:2].rearrange("p t k -> p k t")))
            dve.wait_ge(ex_r, 1)
            step(dve.tensor_scalar(w1[:], w2[:], 1.0, None, ALU.add))
            step(dve.reciprocal(w1[:], w1[:]))
            step(dve.tensor_scalar(w1[:], w1[:], tg[:, 2:3], None, ALU.mult))
            step(dve.tensor_tensor(w2[:], w2[:], w1[:], ALU.mult))
            dve.wait_ge(io_r, 1)
            for k, w in ((0, w1), (1, w2)):
                dst = coefs[:, 0:E_, :] if k == 0 else pick[:]
                each = at_f[:, k, :].unsqueeze(1).broadcast_to([P, E_, T])
                step(dve.tensor_tensor(dst, eids_f[:], each, ALU.is_equal))
                step(dve.tensor_tensor(dst, dst, w[:].unsqueeze(1).broadcast_to([P, E_, T]), ALU.mult))
            step(dve.tensor_tensor(coefs[:, 0:E_, :], coefs[:, 0:E_, :], pick[:], ALU.add))
            ones = coefs[:, E_:MOE_UNITS, :]
            step(dve.memset(ones, 1.0))
            step(dve.tensor_scalar(ones, ones, tg[:, 2:3], None, ALU.mult))
            step(dve.tensor_copy(coef[:, 0, :], coefs[:, 0, :]))
            dve.sem_inc(cf_r, 1)

        def source(u):
            if not isinstance(u, int) or u < E_:
                return expert(g, u)
            at = slice((u - E_) * UH, (u - E_ + 1) * UH)
            return (g["sw_gate"][:, at].rearrange("(c p) h -> p c h", p=P),
                    g["sw_up"][:, at].rearrange("(c p) h -> p c h", p=P),
                    g["sw_down"][at, :].rearrange("(k p) d -> p k d", p=P))

        gated_units(nc, s_, sem, "moe", g, xT_hi, xT_lo, MOE_UNITS, source, coefs=(coefs, coef),
                    raw=g["first_raw"], w_in=g["first_w"], scratch=scratch, h=(h_hi, h_lo),
                    first=dict(gpsimd=constants, scalar=x_hi, tensor=x_turned, vector=x_lo),
                    second=dict(gpsimd=coefs_made, scalar=gap_exp, vector=two_best))


def gated_units(nc, s_, sem, tag, g, xT_hi, xT_lo, units, source, coefs=None, gate=None, mod=None, raw=None,
                w_in=None, scratch=None, h=None, first={}, second={}, out_dram=None):
    x, bank = g["x"], g["bank"]

    def also(work, name, eng):
        if name in work:
            work[name](eng)

    raw_g, raw_u, raw_d = raw
    g_hi = s_(tag + "_g_hi", [P, 2, DC, UH], F32R)
    g_lo = s_(tag + "_g_lo", [P, 2, DC, UH], F32R)
    u_hi = s_(tag + "_u_hi", [P, 2, DC, UH], F32R)
    u_lo = s_(tag + "_u_lo", [P, 2, DC, UH], F32R)
    d_hi = s_(tag + "_d_hi", [P, 2, HC, D], F32R)
    d_lo = s_(tag + "_d_lo", [P, 2, HC, D], F32R)
    sil, hid = scratch[:, 0], scratch[:, 1]
    h_hi, h_lo = h
    if coefs is not None:
        coefs, coef = coefs
    if mod is not None:
        b_stack, m_stack = mod
        b_unit = s_(tag + "_b_unit", [96, 2, UH], F32R)

    w_hi = sem(tag + "_w_hi_ready")
    w_lo = sem(tag + "_w_lo_ready")
    g_ps = sem(tag + "_gate_done")
    u_ps = sem(tag + "_up_done")
    sil_r = sem(tag + "_silu_ready")
    hid_r = sem(tag + "_hidden_ready")
    hhi_r = sem(tag + "_h_hi_ready")
    hlo_r = sem(tag + "_h_lo_ready")
    y_ps = sem(tag + "_y_done")
    acc_r = sem(tag + "_y_added")
    if out_dram is None:
        st_r = sem(tag + "_new_stats_ready")
    else:
        out_s = sem(tag + "_x_stored")
    loops = units // 2 - 1

    with nc.Block() as block:
        @block.sync
        def _(sp):
            def load(u):
                for dst, src in zip((raw_g, raw_u, raw_d), source(u)):
                    sp.dma_start(dst, src).then_inc(w_in, 16)

            also(first, "sync", sp)
            with sp.Fori(0, loops - 1) as i:
                for p in range(2):
                    sp.wait_ge(w_lo, 2 * i + p + 1)
                    load(2 * i + p + 1)
            for u in range(2 * loops - 1, units):
                sp.wait_ge(w_lo, u)
                load(u)
            if out_dram is not None:
                for b in range(B):
                    own = slice(R * b, R * b + R)
                    sp.wait_ge(acc_r, T * (units - 1) + R * (b + 1) + ACC_LEAD)
                    sp.dma_start(out_dram[:, own, :], x[:, own, :]).then_inc(out_s, 16)
                sp.wait_ge(out_s, 16 * B)

        @block.gpsimd
        def _(pool):
            def split_lo(u, p, first_unit=False):
                if coefs is not None and not first_unit:
                    pool.wait_ge(acc_r, 16 * u - 16 + ACC_LEAD)
                pool.wait_ge(w_hi, u + 1)
                pool.tensor_tensor(g_lo[:, p], raw_g, g_hi[:, p].bitcast(F32), ALU.subtract)
                if coefs is not None and not first_unit:
                    pool.tensor_copy(coef[:, p, :], coefs[:, u, :])
                if mod is not None:
                    pool.tensor_copy(b_unit[:, p, :], b_stack[:, bass.ds(u * UH, UH)].bitcast(F32))
                pool.tensor_tensor(u_lo[:, p], raw_u, u_hi[:, p].bitcast(F32), ALU.subtract)
                pool.tensor_tensor(d_lo[:, p], raw_d, d_hi[:, p].bitcast(F32), ALU.subtract).then_inc(w_lo, 1)

            also(first, "gpsimd", pool)
            split_lo(0, 0, first_unit=True)
            also(second, "gpsimd", pool)
            with pool.Fori(0, loops) as i:
                for p in range(2):
                    split_lo(2 * i + p + 1, (p + 1) % 2)
            split_lo(2 * loops + 1, 1)
            if out_dram is None:
                for b in range(B):
                    layer_norm_scales(pool, g, b, st_r, linked(pool, g["pool_chain"]))

        @block.scalar
        def _(act):
            act.sem_inc(sil_r, GU_LEAD)

            def split_hi(u, p, first_unit=False):
                act.wait_ge(w_in, 48 * (u + 1))
                if not first_unit:
                    act.wait_ge(y_ps, 16 * u + Y_LEAD - 16)
                act.activation(g_hi[:, p], raw_g, ACT.Copy)
                act.activation(u_hi[:, p], raw_u, ACT.Copy)
                act.activation(d_hi[:, p], raw_d, ACT.Copy).then_inc(w_hi, 1)

            def hidden(n, tb):
                for c in range(HC):
                    act.wait_ge(g_ps, 2 * n + c + 1)
                    act.wait_ge(hid_r, 2 * n + c - 1 + GU_LEAD)
                    act.activation(sil[:, c, :], bank[:, 2 * c, :], ACT.Silu).then_inc(sil_r, 1)
                for c in range(HC):
                    act.wait_ge(hid_r, 2 * n + c + 1 + GU_LEAD)
                    if c == 0:
                        act.wait_ge(y_ps, 4 * n - 4 + Y_LEAD)
                    act.activation(h_hi[:, tb % 2, c, :], hid[:, c, :], ACT.Copy).then_inc(hhi_r, 1)

            def pair(i, last):
                for p in range(2):
                    for tb in range(TB):
                        n = 8 * i + 4 * p + tb
                        if not (last and p == 1 and tb == TB - 1):
                            hidden(n + 1, (tb + 1) % TB)
                        if tb == 0 and not (last and p == 1):
                            split_hi(2 * i + p + 1, (p + 1) % 2)

            first["scalar"](act, lambda: split_hi(0, 0, first_unit=True))
            hidden(0, 0)
            also(second, "scalar", act)
            with act.Fori(0, loops) as i:
                pair(i, False)
            pair(loops, True)

        @block.tensor
        def _(pe):
            pe.sem_inc(y_ps, Y_LEAD)

            def gate_up(n, u, p, tb):
                if tb == 0:
                    pe.wait_ge(w_lo, u + 1)
                at = slice(tb * 512, (tb + 1) * 512)
                for c in range(HC):
                    hs = slice(c * P, (c + 1) * P)
                    for which, (w_h, w_l) in enumerate(((g_hi, g_lo), (u_hi, u_lo))):
                        pe.wait_ge((sil_r, hid_r)[which], 2 * n + c - 1 + GU_LEAD)
                        passes = [(w, a, k) for k in range(DC) for w, a in ((w_h, xT_hi), (w_h, xT_lo), (w_l, xT_hi))]
                        more = mod is not None and which == 0
                        for k, (w, a, d) in enumerate(passes):
                            last = pe.matmul(bank[:, 2 * c + which, :], w[:, p, d, hs], a[:, d, at], start=k == 0,
                                             stop=k == len(passes) - 1 and not more)
                        if more:
                            last = pe.matmul(bank[:, 2 * c, :], b_unit[:, p, hs], m_stack[:, at], start=False, stop=True)
                        last.then_inc((g_ps, u_ps)[which], 1)

            def down(n, p, tb):
                pe.wait_ge(hlo_r, 2 * n + 2 + GU_LEAD)
                for j in range(4):
                    js = slice(j * P, (j + 1) * P)
                    pe.wait_ge(acc_r, 4 * n + j - 3 + ACC_LEAD)
                    passes = [(h, w, k) for k in range(HC) for h, w in ((h_hi, d_hi), (h_hi, d_lo), (h_lo, d_hi))]
                    for k, (h, w, c) in enumerate(passes):
                        last = pe.matmul(bank[:, 4 + j, :], h[:, tb % 2, c, js], w[:, p, c, :], start=k == 0,
                                         stop=k == len(passes) - 1)
                    last.then_inc(y_ps, 1)

            def pair(i, last):
                for p in range(2):
                    for tb in range(TB):
                        n = 8 * i + 4 * p + tb
                        over = tb == TB - 1
                        if not (last and p == 1 and over):
                            gate_up(n + 1, 2 * i + p + over, (p + over) % 2, (tb + 1) % TB)
                        down(n, p, tb)

            also(first, "tensor", pe)
            gate_up(0, 0, 0, 0)
            also(second, "tensor", pe)
            with pe.Fori(0, loops) as i:
                pair(i, False)
            pair(loops, True)

        @block.vector
        def _(dve):
            dve.sem_inc(hid_r, GU_LEAD)
            dve.sem_inc(acc_r, ACC_LEAD)
            dve.sem_inc(hlo_r, GU_LEAD)

            def hidden(n, tb):
                for c in range(HC):
                    dve.wait_ge(sil_r, 2 * n + c + 1 + GU_LEAD)
                    dve.wait_ge(u_ps, 2 * n + c + 1)
                    dve.wait_ge(hlo_r, 2 * n + c - 1 + GU_LEAD)
                    dve.tensor_tensor(hid[:, c, :], bank[:, 2 * c + 1, :], sil[:, c, :], ALU.mult).then_inc(hid_r, 1)
                for c in range(HC):
                    dve.wait_ge(hhi_r, 2 * n + c + 1)
                    dve.tensor_tensor(h_lo[:, tb % 2, c, :], hid[:, c, :], h_hi[:, tb % 2, c, :].bitcast(F32),
                                      ALU.subtract).then_inc(hlo_r, 1)

            def add(n, p, tb, final=False):
                link = linked(dve, g["vector_chain"])
                for j in range(4):
                    t = 4 * tb + j
                    dve.wait_ge(y_ps, 4 * n + j + 1 + Y_LEAD)
                    dve.wait_ge(acc_r, 4 * n + j - 15 + ACC_LEAD)
                    scalar = coef[:, p, t:t + 1] if coefs is not None else gate
                    dve.scalar_tensor_tensor(x[:, t, :], bank[:, 4 + j, :], scalar, x[:, t, :], ALU.mult, ALU.add)\
                       .then_inc(acc_r, 1)
                    if final and out_dram is None and j >= 1:
                        layer_norm_stats(dve, g, t - 1, (acc_r, 4 * n + j + ACC_LEAD), st_r, link)
                if final and out_dram is None:
                    layer_norm_stats(dve, g, t, (acc_r, 4 * n + 4 + ACC_LEAD), st_r, link)

            def pair(i, last):
                for p in range(2):
                    for tb in range(TB):
                        n = 8 * i + 4 * p + tb
                        if not (last and p == 1 and tb == TB - 1):
                            hidden(n + 1, (tb + 1) % TB)
                        add(n, p, tb, final=last and p == 1)

            also(first, "vector", dve)
            hidden(0, 0)
            also(second, "vector", dve)
            with dve.Fori(0, loops) as i:
                pair(i, False)
            pair(loops, True)


def phase_kv(nc, sb, sem, g):
    x, bank, ident, tg = g["x"], g["bank"], g["ident"], g["tg"]
    half, rstd, nmr = g["half"], g["rstd"], g["nmr"]
    with ExitStack() as scope:
        def s_(name, shape, dt=F32):
            return sb(name, shape, dt, scope)
        ctxT, wk, bk, gamma, beta = g["ctxT"], g["kv_wk"], g["kv_bk"], g["kv_gamma"], g["kv_beta"]
        kvT = s_("kvT", [C, 2, N])
        kv = s_("kv", [P, 2, R, C])
        xn = s_("kv_xn", [P, R, D])
        xnT = s_("kv_xnT", [P, DC, N])
        outT = s_("kv_outT", [C, 2, N])
        sst = s_("kv_sim_stats", [P, R, 6])
        smv = s_("kv_sim_mv", [P, R, 2])
        sr = s_("kv_sim_rstd", [P, R])
        sn = s_("kv_sim_nmr", [P, R])
        sv = s_("kv_sim_var", [P, R])
        y = s_("kv_y", [P, R, N])
        yb = s_("kv_yb", [P, R, N])
        nmax = s_("kv_nmax", [P, R])
        total = s_("kv_total", [P, R])
        share = s_("kv_share", [P, R])
        ex = s_("kv_exp", [P, R, N])

        w_in = g["kv_in"]
        kvT_p = sem("kv_kvT_done")
        kvT_r = sem("kv_kvT_ready")
        kv_p = sem("kv_kv_transposed")
        kv_r = sem("kv_kv_ready")
        xn_r = sem("kv_xn_ready")
        xt_p = sem("kv_xnT_transposed")
        xt_r = sem("kv_xnT_ready")
        ot_p = sem("kv_outT_done")
        ot_r = sem("kv_outT_ready")
        sim_p = sem("kv_sim_done")
        sst_r = sem("kv_sim_stats_ready")
        srs_r = sem("kv_sim_rstd_ready")
        y_r = sem("kv_y_ready")
        yg_r = sem("kv_y_gamma_ready")
        yb_r = sem("kv_y_beta_ready")
        mx_r = sem("kv_max_ready")
        ex_r = sem("kv_exp_ready")
        x_r = sem("kv_x_ready")
        new_st = sem("kv_new_stats_ready")
        att = g["att"]

        with nc.Block() as block:
            @block.sync
            def _(sp):
                att.load(sp)

            @block.tensor
            def _(pe):
                pe.wait_ge(w_in, 64)
                for b in range(B):
                    if b >= 1:
                        pe.wait_ge(xt_r, 4 * b - 2)
                    pe.matmul(bank[:, 0, :], wk[:], ctxT[:, b, :], start=True, stop=True).then_inc(kvT_p, 1)
                    pe.wait_ge(kvT_r, b + 1)
                    for j in range(R):
                        last = pe.transpose(bank[:, 1, j * C:(j + 1) * C], kvT[:, b % 2, j * P:(j + 1) * P], ident[:])
                    last.then_inc(kv_p, 1)
                    pe.wait_ge(xn_r, R * (b + 1))
                    for c in range(DC):
                        if b >= 1 or c >= 2:
                            pe.wait_ge(xt_r, 4 * b + c - 2)
                        if c == 2:
                            pe.wait_ge(kvT_r, b + 1)
                            pe.wait_ge(kv_r, b + 1)
                        for r in range(R):
                            last = pe.transpose(bank[:, (c + 2) % 4, r * P:(r + 1) * P], xn[:, r, c * P:(c + 1) * P],
                                                ident[:])
                        last.then_inc(xt_p, 1)
                    pe.wait_ge(kv_r, b + 1)
                    pe.wait_ge(xt_r, 4 * b + 4)
                    if b >= 1:
                        pe.wait_ge(ot_r, b)
                    for c in range(DC):
                        last = pe.matmul(bank[:, 2, :], kv[:, b % 2, c, :], xnT[:, c, :], start=c == 0, stop=c == DC - 1)
                    last.then_inc(ot_p, 1)
                    pe.wait_ge(ot_r, b + 1)
                    for r in range(R):
                        if b >= 1:
                            pe.wait_ge(y_r, R * (b - 1) + r + 1)
                        pe.matmul(bank[:, 4 + r, :], outT[:, b % 2, r * P:(r + 1) * P], kvT[:, b % 2, :],
                                  start=True, stop=True).then_inc(sim_p, 1)
                att.value_weights(pe)

            @block.scalar
            def _(act):
                act.wait_ge(w_in, 64)

                def values(b):
                    act.wait_ge(kvT_p, b + 1)
                    if b >= 2:
                        act.wait_ge(sim_p, R * (b - 1))
                    act.activation(kvT[:, b % 2, :], bank[:, 0, :], ACT.Identity, bias=bk[:, 0:1]).then_inc(kvT_r, 1)
                    act.wait_ge(kv_p, b + 1)
                    act.activation(kv[:, b % 2], bank[:, 1, :].rearrange("p (j c) -> p j c", j=R), ACT.Copy)\
                       .then_inc(kv_r, 1)
                    if b >= 1:
                        act.wait_ge(xt_p, DC * b)
                    for r in range(R):
                        t = R * b + r
                        act.activation(xn[:, r, :], x[:, t, :], ACT.Identity, bias=nmr[:, t:t + 1],
                                       scale=rstd[:, t:t + 1]).then_inc(xn_r, 1)

                def turned(b):
                    for c in range(DC):
                        act.wait_ge(xt_p, DC * b + c + 1)
                        if b >= 1:
                            act.wait_ge(ot_p, b)
                        act.activation(xnT[:, c, :], bank[:, (c + 2) % 4, :], ACT.Copy).then_inc(xt_r, 1)

                def out(b):
                    act.wait_ge(ot_p, b + 1)
                    act.activation(outT[:, b % 2, :], bank[:, 2, :], ACT.Copy).then_inc(ot_r, 1)

                def scale(b):
                    act.wait_ge(srs_r, b + 1)
                    if b >= 1:
                        act.wait_ge(yb_r, R * b)
                    for r in range(R):
                        act.activation(y[:, r, :], bank[:, 4 + r, :], ACT.Identity, bias=sn[:, r:r + 1],
                                       scale=sr[:, r:r + 1]).then_inc(y_r, 1)

                def soften(b):
                    act.wait_ge(mx_r, b + 1)
                    if b >= 1:
                        act.wait_ge(x_r, R * b)
                    for r in range(R):
                        act.activation(ex[:, r, :], yb[:, r, :], ACT.Exp, bias=nmax[:, r:r + 1],
                                       accum_out=total[:, r:r + 1]).then_inc(ex_r, 1)

                values(0)
                turned(0)
                out(0)
                for b in range(B):
                    if b + 1 < B:
                        values(b + 1)
                    scale(b)
                    if b + 1 < B:
                        turned(b + 1)
                        out(b + 1)
                    else:
                        att.value_weights_hi(act)
                    soften(b)
                    if b == 0:
                        att.query_weights_hi(act)

            @block.gpsimd
            def _(pool):
                step = linked(pool, g["pool_chain"])
                pool.wait_ge(w_in, 64)
                for b in range(B):
                    step = linked(pool, g["pool_chain"])
                    pool.wait_ge(sst_r, b + 1)
                    if b >= 1:
                        pool.wait_ge(y_r, R * b)
                    step(pool.tensor_scalar(sv[:], smv[:, :, 1], KV_SCALE * KV_SCALE, KV_EPS, ALU.mult, ALU.add))
                    step(pool.tensor_tensor(sv[:], sv[:], half[:, 0:R], ALU.pow))
                    step(pool.tensor_scalar(sr[:], sv[:], KV_SCALE, None, ALU.mult))
                    step(pool.tensor_tensor(sn[:], smv[:, :, 0], sr[:], ALU.mult))
                    pool.tensor_scalar(sn[:], sn[:], -1.0, None, ALU.mult).then_inc(srs_r, 1)
                    for r in range(R):
                        pool.wait_ge(yg_r, R * b + r + 1)
                        if b >= 1 and r == 0:
                            pool.wait_ge(ex_r, R * b)
                        pool.tensor_tensor(yb[:, r, :], y[:, r, :], beta, ALU.add).then_inc(yb_r, 1)
                    if b == 0:
                        att.constants(pool)
                    if b == 1:
                        att.query_weights_lo(pool)
                    if b >= 1:
                        att.scales(pool, b - 1, new_st)
                att.scales(pool, B - 1, new_st)

            @block.vector
            def _(dve):
                dve.wait_ge(w_in, 64)
                for b in range(B):
                    step = linked(dve, g["vector_chain"])
                    for r in range(R):
                        dve.wait_ge(sim_p, R * b + r + 1)
                        last = dve.bn_stats(sst[:, r, :], bank[:, 4 + r, :])
                    step(last)
                    for r in range(R):
                        last = dve.bn_aggr(smv[:, r, :], sst[:, r, :])
                    last.then_inc(sst_r, 1)
                    if b == B - 1:
                        att.value_weights_lo(dve)
                    for r in range(R):
                        dve.wait_ge(y_r, R * b + r + 1)
                        dve.tensor_tensor(y[:, r, :], y[:, r, :], gamma, ALU.mult).then_inc(yg_r, 1)
                    for r in range(R):
                        dve.wait_ge(yb_r, R * b + r + 1)
                        if b >= 1 and r == 0:
                            dve.wait_ge(ex_r, R * b)
                        last = dve.reduce_max(nmax[:, r:r + 1], yb[:, r, :], AX)
                    step(last)
                    dve.tensor_scalar(nmax[:], nmax[:], -1.0, None, ALU.mult).then_inc(mx_r, 1)
                    dve.wait_ge(ex_r, R * b + R)
                    if b >= 1:
                        dve.wait_ge(x_r, R * b)
                    step(dve.reciprocal(share[:], total[:]))
                    step(dve.tensor_scalar(share[:], share[:], tg[:, 1:2], None, ALU.mult))
                    for r in range(R):
                        t = R * b + r
                        dve.scalar_tensor_tensor(x[:, t, :], ex[:, r, :], share[:, r:r + 1], x[:, t, :],
                                                 ALU.mult, ALU.add).then_inc(x_r, 1)
                        if r >= 1:
                            layer_norm_stats(dve, g, t - 1, (x_r, t), new_st, step)
                    layer_norm_stats(dve, g, R * b + R - 1, (x_r, R * b + R), new_st, step)


GH = P // HD
GB = HEADS // GH
KQ = 3 * HD
UC = 2 * RK + 1
OC = RK + 1


class AttentionOperands:

    def __init__(self, s_, sem, g):
        self.g = g
        self.raw = s_("at_raw", [P, 2, DC, D])
        self.wq_hi = s_("at_wq_hi", [P, DC, D], F32R)
        self.wq_lo = s_("at_wq_lo", [P, DC, D], F32R)
        self.wk_hi = s_("at_wk_hi", [P, DC, D], F32R)
        self.wk_lo = s_("at_wk_lo", [P, DC, D], F32R)
        self.wu_hi = s_("at_wu_hi", [P, DC, HEADS * RK], F32R)
        self.wu_lo = s_("at_wu_lo", [P, DC, HEADS * RK], F32R)
        self.A = s_("at_A", [P, DC, RK])
        self.woa = s_("at_woa", [P, DC, GH, RK])
        self.ln1 = s_("at_ln1", [P, DC])
        self.K = s_("at_K", [KQ + 2, 2, GH, N], F32R)
        self.V = s_("at_V", [P, 2, R, GH, 2 * UC], F32R)
        self.ones = s_("at_ones", [P, N])
        self.zeros = s_("at_zeros", [P, GH * 2 * UC])
        self.sel = s_("at_sel", [2 * UC, 2 * OC])
        self.mask_f = s_("at_mask_f", [P, P])
        self.mask = s_("at_mask", [P, P], F32R)
        self.maskT = s_("at_maskT", [P, P], F32R)
        self.ident_r = s_("at_ident", [P, P], F32R)
        self.small_in = sem("at_small_arrived")
        self.v_in, self.q_in = sem("at_values_arrived"), sem("at_queries_arrived")
        self.wqk_h, self.wqk_l = sem("at_wqk_hi_ready"), sem("at_wqk_lo_ready")
        self.ones_r, self.K_in = sem("at_ones_ready"), sem("at_K_ones_placed")
        self.woa_0, self.woa_p, self.woa_r = sem("at_woa_cleared"), sem("at_woa_done"), sem("at_woa_ready")
        self.wu_p, self.wu_h, self.wu_l = sem("at_wu_done"), sem("at_wu_hi_ready"), sem("at_wu_lo_ready")

    def load(self, sp):
        g, raw = self.g, self.raw
        sp.dma_start(raw[:, 0], g["WqT"].rearrange("(c p) o -> p c o", p=P)).then_inc(self.q_in, 16)
        sp.dma_start(raw[:, 1], g["WkT1"].rearrange("(c p) o -> p c o", p=P)).then_inc(self.q_in, 16)
        sp.dma_start(self.A[:], g["A_in"].rearrange("(c p) r -> p c r", p=P)).then_inc(self.small_in, 16)
        sp.dma_start(self.ln1[:], g["ln1_w"]).then_inc(self.small_in, 16)
        sp.wait_ge(self.ones_r, 1)
        for par in range(2):
            for j in range(GH):
                sp.dma_start(self.K[KQ:KQ + 2, par, j, :].bitcast(F32), self.ones[KQ:KQ + 2, :]).then_inc(self.K_in, 16)
        sp.wait_ge(self.K_in, 16 * 2 * GH)
        sp.wait_ge(self.wqk_l, 1)
        sp.dma_start(raw[:, 0], g["Wo"].rearrange("(c p) o -> p c o", p=P)).then_inc(self.v_in, 16)
        sp.dma_start(raw[:, 1], g["Wv"].rearrange("(c p) d -> p c d", p=P)).then_inc(self.v_in, 16)

    def constants(self, pool):
        step = linked(pool, self.g["pool_chain"])
        V, ones, sel = self.V, self.ones, self.sel
        pool.memset(self.woa[:], 0.0).then_inc(self.woa_0, 1)
        step(pool.memset(self.g["mod"][:], 0.0))
        step(pool.memset(ones[:], 1.0))
        step(pool.memset(self.zeros[:], 0.0))
        pool.sem_inc(self.ones_r, 1)
        for par in range(2):
            for r in range(R):
                step(pool.tensor_copy(V[:, par, r].rearrange("p h c -> p (h c)"), self.zeros[:]))
            for h in range(GH):
                at = UC * (h % 2) + RK
                step(pool.tensor_copy(V[:, par, :, h, at:at + 1], ones[:, 0:R].unsqueeze(2)))
        step(pool.memset(sel[:], 0.0))
        for h in range(2):
            for row, cols in ((UC * h, OC), (UC * h + OC, RK)):
                at = sel[:, OC * h:OC * h + cols]
                step(pool.affine_select(out=at, in_=at, compare_op=ALU.not_equal, fill=1.0, base=-row,
                                        pattern=[[-1, cols]], channel_multiplier=1))
        for dst, sign in ((self.mask, 1), (self.maskT, -1)):
            step(pool.memset(self.mask_f[:], 0.0))
            step(pool.affine_select(out=self.mask_f[:], in_=self.mask_f[:], compare_op=ALU.is_ge, fill=MASKED, base=0,
                                    pattern=[[-sign, P]], channel_multiplier=sign))
            step(pool.tensor_copy(dst[:], self.mask_f[:]))
        step(pool.tensor_copy(self.ident_r[:], self.g["ident"][:]))

    def query_weights_hi(self, act):
        act.wait_ge(self.q_in, 32)
        act.activation(self.wq_hi[:], self.raw[:, 0], ACT.Copy)
        act.activation(self.wk_hi[:], self.raw[:, 1], ACT.Copy).then_inc(self.wqk_h, 1)

    def query_weights_lo(self, pool):
        pool.wait_ge(self.wqk_h, 1)
        pool.tensor_tensor(self.wq_lo[:], self.raw[:, 0], self.wq_hi[:].bitcast(F32), ALU.subtract)
        pool.tensor_tensor(self.wk_lo[:], self.raw[:, 1], self.wk_hi[:].bitcast(F32), ALU.subtract)\
            .then_inc(self.wqk_l, 1)

    WU_BANKS = (0, 1, 3, 2)

    def value_weights(self, pe):
        bank, raw = self.g["bank"], self.raw
        pe.wait_ge(self.small_in, 32)
        pe.wait_ge(self.v_in, 32)
        for m in range(DC):
            for c in range(DC):
                last = pe.matmul(bank[:, 2, m * RK:(m + 1) * RK], raw[:, 0, c, m * P:(m + 1) * P], self.A[:, c, :],
                                 start=c == 0, stop=c == DC - 1)
        last.then_inc(self.woa_p, 1)
        pe.wait_ge(self.woa_r, 1)
        for d in range(DC):
            for m in range(DC):
                last = pe.matmul(bank[:, self.WU_BANKS[d], m * GH * RK:(m + 1) * GH * RK],
                                 raw[:, 1, m, d * P:(d + 1) * P], self.woa[:, m], start=True, stop=True)
            last.then_inc(self.wu_p, 1)

    def value_weights_hi(self, act):
        for d in range(DC):
            act.wait_ge(self.wu_p, d + 1)
            act.activation(self.wu_hi[:, d, :], self.g["bank"][:, self.WU_BANKS[d], 0:HEADS * RK], ACT.Copy)\
               .then_inc(self.wu_h, 1)

    def value_weights_lo(self, dve):
        bank = self.g["bank"]
        dve.wait_ge(self.woa_p, 1)
        dve.wait_ge(self.woa_0, 1)
        for j in range(GH):
            rows = slice(j * HD, (j + 1) * HD)
            last = dve.tensor_copy(self.woa[rows, :, j, :],
                                   bank[rows, 2, 0:DC * RK].rearrange("p (m r) -> p m r", r=RK))
        last.then_inc(self.woa_r, 1)
        for d in range(DC):
            dve.wait_ge(self.wu_h, d + 1)
            dve.tensor_tensor(self.wu_lo[:, d, :], bank[:, self.WU_BANKS[d], 0:HEADS * RK],
                              self.wu_hi[:, d, :].bitcast(F32), ALU.subtract).then_inc(self.wu_l, 1)

    def scales(self, pool, b, st_r):
        g = self.g
        step = linked(pool, g["pool_chain"])
        own = slice(R * b, R * b + R)
        layer_norm_scales(pool, g, b, st_r, step)
        rstd, nmr, sm1, tg = g["rstd"][:, own], g["nmr"][:, own], g["sm1"][:, own], g["tg"]
        step(pool.tensor_tensor(sm1, rstd, rstd, ALU.mult))
        step(pool.tensor_tensor(sm1, sm1, g["mv"][:, own, 1], ALU.mult))
        step(pool.tensor_scalar(sm1, sm1, 1.0, KV_EPS, ALU.mult, ALU.add))
        step(pool.tensor_tensor(sm1, sm1, g["half"][:, own], ALU.pow))
        step(pool.tensor_tensor(g["n_sc"][:, own], rstd, sm1, ALU.mult))
        step(pool.tensor_tensor(g["n_bi"][:, own], nmr, sm1, ALU.mult))
        step(pool.tensor_scalar(g["r_sc"][:, own], rstd, tg[:, 3:4], 1.0, ALU.mult, ALU.add))
        step(pool.tensor_scalar(g["r_bi"][:, own], nmr, tg[:, 3:4], 0.0, ALU.mult, ALU.add))


def phase_attention(nc, s_, sem, g):
    x, bank, ident, n_sc, n_bi, mod, att = g["x"], g["bank"], g["ident"], g["n_sc"], g["n_bi"], g["mod"], g["att"]
    wq_hi, wq_lo, wk_hi, wk_lo, wu_hi, wu_lo = att.wq_hi, att.wq_lo, att.wk_hi, att.wk_lo, att.wu_hi, att.wu_lo
    K, V, ones, sel, ln1 = att.K, att.V, att.ones, att.sel, att.ln1
    mask, maskT, ident_r = att.mask, att.maskT, att.ident_r
    US = GH * R
    pT, xn = att.raw[:, 0], att.raw[:, 1]
    xT_hi = s_("at_xT_hi", [P, DC, N], F32R)
    xT_lo = s_("at_xT_lo", [P, DC, N], F32R)
    q_hi = s_("at_q_hi", [P, N], F32R)
    q_lo = s_("at_q_lo", [P, N], F32R)
    k_hi = s_("at_k_hi", [P, N], F32R)
    k_lo = s_("at_k_lo", [P, N], F32R)
    Q = s_("at_Q", [KQ + 2, 2, GH, N], F32R)
    U = s_("at_U", [P, R, HEADS, RK])
    mx = s_("at_max", [P, 2, US // 2])
    m_hi = s_("at_m_hi", [US // 2, 2, P], F32R)
    m_lo = s_("at_m_lo", [US // 2, 2, P], F32R)
    SLOT = [N * k - P * k * (k - 1) // 2 for k in range(R + 1)]
    p_hi = s_("at_probsT_hi", [P, 2, SLOT[R]], F32R)
    p_lo = s_("at_probsT_lo", [P, 2, SLOT[R]], F32R)
    oT = s_("at_outT", [2 * UC, 2, N])
    rto = s_("at_rtotal", [P, R, 2])
    ou = s_("at_out", [P, R, 2, RK])
    red = s_("at_red", [P, R, RK])

    n_r = sem("at_n_ready")
    xt_p, xt_h, xt_l = sem("at_xT_transposed"), sem("at_xT_hi_ready"), sem("at_xT_lo_ready")
    q_p, q_h, q_l = sem("at_q_done"), sem("at_q_hi_ready"), sem("at_q_lo_ready")
    k_p, k_h, k_l = sem("at_k_done"), sem("at_k_hi_ready"), sem("at_k_lo_ready")
    u_p, u_r = sem("at_U_done"), sem("at_U_ready")
    qk_in = [sem(f"at_qk_of_head{j}_placed") for j in range(GH)]
    s_p, mx_r = sem("at_scores_done"), sem("at_max_ready")
    mt_p, m_h, m_l = sem("at_maxT_done"), sem("at_m_hi_ready"), sem("at_m_lo_ready")
    m_in = [sem(f"at_m_of_half{h}_placed") for h in range(2)]
    st_p, ex_r = sem("at_scoresT_done"), sem("at_probsT_ready")
    pl_r = sem("at_probs_lo_ready")
    v_h, v_r = sem("at_V_hi_ready"), sem("at_V_ready")
    o_p, ot_r, sl_p, o_r = sem("at_pv_done"), sem("at_outT_ready"), sem("at_out_turned"), sem("at_out_ready")
    och = sem("at_out_chain")
    ST_LEAD, EX_LEAD, O_LEAD, OR_LEAD, PL_LEAD, SL_LEAD, M_LEAD = 1, 2, 8, 2, 4, 2, 16
    LOW, PRODUCT, COPY, TURN, FINISH = 1, 4, 13, 15, 16
    TAIL = 12

    def at_least(eng, s, value):
        if not isinstance(value, int) or value > 0:
            eng.wait_ge(s, value)

    def each_step(step):
        step(-2, 2, True, False, False)
        step(-1, 3, True, True, False)
        return lambda b, last: [step(GB * b + oc, oc, not (last and oc >= 2), not (last and oc == 3), True)
                                for oc in range(GB)]

    def run(eng, step):
        batch = each_step(step)
        with eng.Fori(0, B - 1) as b:
            batch(b, False)
        batch(B - 1, True)

    def late(G, oc, s, lag):
        u = s - lag
        if 0 <= u < US:
            return G, oc, u
        return (G - 1, oc - 1, u + US) if u < 0 and oc > 0 else None

    def packed(p, s):
        h, k = s // R, s % R
        return p[:, h % 2, SLOT[k]:SLOT[k + 1]]

    BANK = {"m1": 1, "x0": 0, "x1": 1, "x2": 0, "x3": 1, "q": 0, "k": 1, "m0": 0, "u0": 1, "u1": 0}

    with nc.Block() as block:
        @block.sync
        def _(sp):
            sp.sem_inc(m_in[0], M_LEAD)
            sp.sem_inc(m_in[1], M_LEAD)
            for dst, src in zip(g["third_raw"], mlp_source(g, 0)):
                sp.dma_start(dst, src).then_inc(g["third_w"], 16)

            def place_max(group, par, h):
                at_least(sp, m_l, 2 * group + h + 1)
                rows = slice(GH // 2 * h, GH // 2 * (h + 1))
                for row, part in ((KQ, m_hi), (KQ + 1, m_lo)):
                    sp.dma_start(Q[row:row + 1, par, rows, :].rearrange("o j t -> o (j t)").bitcast(F32),
                                 part[:, h, :].bitcast(F32)).then_inc(m_in[h], 16)

            def place_qk(G, oc, probs, j):
                if j == 0:
                    at_least(sp, q_l, G + 3)
                    at_least(sp, k_l, G + 3)
                if probs:
                    at_least(sp, st_p, US * G + R * (j + 1) + ST_LEAD)
                hp = slice(j * HD, (j + 1) * HD)
                for k, (pq, pk) in enumerate(((q_hi, k_hi), (q_lo, k_hi), (q_hi, k_lo))):
                    rows = slice(k * HD, (k + 1) * HD)
                    sp.dma_start(Q[rows, oc % 2, j, :].bitcast(F32), pq[hp, :].bitcast(F32)).then_inc(qk_in[j], 16)
                    sp.dma_start(K[rows, oc % 2, j, :].bitcast(F32), pk[hp, :].bitcast(F32)).then_inc(qk_in[j], 16)

            def step(G, oc, project, maxima, probs):
                if probs:
                    place_max(G, oc % 2, 1)
                if maxima:
                    place_max(G + 1, (oc + 1) % 2, 0)
                if project:
                    for j in range(GH):
                        place_qk(G, oc, probs, j)
            run(sp, step)

        @block.gpsimd
        def _(pool):
            def values(G, oc):
                one = ones[:, 0:R * RK].rearrange("p (r k) -> p r k", r=R)
                of, par = (oc + 1) % GB, (oc + 1) % 2
                if of == 0:
                    at_least(pool, u_r, G + 1 + R)
                at_least(pool, o_p, US * G + O_LEAD)
                for part in range(2):
                    for j in range(GH):
                        own = U[:, :, of * GH + j, :]
                        hi = V[:, par, :, j, UC * (j % 2):UC * (j % 2) + RK]
                        lo = V[:, par, :, j, UC * (j % 2) + OC:UC * (j % 2) + UC]
                        if part == 0:
                            last = pool.tensor_tensor(hi, own, one, ALU.mult)
                        else:
                            last = pool.tensor_tensor(lo, own, hi.bitcast(F32), ALU.subtract)
                    last.then_inc((v_h, v_r)[part], 1)
                    if part == 0:
                        at_least(pool, v_h, G + 2)

            def group(G, oc, project, maxima, probs):
                if maxima:
                    values(G, oc)
            run(pool, group)

        @block.tensor
        def _(pe):
            pe.sem_inc(st_p, ST_LEAD)
            pe.sem_inc(o_p, O_LEAD)
            pe.sem_inc(sl_p, SL_LEAD)
            def turn_x(G, c):
                at_least(pe, n_r, G + 2 + R)
                at_least(pe, *((m_l, 2 * G + 1), (m_l, 2 * G + 2), (xt_l, G + 3), (xt_l, G + 4))[c])
                for r in range(R):
                    last = pe.transpose(bank[:, BANK[f"x{c}"], r * P:(r + 1) * P], xn[:, r, c * P:(c + 1) * P], ident[:])
                last.then_inc(xt_p, 1)

            def project(G, oc, which, part, parts):
                heads = (oc + 2) % GB
                if part == 0 and which == "q":
                    if oc == 2:
                        at_least(pe, xt_l, G + 2 + DC)
                    elif oc == 3:
                        at_least(pe, u_r, G + 1 + R)
                    else:
                        at_least(pe, m_l, 2 * G + 1)
                if part == 0 and which == "k" and oc != 2:
                    at_least(pe, m_l, 2 * G + 2)
                w_h, w_l = (wq_hi, wq_lo) if which == "q" else (wk_hi, wk_lo)
                passes = [(w, a, c) for c in range(DC) for w, a in ((w_h, xT_hi), (w_h, xT_lo), (w_l, xT_hi))]
                for n in range(part * 12 // parts, (part + 1) * 12 // parts):
                    w, a, c = passes[n]
                    last = pe.matmul(bank[:, BANK[which], :], w[:, c, heads * P:(heads + 1) * P], a[:, c, :],
                                     start=n == 0, stop=n == 11)
                if part == parts - 1:
                    last.then_inc(q_p if which == "q" else k_p, 1)

            def project_values(G, r):
                if r == 0:
                    at_least(pe, k_l, G + 3)
                if r == 2:
                    at_least(pe, m_l, 2 * G + 3)
                for n, (a, w, c) in enumerate([(a, w, c) for c in range(DC)
                                               for a, w in ((xT_hi, wu_hi), (xT_hi, wu_lo), (xT_lo, wu_hi))]):
                    last = pe.matmul(bank[:, BANK[f"u{r // 2}"], r % 2 * 256:(r % 2 + 1) * 256],
                                     a[:, c, r * P:(r + 1) * P], w[:, c, :], start=n == 0, stop=n == 11)
                last.then_inc(u_p, 1)

            def scores(G, oc, s):
                h, qt = s // R, s % R
                keys, par = (qt + 1) * P, (oc + 1) % 2
                if qt == 0:
                    at_least(pe, qk_in[h], 96 * (G + 2))
                at_least(pe, mx_r, US * (G + 1) + s - 1)
                pe.matmul(bank[:, 2 + s % 2, 0:keys], Q[0:KQ, par, h, qt * P:keys], K[0:KQ, par, h, 0:keys],
                          start=True, stop=False)
                pe.matmul(bank[:, 2 + s % 2, qt * P:keys], ident_r[:], mask[:], start=False, stop=True).then_inc(s_p, 1)

            def turn_max(group, hf, last_use):
                at_least(pe, *last_use)
                at_least(pe, mx_r, US * group + US // 2 * (hf + 1))
                pe.transpose(bank[0:US // 2, BANK[f"m{hf}"], 0:P], mx[:, hf, :], ident[:]).then_inc(mt_p, 1)

            def scores_T(G, oc, s):
                h, k = s // R, s % R
                par, at = oc % 2, slice(k * P, (k + 1) * P)
                if s % (US // 2) == 0:
                    at_least(pe, m_in[s // (US // 2)], 32 * (G + 1) + M_LEAD)
                at_least(pe, ex_r, US * G + s - 1 + EX_LEAD)
                pe.matmul(bank[:, 4 + s % 2, k * P:], K[:, par, h, at], Q[:, par, h, k * P:], start=True, stop=False)
                pe.matmul(bank[:, 4 + s % 2, at], ident_r[:], maskT[:], start=False, stop=True).then_inc(st_p, 1)

            def product(G, oc, s):
                h, k = s // R, s % R
                hf, of = s // (US // 2), s % (US // 2)
                if s == 0:
                    at_least(pe, v_r, G + 1)
                if of == 0:
                    at_least(pe, o_r, 2 * (G - 1) + hf + 1 + OR_LEAD)
                at_least(pe, pl_r, US * G + s + 1 + PL_LEAD)
                for n, part in enumerate((p_hi, p_lo)):
                    last = pe.matmul(bank[0:2 * UC, 6 + hf, k * P:], V[:, oc % 2, k, h, :], packed(part, s),
                                     start=of == 0 and n == 0, stop=of == US // 2 - 1 and n == 1)
                last.then_inc(o_p, 1)

            def turn_out(G, hf):
                at_least(pe, ot_r, 2 * G + hf + 1)
                for r in range(R):
                    last = pe.matmul(bank[:, 6 + hf, r * 2 * OC:(r + 1) * 2 * OC], oT[:, hf, r * P:(r + 1) * P], sel[:],
                                     start=True, stop=True)
                last.then_inc(sl_p, 1)

            def step(G, oc, project_, maxima, probs):
                for s in range(US + (TAIL if probs and oc == 3 else 0)):
                    if maxima and s < US:
                        scores(G, oc, s)
                    if probs and s < US:
                        scores_T(G, oc, s)
                    if probs and late(G, oc, s, PRODUCT):
                        product(*late(G, oc, s, PRODUCT))
                    if probs and late(G, oc, s, TURN) and late(G, oc, s, TURN)[2] % (US // 2) == 0:
                        group, _, of = late(G, oc, s, TURN)
                        turn_out(group, of // (US // 2))
                    if probs and s == 1:
                        turn_max(G, 1, (k_l, G + 2) if oc != 3 else (u_r, G + 3) if project_ else (m_l, 2 * G))
                    if project_:
                        start = 4 if oc == 2 else 1
                        if oc == 2 and s < 4:
                            turn_x(G, s)
                        if start <= s < start + 4:
                            project(G, oc, "q", s - start, 4)
                        elif start + 4 <= s < start + 8:
                            project(G, oc, "k", s - start - 4, 4)
                    if maxima and s == (12 if project_ and oc == 2 else 10):
                        turn_max(G + 1, 0, (q_l, G + 3) if project_ else (m_l, 2 * G + 1))
                    if project_ and oc == 2 and 12 <= s < US:
                        project_values(G, s - 12)
            run(pe, step)

        @block.scalar
        def _(act):
            act.sem_inc(ex_r, EX_LEAD)
            def normalise(b):
                at_least(act, xt_p, DC * b)
                for r in range(R):
                    act.activation(xn[:, r, :], x[:, bass.ds(R * b + r, 1), :].rearrange("p o d -> p (o d)"),
                                   ACT.Identity, bias=n_bi[:, bass.ds(R * b + r, 1)],
                                   scale=n_sc[:, bass.ds(R * b + r, 1)]).then_inc(n_r, 1)

            def x_hi(G, oc, c):
                at_least(act, xt_p, G + 2 + c + 1)
                if c == 0:
                    at_least(act, k_p, G + 2)
                act.activation(xT_hi[:, c, :], bank[:, BANK[f"x{c}"], :], ACT.Copy,
                               scale=ln1[:, c:c + 1]).then_inc(xt_h, 1)

            def qk_hi(G, oc, which):
                done, dst, ready = (q_p, q_hi, q_h) if which == "q" else (k_p, k_hi, k_h)
                for j in range(GH):
                    at_least(act, qk_in[j], 96 * (G + 2))
                at_least(act, done, G + 3)
                act.activation(dst[:], bank[:, BANK[which], :], ACT.Copy).then_inc(ready, 1)

            def u_copy(G, hf):
                if hf == 0:
                    at_least(act, v_r, G + 2)
                at_least(act, u_p, G + 4 + 2 * hf)
                act.activation(U[:, 2 * hf:2 * hf + 2].rearrange("p r h k -> p (r h k)"), bank[:, BANK[f"u{hf}"], :],
                               ACT.Copy).then_inc(u_r, 2)

            def max_hi(group, hf):
                at_least(act, m_in[hf], 32 * group + M_LEAD)
                at_least(act, mt_p, 2 * group + hf + 1)
                act.activation(m_hi[:, hf, :], bank[0:US // 2, BANK[f"m{hf}"], 0:P], ACT.Copy, scale=-1.0)\
                   .then_inc(m_h, 1)

            def probs_T(G, oc, s):
                k = s % R
                at_least(act, pl_r, US * G + s - 3 + PL_LEAD)
                at_least(act, o_p, US * G + s - 7 + O_LEAD)
                at_least(act, st_p, US * G + s + 1 + ST_LEAD)
                act.activation(packed(p_hi, s), bank[:, 4 + s % 2, k * P:], ACT.Exp, scale=ATT_SCALE)
                act.activation(pT[:, s % 4, k * P:], bank[:, 4 + s % 2, k * P:], ACT.Exp, scale=ATT_SCALE)\
                   .then_inc(ex_r, 1)

            def out_copy(G, hf):
                at_least(act, sl_p, 2 * (G - 1) + hf + 1 + SL_LEAD)
                at_least(act, o_p, US * G + US // 2 * (hf + 1) + O_LEAD)
                act.activation(oT[:, hf, :], bank[0:2 * UC, 6 + hf, :], ACT.Copy).then_inc(ot_r, 1)

            def step(G, oc, project_, maxima, probs):
                after = 3 if oc == 2 else 0
                for s in range(US + (TAIL if probs and oc == 3 else 0)):
                    if probs and s < US:
                        probs_T(G, oc, s)
                    if probs and late(G, oc, s, COPY) and late(G, oc, s, COPY)[2] % (US // 2) == 0:
                        group, _, of = late(G, oc, s, COPY)
                        out_copy(group, of // (US // 2))
                    if probs and s == 1:
                        max_hi(G, 1)
                    if project_:
                        if oc == 2 and s < 4:
                            x_hi(G, oc, s)
                        if s == 5 + after:
                            qk_hi(G, oc, "q")
                        if s == 9 + after:
                            qk_hi(G, oc, "k")
                    if maxima and s == (12 if project_ and oc == 2 else 10):
                        max_hi(G + 1, 0)
                    if oc == 1 and s == 13 and not isinstance(G, int):
                        normalise(turn[0] + 1)
                    if project_ and oc == 2 and s in (14, 15):
                        u_copy(G, s - 14)

            normalise(0)
            turn = [0]
            batch = each_step(step)
            with act.Fori(0, B - 1) as b:
                turn[0] = b
                batch(b, False)
            batch(B - 1, True)

        @block.vector
        def _(dve):
            dve.sem_inc(o_r, OR_LEAD)
            dve.sem_inc(pl_r, PL_LEAD)
            def x_lo(G, oc, c):
                at_least(dve, xt_h, G + 2 + c + 1)
                dve.scalar_tensor_tensor(xT_lo[:, c, :], bank[:, BANK[f"x{c}"], :], ln1[:, c:c + 1],
                                         xT_hi[:, c, :].bitcast(F32), ALU.mult, ALU.subtract).then_inc(xt_l, 1)

            def qk_lo(G, oc, which):
                ready, hi, lo, done = (q_h, q_hi, q_lo, q_l) if which == "q" else (k_h, k_hi, k_lo, k_l)
                at_least(dve, ready, G + 3)
                dve.tensor_tensor(lo[:], bank[:, BANK[which], :], hi[:].bitcast(F32), ALU.subtract)\
                   .then_inc(done, 1)

            def max_lo(group, hf):
                at_least(dve, m_h, 2 * group + hf + 1)
                dve.scalar_tensor_tensor(m_lo[:, hf, :], bank[0:US // 2, BANK[f"m{hf}"], 0:P], -1.0,
                                         m_hi[:, hf, :].bitcast(F32), ALU.mult, ALU.subtract).then_inc(m_l, 1)

            def maximum(G, oc, s):
                hf, at, keys = s // (US // 2), s % (US // 2), (s % R + 1) * P
                if at == 0:
                    at_least(dve, mt_p, 2 * (G + 1) + hf - 1)
                at_least(dve, s_p, US * (G + 1) + s + 1)
                dve.reduce_max(mx[:, hf, at:at + 1], bank[:, 2 + s % 2, 0:keys], AX).then_inc(mx_r, 1)

            def probs_lo(G, s):
                k = s % R
                at_least(dve, ex_r, US * G + s + 1 + EX_LEAD)
                dve.tensor_tensor(packed(p_lo, s), pT[:, s % 4, k * P:], packed(p_hi, s).bitcast(F32),
                                  ALU.subtract).then_inc(pl_r, 1)

            def finish(G, hf, part):
                if part == 0:
                    at_least(dve, sl_p, 2 * G + hf + 1 + SL_LEAD)
                else:
                    dve.wait_ge(och, 8 * G + 4 * hf + part)
                out = bank[:, 6 + hf, 0:R * 2 * OC].rearrange("p (r h c) -> p r h c", r=R, h=2)
                own = mod[:, bass.ds(R * now[0], R), :]
                if part == 0:
                    dve.reciprocal(rto[:], out[:, :, :, RK]).then_inc(och, 1)
                elif part == 1:
                    dve.tensor_tensor(ou[:], out[:, :, :, 0:RK], rto[:].unsqueeze(3).broadcast_to([P, R, 2, RK]),
                                      ALU.mult).then_inc(och, 1)
                elif part == 2:
                    dve.sem_inc(o_r, 1)
                    dve.tensor_tensor(red[:], ou[:, :, 0, :], ou[:, :, 1, :], ALU.add).then_inc(och, 1)
                else:
                    dve.tensor_tensor(own, own, red[:], ALU.add).then_inc(och, 1)

            def step(G, oc, project_, maxima, probs):
                after = 3 if oc == 2 else 0
                for s in range(US + (TAIL if probs and oc == 3 else 0)):
                    if maxima and s < US:
                        maximum(G, oc, s)
                    if probs and late(G, oc, s, LOW):
                        group, _, of = late(G, oc, s, LOW)
                        probs_lo(group, of)
                    for part in range(4) if probs else ():
                        if late(G, oc, s, FINISH + part) and late(G, oc, s, FINISH + part)[2] in (0, US // 2):
                            group, _, of = late(G, oc, s, FINISH + part)
                            finish(group, of // (US // 2), part)
                    if probs and s == 1:
                        max_lo(G, 1)
                    if project_:
                        if oc == 2 and s < 4:
                            x_lo(G, oc, s)
                        if s == 5 + after:
                            qk_lo(G, oc, "q")
                        if s == 9 + after:
                            qk_lo(G, oc, "k")
                    if maxima and s == (12 if project_ and oc == 2 else 10):
                        max_lo(G + 1, 0)

            now = [0]
            batch = each_step(step)
            with dve.Fori(0, B - 1) as b:
                now[0] = b
                batch(b, False)
            now[0] = B - 1
            batch(B - 1, True)


def mlp_source(g, u):
    at = bass.ds(u * UH, UH)
    return (g["W_inT"][:, at].rearrange("(c p) h -> p c h", p=P), g["W_upT"][:, at].rearrange("(c p) h -> p c h", p=P),
            g["W_downT"][at, :].rearrange("(k p) d -> p k d", p=P))


def phase_mlp(nc, s_, sem, g):
    x, bank, ident, tg = g["x"], g["bank"], g["ident"], g["tg"]
    n_sc, n_bi, r_sc, r_bi, mod = g["n_sc"], g["n_bi"], g["r_sc"], g["r_bi"], g["mod"]
    xT_hi = s_("ml_xT_hi", [P, DC, B * N], F32R)
    xT_lo = s_("ml_xT_lo", [P, DC, B * N], F32R)
    b_stack = s_("ml_b_stack", [96, F_], F32R)
    m_stack = s_("ml_m_stack", [96, B * N], F32R)
    ln2 = s_("ml_ln2", [P, DC])
    A = s_("ml_A", [P, DC, RK])
    A_split = s_("ml_A_split", [P, DC, 2, RK], F32R)
    ha = s_("ml_hA", [P, R, RK])
    scratch = s_("ml_scratch", [P, 2, HC, 512])
    h_hi = s_("ml_h_hi", [P, 2, HC, 512], F32R)
    h_lo = s_("ml_h_lo", [P, 2, HC, 512], F32R)
    xn = scratch[:].rearrange("p a c n -> p (a c) n")
    m_hi = h_hi[0:96, 0, 0, :]
    m_rows = s_("ml_m_rows", [P, R, 3, 32])
    FH = F_ // 2
    b_raw = s_("ml_b_raw", [96, FH])

    small_in = sem("ml_small_arrived")
    cleared = sem("ml_rows_cleared")
    b_in = sem("ml_b_arrived")
    a_h = sem("ml_A_hi_ready")
    a_l = sem("ml_A_lo_ready")
    bst_h = sem("ml_b_hi_ready")
    bst_r = sem("ml_b_stack_ready")
    n_r = sem("ml_n_ready")
    xt_p = sem("ml_xT_transposed")
    xt_h = sem("ml_xT_hi_ready")
    xt_l = sem("ml_xT_lo_ready")
    th_r = sem("ml_tanh_ready")
    ha_p = sem("ml_hA_done")
    m_r = sem("ml_m_ready")
    mt_p = sem("ml_mT_done")
    mh_r = sem("ml_m_hi_ready")
    ms_r = sem("ml_m_stack_ready")
    res_r = sem("ml_residual_ready")

    def load(sp):
        sp.dma_start(ln2[:], g["ln2_w"]).then_inc(small_in, 16)
        sp.dma_start(A[:], g["A_in"].rearrange("(c p) r -> p c r", p=P)).then_inc(small_in, 16)
        sp.wait_ge(cleared, 1)
        for hf in range(2):
            if hf:
                sp.wait_ge(bst_r, 1)
            for k in range(3):
                sp.dma_start(b_raw[32 * k:32 * k + RK, :], g["B_in"][:, hf * FH:(hf + 1) * FH]).then_inc(b_in, 16)

    def constants(pool):
        pool.memset(b_raw[:], 0.0).then_inc(cleared, 1)
        pool.memset(m_rows[:], 0.0).then_inc(cleared, 1)
        pool.wait_ge(a_h, 1)
        pool.tensor_tensor(A_split[:, :, 1, :], A[:], A_split[:, :, 0, :].bitcast(F32), ALU.subtract).then_inc(a_l, 1)
        pool.wait_ge(bst_r, 2)

    def residual(pool):
        pool.wait_ge(n_r, T)
        for t in range(T):
            pool.tensor_scalar(x[:, t, :], x[:, t, :], r_sc[:, t:t + 1], r_bi[:, t:t + 1], ALU.mult, ALU.add)\
                .then_inc(res_r, 1)

    def x_hi(act, split_first):
        def normalise(b):
            if b >= 1:
                act.wait_ge(xt_p, DC * b)
            for r in range(R):
                t = R * b + r
                act.activation(xn[:, r, :], x[:, t, :], ACT.Identity, bias=n_bi[:, t:t + 1],
                               scale=n_sc[:, t:t + 1]).then_inc(n_r, 1)

        def m_split(b):
            act.wait_ge(mt_p, b + 1)
            if b >= 1:
                act.wait_ge(ms_r, b)
            act.activation(m_hi, bank[0:96, 6 + b % 2, :], ACT.Copy).then_inc(mh_r, 1)

        normalise(0)
        act.activation(mod[:], mod[:], ACT.Tanh).then_inc(th_r, 1)
        act.wait_ge(small_in, 32)
        act.activation(A_split[:, :, 0, :], A[:], ACT.Copy).then_inc(a_h, 1)
        for b in range(B):
            for c in range(DC):
                act.wait_ge(xt_p, DC * b + c + 1)
                act.activation(xT_hi[:, c, b * N:(b + 1) * N], bank[:, c, :], ACT.Copy,
                               scale=ln2[:, c:c + 1]).then_inc(xt_h, 1)
            if b + 1 < B:
                normalise(b + 1)
            if b < 2:
                act.wait_ge(b_in, 48 * (b + 1))
                act.activation(b_stack[:, b * FH:(b + 1) * FH], b_raw[:], ACT.Copy).then_inc(bst_h, 1)
            if b == 0:
                split_first()
            if b >= 2:
                m_split(b - 2)
        m_split(2)
        m_split(3)

    def x_turned(pe):
        def turn(b):
            pe.wait_ge(n_r, R * b + R)
            for c in range(DC):
                if b >= 1:
                    pe.wait_ge(xt_l, DC * b + c - 3)
                for r in range(R):
                    last = pe.transpose(bank[:, c, r * P:(r + 1) * P], xn[:, r, c * P:(c + 1) * P], ident[:])
                last.then_inc(xt_p, 1)

        def h_A(b):
            pe.wait_ge(xt_l, DC * b + DC)
            if b == 0:
                pe.wait_ge(a_l, 1)
            if b >= 2:
                pe.wait_ge(m_r, b - 1)
            for r in range(R):
                at = slice((R * b + r) * P, (R * b + r + 1) * P)
                to = 2 * RK * r
                for c in range(DC):
                    pe.matmul(bank[:, 4 + b % 2, to:to + 2 * RK], xT_hi[:, c, at],
                              A_split[:, c].rearrange("p k r -> p (k r)"), start=c == 0, stop=False)
                for c in range(DC):
                    last = pe.matmul(bank[:, 4 + b % 2, to:to + RK], xT_lo[:, c, at], A_split[:, c, 0, :],
                                     start=False, stop=c == DC - 1)
            last.then_inc(ha_p, 1)

        def turn_m(b):
            pe.wait_ge(m_r, b + 1)
            if b >= 2:
                pe.wait_ge(ms_r, b - 1)
            for r in range(R):
                last = pe.transpose(bank[0:96, 6 + b % 2, r * P:(r + 1) * P],
                                    m_rows[:, r].rearrange("p k m -> p (k m)"), ident[:])
            last.then_inc(mt_p, 1)

        turn(0)
        turn(1)
        h_A(0)
        turn(2)
        turn_m(0)
        h_A(1)
        turn(3)
        turn_m(1)
        h_A(2)
        h_A(3)
        turn_m(2)
        turn_m(3)
        pe.wait_ge(ms_r, 1)

    def m_stacked(pe):
        pe.wait_ge(ms_r, B)

    def x_lo(dve):
        step = linked(dve, g["vector_chain"])

        def split(b):
            at = slice(b * N, (b + 1) * N)
            for c in range(DC):
                dve.wait_ge(xt_h, DC * b + c + 1)
                dve.scalar_tensor_tensor(xT_lo[:, c, at], bank[:, c, :], ln2[:, c:c + 1], xT_hi[:, c, at].bitcast(F32),
                                         ALU.mult, ALU.subtract).then_inc(xt_l, 1)

        def b_split(hf):
            at = slice(hf * FH, (hf + 1) * FH)
            dve.wait_ge(bst_h, hf + 1)
            dve.tensor_tensor(b_stack[32:64, at], b_raw[32:64], b_stack[32:64, at].bitcast(F32), ALU.subtract)\
               .then_inc(bst_r, 1)

        def m_made(b):
            own = slice(R * b, R * b + R)
            dve.wait_ge(ha_p, b + 1)
            both = bank[:, 4 + b % 2, 0:R * 2 * RK].rearrange("p (t k r) -> p t k r", k=2, r=RK)
            step(dve.tensor_copy(ha[:], both[:, :, 0, :]))
            step(dve.tensor_tensor(ha[:], ha[:], both[:, :, 1, :], ALU.add))
            if b >= 1:
                dve.wait_ge(mt_p, b)
            step(dve.scalar_tensor_tensor(m_rows[:, :, 0, 0:RK], mod[:, own, :], MOD_SCALE, ha[:], ALU.mult, ALU.mult))
            dve.tensor_copy(m_rows[:, :, 1, 0:RK], m_rows[:, :, 0, 0:RK])
            dve.tensor_copy(m_rows[:, :, 2, 0:RK], m_rows[:, :, 0, 0:RK]).then_inc(m_r, 1)

        def m_split(b):
            at = slice(b * N, (b + 1) * N)
            dve.wait_ge(mh_r, b + 1)
            dve.tensor_copy(m_stack[0:64, at], m_hi[0:64].bitcast(F32))
            dve.tensor_tensor(m_stack[64:96, at], bank[64:96, 6 + b % 2, :], m_hi[64:96].bitcast(F32), ALU.subtract)\
               .then_inc(ms_r, 1)

        dve.wait_ge(small_in, 32)
        dve.wait_ge(cleared, 2)
        dve.wait_ge(th_r, 1)
        split(0)
        b_split(0)
        split(1)
        b_split(1)
        m_made(0)
        split(2)
        m_split(0)
        m_made(1)
        split(3)
        m_split(1)
        m_made(2)
        m_made(3)
        m_split(2)
        m_split(3)

    def residual_made(dve):
        dve.wait_ge(res_r, T)

    gated_units(nc, s_, sem, "ml", g, xT_hi, xT_lo, MLP_UNITS, lambda u: mlp_source(g, u), gate=tg[:, 3:4],
                mod=(b_stack, m_stack), raw=g["third_raw"], w_in=g["third_w"], scratch=scratch, h=(h_hi, h_lo),
                first=dict(sync=load, gpsimd=constants, scalar=x_hi, tensor=x_turned, vector=x_lo),
                second=dict(gpsimd=residual, tensor=m_stacked, vector=residual_made), out_dram=g["out_dram"])


def layout(inputs):
    import numpy as np
    a = {k: np.asarray(v) for k, v in inputs.items()}
    c = np.ascontiguousarray
    return {
        "x_in": a["x"], "ctxT_in": c(a["ctx_512"].reshape(B * N, C).T),
        "g_xattn": a["g_xattn"], "g_ffn": a["g_ffn"],
        "gr_Wq": a["L0_xattn_Wq"], "gr_Wk": a["L0_xattn_Wk"], "gr_gamma": a["L0_xattn_gamma_raw"].reshape(1),
        "router_w": a["L0_ffn_router_w"], "w_gate": a["L0_ffn_w_gate"], "w_up": a["L0_ffn_w_up"],
        "w_down": a["L0_ffn_w_down"], "sw_gate": a["L0_ffn_sw_gate"], "sw_up": a["L0_ffn_sw_up"],
        "sw_down": a["L0_ffn_sw_down"],
        "WkT": c(a["L1_xattn_W_k"].T), "b_k": a["L1_xattn_b_k"], "ln_gamma": a["L1_xattn_ln_gamma"],
        "ln_beta": a["L1_xattn_ln_beta"], "ln1_w": c(a["L1_ffn_ln1_w"].reshape(DC, P).T),
        "ln2_w": c(a["L1_ffn_ln2_w"].reshape(DC, P).T),
        "WqT": c(a["L1_ffn_Wq"].T), "WkT1": c(a["L1_ffn_Wk"].T), "Wv": a["L1_ffn_Wv"], "Wo": a["L1_ffn_Wo"],
        "A_in": a["L1_ffn_A"], "B_in": a["L1_ffn_B"], "W_inT": c(a["L1_ffn_W_in_base"].T),
        "W_upT": c(a["L1_ffn_W_up_base"].T), "W_downT": c(a["L1_ffn_W_down"].T),
    }


def kernel(**inputs):
    import numpy as _np
    import concourse.bacc as _bacc
    from concourse import mybir as _mybir
    from concourse.bass_utils import run_bass_kernel_spmd as _run

    nc = _bacc.Bacc("TRN2", target_bir_lowering=False, num_devices=1)
    arrays, args = {}, []
    for name, a in layout(inputs).items():
        arrays[f"in_{name}"] = _np.ascontiguousarray(a)
        args.append(nc.dram_tensor(f"in_{name}", a.shape, _mybir.dt.from_np(a.dtype), kind="ExternalInput").ap())
    out = nc.dram_tensor("out_0", (B, N, D), _mybir.dt.float32, kind="ExternalOutput").ap()
    flamingo_kernel(nc, *args, out)
    r = _run(nc, [arrays], core_ids=[0])
    return r.results[0]["out_0"]
```
